# Optimizing a Trainium2 kernel written in Bass

```python
import numpy as np
import jax
import jax.numpy as jnp

def _softmax(x, axis=-1):
    return jax.nn.softmax(x, axis=axis)

def _gelu(x):
    return jax.nn.gelu(x, approximate=True)

def _silu(x):
    return jax.nn.silu(x)

def _sigmoid(x):
    return jax.nn.sigmoid(x)

def _layernorm(x, axis=-1, eps=1e-05):
    m = jnp.mean(x, axis=axis, keepdims=True)
    v = jnp.var(x, axis=axis, keepdims=True)
    return (x - m) / jnp.sqrt(v + eps)

def _scatter_add(tgt, idx, src, axis=0):
    return tgt.at[idx].add(src)

def _segment_sum(src, seg, n):
    return jax.ops.segment_sum(src, seg, n)
kernel_name = 'mk_adaln_d2_jaxref_r8_9b8a67'

def setup_inputs(seed: int=0):
    np.random.seed(seed)
    _w = jnp.asarray

    def _L0_attn_setup():
        import jax, jax.numpy as jnp
        import numpy as np
        from jax import lax
        D_MODEL, D_INNER, N_STATE, DT_RANK, K = (128, 256, 16, 64, 3)
        B_SZ, SEQ = (2, 128)

        def silu(v):
            return v * jax.nn.sigmoid(v)

        def selective_scan(u, delta, A, B, C):
            deltaA = jnp.exp(jnp.einsum('bld,dn->bldn', delta, A))
            deltaBu = jnp.einsum('bld,bln,bld->bldn', delta, B, u)
            h0 = jnp.zeros((u.shape[0], u.shape[2], A.shape[1]), u.dtype)

            def step(h, inp):
                dA_t, dBu_t, C_t = inp
                h = dA_t * h + dBu_t
                y = jnp.einsum('bdn,bn->bd', h, C_t)
                return (h, y)
            xs = (jnp.moveaxis(deltaA, 1, 0), jnp.moveaxis(deltaBu, 1, 0), jnp.moveaxis(C, 1, 0))
            _, ys = lax.scan(step, h0, xs)
            return jnp.moveaxis(ys, 0, 1)
        key = jax.random.key(seed)
        ks = jax.random.split(key, 12)
        s = 0.02
        return {'x': jax.random.normal(ks[0], (B_SZ, SEQ, D_MODEL), jnp.float32), 'A_log': jax.random.normal(ks[1], (D_INNER, N_STATE), jnp.float32) * 0.5, 'W_in': jax.random.normal(ks[2], (D_MODEL, 2 * D_INNER), jnp.float32) * s, 'b_in': jax.random.normal(ks[3], (2 * D_INNER,), jnp.float32) * s, 'conv_w': jax.random.normal(ks[4], (D_INNER, 1, K), jnp.float32) * s, 'conv_b': jax.random.normal(ks[5], (D_INNER,), jnp.float32) * s, 'W_x': jax.random.normal(ks[6], (D_INNER, DT_RANK + 2 * N_STATE), jnp.float32) * s, 'W_dt': jax.random.normal(ks[7], (DT_RANK, D_INNER), jnp.float32) * s, 'b_dt': jax.random.normal(ks[8], (D_INNER,), jnp.float32) * s, 'W_out': jax.random.normal(ks[9], (D_INNER, D_MODEL), jnp.float32) * s, 'b_out': jax.random.normal(ks[10], (D_MODEL,), jnp.float32) * s}
    _L0_attn_in = _L0_attn_setup()

    def _L0_ffn_setup():
        import jax, jax.numpy as jnp
        import numpy as np
        E = 8
        TOPK = 2

        def _moe_forward(x, Wg, W1, W2, W3):
            B, S, D = x.shape
            xt = x.reshape(-1, D)
            T = xt.shape[0]
            logits = xt @ Wg.T
            scores = jax.nn.softmax(logits, axis=-1)
            w, idx = jax.lax.top_k(scores, TOPK)
            w = w / (w.sum(axis=-1, keepdims=True) + 1e-20)
            cw = jnp.zeros((T, E), xt.dtype).at[jnp.arange(T)[:, None], idx].add(w)
            h = jax.nn.silu(jnp.einsum('td,ehd->teh', xt, W1)) * jnp.einsum('td,ehd->teh', xt, W3)
            out = jnp.einsum('teh,edh->ted', h, W2)
            y = jnp.einsum('te,ted->td', cw, out)
            return y.reshape(B, S, D)
        key = jax.random.key(seed)
        k0, k1, k2, k3, k4 = jax.random.split(key, 5)
        B, S, D, H = (1, 256, 128, 352)
        scale = 0.02
        x = jax.random.normal(k0, (B, S, D), jnp.float32)
        Wg = jax.random.normal(k1, (E, D), jnp.float32) * scale
        W1 = jax.random.normal(k2, (E, H, D), jnp.float32) * scale
        W2 = jax.random.normal(k3, (E, D, H), jnp.float32) * scale
        W3 = jax.random.normal(k4, (E, H, D), jnp.float32) * scale
        return {'x': x, 'Wg': Wg, 'W1': W1, 'W2': W2, 'W3': W3}
    _L0_ffn_in = _L0_ffn_setup()
    _L0_c = _w((lambda *s: np.random.randn(*s).astype(np.float32) * 0.05)(1, 128))
    _L0_wmod = _w((lambda *s: np.random.randn(*s).astype(np.float32) * 0.05)(128, 6 * 128) * 128 ** (-0.5))

    def _L1_attn_setup():
        import jax, jax.numpy as jnp
        import numpy as np
        B, N, D, H, DH, M = (4, 512, 128, 16, 64, 32)
        EPS = 0.0001

        def softmax_kernel(data, P, is_query):
            dn = data.shape[-1] ** (-0.25)
            ratio = P.shape[0] ** (-0.5)
            dd = jnp.einsum('bhnd,md->bhnm', dn * data, P)
            diag = (jnp.sum(data * data, axis=-1) * 0.5 * dn * dn)[..., None]
            if is_query:
                mx = jnp.max(dd, axis=-1, keepdims=True)
            else:
                mx = jnp.max(dd)
            return ratio * (jnp.exp(dd - diag - mx) + EPS)
        key = jax.random.key(seed)
        ks = jax.random.split(key, 6)
        s = 1.0 / np.sqrt(D).astype(np.float32)
        x = jax.random.normal(ks[0], (B, N, D), jnp.float32)
        Wq = jax.random.normal(ks[1], (D, H * DH), jnp.float32) * s
        Wk = jax.random.normal(ks[2], (D, H * DH), jnp.float32) * s
        Wv = jax.random.normal(ks[3], (D, H * DH), jnp.float32) * s
        Wo = jax.random.normal(ks[4], (H * DH, D), jnp.float32) * s
        bo = jnp.zeros((D,), jnp.float32)
        P = jax.random.normal(ks[5], (M, DH), jnp.float32)
        return {'x': x, 'Wq': Wq, 'Wk': Wk, 'Wv': Wv, 'Wo': Wo, 'bo': bo, 'P': P}
    _L1_attn_in = _L1_attn_setup()

    def _L1_ffn_setup():
        import jax, jax.numpy as jnp
        import numpy as np
        TOP_K = 2
        B, T, D, H, E = (4, 256, 128, 256, 8)
        key = jax.random.key(seed)
        ks = jax.random.split(key, 5)
        x = jax.random.normal(ks[0], (B, T, D), dtype=jnp.float32)
        router_w = jax.random.normal(ks[1], (E, D), dtype=jnp.float32) * D ** (-0.5)
        router_b = jnp.zeros((E,), dtype=jnp.float32)
        w_gate = jax.random.normal(ks[2], (E, H, D), dtype=jnp.float32) * D ** (-0.5)
        w_up = jax.random.normal(ks[3], (E, H, D), dtype=jnp.float32) * D ** (-0.5)
        w_down = jax.random.normal(ks[4], (E, D, H), dtype=jnp.float32) * H ** (-0.5)
        return {'x': x, 'router_w': router_w, 'router_b': router_b, 'w_gate': w_gate, 'w_up': w_up, 'w_down': w_down}
    _L1_ffn_in = _L1_ffn_setup()
    _L1_c = _w((lambda *s: np.random.randn(*s).astype(np.float32) * 0.05)(1, 128))
    _L1_wmod = _w((lambda *s: np.random.randn(*s).astype(np.float32) * 0.05)(128, 6 * 128) * 128 ** (-0.5))
    _d = {'L0_attn_x': _L0_attn_in['x'], 'L0_attn_A_log': _L0_attn_in['A_log'], 'L0_attn_W_in': _L0_attn_in['W_in'], 'L0_attn_b_in': _L0_attn_in['b_in'], 'L0_attn_conv_w': _L0_attn_in['conv_w'], 'L0_attn_conv_b': _L0_attn_in['conv_b'], 'L0_attn_W_x': _L0_attn_in['W_x'], 'L0_attn_W_dt': _L0_attn_in['W_dt'], 'L0_attn_b_dt': _L0_attn_in['b_dt'], 'L0_attn_W_out': _L0_attn_in['W_out'], 'L0_attn_b_out': _L0_attn_in['b_out'], 'L0_ffn_Wg': _L0_ffn_in['Wg'], 'L0_ffn_W1': _L0_ffn_in['W1'], 'L0_ffn_W2': _L0_ffn_in['W2'], 'L0_ffn_W3': _L0_ffn_in['W3'], 'L0_c': _L0_c, 'L0_wmod': _L0_wmod, 'L1_attn_Wq': _L1_attn_in['Wq'], 'L1_attn_Wk': _L1_attn_in['Wk'], 'L1_attn_Wv': _L1_attn_in['Wv'], 'L1_attn_Wo': _L1_attn_in['Wo'], 'L1_attn_bo': _L1_attn_in['bo'], 'L1_attn_P': _L1_attn_in['P'], 'L1_ffn_router_w': _L1_ffn_in['router_w'], 'L1_ffn_router_b': _L1_ffn_in['router_b'], 'L1_ffn_w_gate': _L1_ffn_in['w_gate'], 'L1_ffn_w_up': _L1_ffn_in['w_up'], 'L1_ffn_w_down': _L1_ffn_in['w_down'], 'L1_c': _L1_c, 'L1_wmod': _L1_wmod}
    _x0 = _d['L0_attn_x']
    _d['L0_attn_x'] = jax.random.normal(jax.random.fold_in(jax.random.key(seed), 1), (1, 2048, 128), dtype=_x0.dtype)
    del _x0
    return _d

def reference(L0_attn_x, L0_attn_A_log, L0_attn_W_in, L0_attn_b_in, L0_attn_conv_w, L0_attn_conv_b, L0_attn_W_x, L0_attn_W_dt, L0_attn_b_dt, L0_attn_W_out, L0_attn_b_out, L0_ffn_Wg, L0_ffn_W1, L0_ffn_W2, L0_ffn_W3, L0_c, L0_wmod, L1_attn_Wq, L1_attn_Wk, L1_attn_Wv, L1_attn_Wo, L1_attn_bo, L1_attn_P, L1_ffn_router_w, L1_ffn_router_b, L1_ffn_w_gate, L1_ffn_w_up, L1_ffn_w_down, L1_c, L1_wmod):

    def _L0_attn_ref(x, A_log, W_in, b_in, conv_w, conv_b, W_x, W_dt, b_dt, W_out, b_out):
        import jax, jax.numpy as jnp
        import numpy as np
        from jax import lax
        D_MODEL, D_INNER, N_STATE, DT_RANK, K = (128, 256, 16, 64, 3)
        B_SZ, SEQ = (2, 128)

        def silu(v):
            return v * jax.nn.sigmoid(v)

        def selective_scan(u, delta, A, B, C):
            deltaA = jnp.exp(jnp.einsum('bld,dn->bldn', delta, A))
            deltaBu = jnp.einsum('bld,bln,bld->bldn', delta, B, u)
            h0 = jnp.zeros((u.shape[0], u.shape[2], A.shape[1]), u.dtype)

            def step(h, inp):
                dA_t, dBu_t, C_t = inp
                h = dA_t * h + dBu_t
                y = jnp.einsum('bdn,bn->bd', h, C_t)
                return (h, y)
            xs = (jnp.moveaxis(deltaA, 1, 0), jnp.moveaxis(deltaBu, 1, 0), jnp.moveaxis(C, 1, 0))
            _, ys = lax.scan(step, h0, xs)
            return jnp.moveaxis(ys, 0, 1)
        xr = x @ W_in + b_in
        u, res = jnp.split(xr, 2, axis=-1)
        uc = lax.conv_general_dilated(jnp.moveaxis(u, 1, 2), conv_w, window_strides=(1,), padding=[(K - 1, 0)], feature_group_count=D_INNER, dimension_numbers=('NCH', 'OIH', 'NCH'))
        u = silu(jnp.moveaxis(uc, 2, 1) + conv_b)
        xp = u @ W_x
        dt, Bm, Cm = jnp.split(xp, [DT_RANK, DT_RANK + N_STATE], axis=-1)
        delta = jax.nn.softplus(dt @ W_dt + b_dt)
        A = -jnp.exp(A_log)
        y = selective_scan(u, delta, A, Bm, Cm)
        y = y * silu(res)
        return y @ W_out + b_out

    def _L0_ffn_ref(x, Wg, W1, W2, W3):
        import jax, jax.numpy as jnp
        import numpy as np
        E = 8
        TOPK = 2

        def _moe_forward(x, Wg, W1, W2, W3):
            B, S, D = x.shape
            xt = x.reshape(-1, D)
            T = xt.shape[0]
            logits = xt @ Wg.T
            scores = jax.nn.softmax(logits, axis=-1)
            w, idx = jax.lax.top_k(scores, TOPK)
            w = w / (w.sum(axis=-1, keepdims=True) + 1e-20)
            cw = jnp.zeros((T, E), xt.dtype).at[jnp.arange(T)[:, None], idx].add(w)
            h = jax.nn.silu(jnp.einsum('td,ehd->teh', xt, W1)) * jnp.einsum('td,ehd->teh', xt, W3)
            out = jnp.einsum('teh,edh->ted', h, W2)
            y = jnp.einsum('te,ted->td', cw, out)
            return y.reshape(B, S, D)
        return _moe_forward(x, Wg, W1, W2, W3)

    def _L1_attn_ref(x, Wq, Wk, Wv, Wo, bo, P):
        import jax, jax.numpy as jnp
        import numpy as np
        B, N, D, H, DH, M = (4, 512, 128, 16, 64, 32)
        EPS = 0.0001

        def softmax_kernel(data, P, is_query):
            dn = data.shape[-1] ** (-0.25)
            ratio = P.shape[0] ** (-0.5)
            dd = jnp.einsum('bhnd,md->bhnm', dn * data, P)
            diag = (jnp.sum(data * data, axis=-1) * 0.5 * dn * dn)[..., None]
            if is_query:
                mx = jnp.max(dd, axis=-1, keepdims=True)
            else:
                mx = jnp.max(dd)
            return ratio * (jnp.exp(dd - diag - mx) + EPS)
        b, n, _ = x.shape

        def proj(W):
            return (x @ W).reshape(b, n, H, DH).transpose(0, 2, 1, 3)
        q, k, v = (proj(Wq), proj(Wk), proj(Wv))
        qp = softmax_kernel(q, P, is_query=True)
        kp = softmax_kernel(k, P, is_query=False)
        k_cumsum = kp.sum(axis=-2)
        D_inv = 1.0 / jnp.einsum('bhnm,bhm->bhn', qp, k_cumsum)
        ctx = jnp.einsum('bhnm,bhne->bhme', kp, v)
        out = jnp.einsum('bhme,bhnm,bhn->bhne', ctx, qp, D_inv)
        out = out.transpose(0, 2, 1, 3).reshape(b, n, H * DH)
        return out @ Wo + bo

    def _L1_ffn_ref(x, router_w, router_b, w_gate, w_up, w_down):
        import jax, jax.numpy as jnp
        import numpy as np
        TOP_K = 2
        B, T, D, H, E = (4, 256, 128, 256, 8)
        b, t, d = x.shape
        n_exp = router_w.shape[0]
        flat = x.reshape(-1, d)
        logits = flat @ router_w.T + router_b
        probs = jax.nn.softmax(logits, axis=-1)
        top_vals, top_idx = jax.lax.top_k(probs, TOP_K)
        top_vals = top_vals / (jnp.sum(top_vals, axis=-1, keepdims=True) + 1e-09)
        comb = jnp.sum(jax.nn.one_hot(top_idx, n_exp, dtype=flat.dtype) * top_vals[..., None], axis=1)
        g = jnp.einsum('nd,ehd->enh', flat, w_gate)
        u = jnp.einsum('nd,ehd->enh', flat, w_up)
        h = jax.nn.silu(g) * u
        e_out = jnp.einsum('enh,edh->end', h, w_down)
        out = jnp.einsum('ne,end->nd', comb, e_out)
        return out.reshape(b, t, d)
    x = L0_attn_x
    mod = (_silu(L0_c) @ L0_wmod).reshape(L0_c.shape[0], 6, 1, -1)
    sa, ca, ga, sb, cb, gb = (mod[:, 0], mod[:, 1], mod[:, 2], mod[:, 3], mod[:, 4], mod[:, 5])
    ga = (2 * (ga >= 0) - 1) * jnp.maximum(jnp.abs(ga), 0.25)
    gb = (2 * (gb >= 0) - 1) * jnp.maximum(jnp.abs(gb), 0.25)
    h = _layernorm(x, axis=-1) * (1 + ca) + sa
    x = x + ga * _L0_attn_ref(h, L0_attn_A_log, L0_attn_W_in, L0_attn_b_in, L0_attn_conv_w, L0_attn_conv_b, L0_attn_W_x, L0_attn_W_dt, L0_attn_b_dt, L0_attn_W_out, L0_attn_b_out)
    h = _layernorm(x, axis=-1) * (1 + cb) + sb
    x = x + gb * _L0_ffn_ref(h, L0_ffn_Wg, L0_ffn_W1, L0_ffn_W2, L0_ffn_W3)
    mod = (_silu(L1_c) @ L1_wmod).reshape(L1_c.shape[0], 6, 1, -1)
    sa, ca, ga, sb, cb, gb = (mod[:, 0], mod[:, 1], mod[:, 2], mod[:, 3], mod[:, 4], mod[:, 5])
    ga = (2 * (ga >= 0) - 1) * jnp.maximum(jnp.abs(ga), 0.25)
    gb = (2 * (gb >= 0) - 1) * jnp.maximum(jnp.abs(gb), 0.25)
    h = _layernorm(x, axis=-1) * (1 + ca) + sa
    x = x + ga * _L1_attn_ref(h, L1_attn_Wq, L1_attn_Wk, L1_attn_Wv, L1_attn_Wo, L1_attn_bo, L1_attn_P)
    h = _layernorm(x, axis=-1) * (1 + cb) + sb
    x = x + gb * _L1_ffn_ref(h, L1_ffn_router_w, L1_ffn_router_b, L1_ffn_w_gate, L1_ffn_w_up, L1_ffn_w_down)
    return x

_drawn_inputs = setup_inputs


def setup_inputs(seed=0):
    import zlib

    import numpy as np

    out = dict(_drawn_inputs(seed))
    spreads = {'L1_attn_bo': (0.0, 2.0), 'L1_ffn_router_b': (0.0, 2.0)}
    factors = {'L0_attn_A_log': 8.0,
     'L0_attn_W_in': 8.0,
     'L0_attn_b_in': 8.0,
     'L0_attn_conv_w': 8.0,
     'L0_attn_conv_b': 8.0,
     'L0_attn_W_x': 8.0,
     'L0_attn_W_dt': 8.0,
     'L0_attn_b_dt': 8.0,
     'L0_attn_W_out': 8.0,
     'L0_attn_b_out': 52.704,
     'L0_ffn_Wg': 8.0,
     'L0_ffn_W1': 8.0,
     'L0_ffn_W2': 8.0,
     'L0_ffn_W3': 8.0,
     'L0_c': 6.811,
     'L0_wmod': 6.789,
     'L1_attn_Wq': 8.0,
     'L1_attn_Wk': 8.0,
     'L1_attn_Wv': 2.927,
     'L1_attn_Wo': 2.821,
     'L1_attn_P': 8.0,
     'L1_ffn_router_w': 8.0,
     'L1_ffn_w_gate': 7.74,
     'L1_ffn_w_up': 7.218,
     'L1_ffn_w_down': 7.248}
    for name, (base, spread) in spreads.items():
        noise = np.random.default_rng([zlib.crc32(name.encode()), seed]).standard_normal(out[name].shape)
        drawn = base * np.exp(spread * noise) if base else spread * noise
        out[name] = jnp.asarray(drawn.astype(out[name].dtype))
    for name, factor in factors.items():
        out[name] = (out[name] * factor).astype(out[name].dtype)
    return out
```

```python
import math
from contextlib import ExitStack

import concourse.bass as bass
from concourse import mybir

F32 = mybir.dt.float32
BF16 = mybir.dt.bfloat16
ALU = mybir.AluOpType
ACT = mybir.ActivationFunctionType
AX = mybir.AxisListType
ds = bass.ds

P = 128
T = 2048
CH = 512
NC = T // CH
TPC = CH // P
NT = T // P
DI = 256
HV = DI // P
NS = 16
RK = 64
KW = 3
NE = 8
H0 = 352
H1 = 256
NH, DH, M = 16, 64, 32
NP = NH // 2
FE = NH * M
LN_EPS = 1e-5
FEAT_EPS = 1e-4
DN = DH ** -0.25
RATIO = M ** -0.5


def hidden_tiles(width):
    return [(j, min(P, width - j)) for j in range(0, width, P)]


def build(nc, a, out):
    top = ExitStack()
    with top:
        def sb(name, shape, dt=F32, on=top):
            return on.enter_context(nc.sbuf_tensor(name, shape, dt))

        def sem(name):
            return top.enter_context(nc.semaphore(name))

        PS = top.enter_context(nc.psum_tensor("PS", [P, 8 * CH], F32))

        def bank(b, n=1):
            return PS[:, b * CH:(b + n) * CH]

        x = sb("x", [P, T])
        h = sb("h", [P, T])
        ident = sb("ident", [P, P])
        mean_w = sb("mean_w", [P, P])
        ones = sb("ones", [P, P])
        ln_eps = sb("ln_eps", [P, 1])
        sel = sb("sel", [96, 32, P], BF16)
        cvec = sb("cvec", [P, 2])
        wmod = sb("wmod", [P, 2, 6 * P])
        mod = sb("mod", [P, 2, 6])
        gtmp = sb("gtmp", [P, 2, 2, 2])
        wg = sb("wg", [P, 2, NE])
        rb = sb("rb", [P, NE])
        cw_split = sb("cw_split", [96, T], BF16)

        s_load = sem("s_load")
        s_w0 = sem("s_w0")
        s_w1 = sem("s_w1")
        s_wa = sem("s_wa")

        def layernorm(tag, layer, shift_col, scale_col):
            ctx = ExitStack()
            with ctx:
                xc = sb(f"xc_{tag}", [P, T], on=ctx)
                sq = sb(f"sq_{tag}", [P, T], on=ctx)
                mean_ready = sem(f"mean_ready_{tag}")
                centred = sem(f"centred_{tag}")
                squared = sem(f"squared_{tag}")
                var_ready = sem(f"var_ready_{tag}")
                log_ready = sem(f"log_ready_{tag}")
                rstd_ready = sem(f"rstd_ready_{tag}")
                normed = sem(f"normed_{tag}")

                block = ctx.enter_context(nc.Block())

                @block.tensor
                def _(pe):
                    for c in range(NC):
                        pe.matmul(PS[:, c * CH:(c + 1) * CH], mean_w[:], x[:, c * CH:(c + 1) * CH],
                                  start=True, stop=True).then_inc(mean_ready, 1)
                    for c in range(NC):
                        pe.wait_ge(squared, c + 1)
                        pe.matmul(PS[:, (NC + c) * CH:(NC + c + 1) * CH], mean_w[:], sq[:, c * CH:(c + 1) * CH],
                                  start=True, stop=True).then_inc(var_ready, 1)

                @block.vector
                def _(dve):
                    for c in range(NC):
                        dve.wait_ge(mean_ready, c + 1)
                        dve.tensor_tensor(xc[:, c * CH:(c + 1) * CH], x[:, c * CH:(c + 1) * CH], PS[:, c * CH:(c + 1) * CH],
                                          ALU.subtract).then_inc(centred, 1)
                    for c in range(NC):
                        dve.wait_ge(rstd_ready, c + 1)
                        dve.tensor_tensor(xc[:, c * CH:(c + 1) * CH], xc[:, c * CH:(c + 1) * CH], sq[:, c * CH:(c + 1) * CH],
                                          ALU.mult).then_inc(normed, 1)

                @block.scalar
                def _(act):
                    for c in range(NC):
                        act.wait_ge(centred, c + 1)
                        act.activation(sq[:, c * CH:(c + 1) * CH], xc[:, c * CH:(c + 1) * CH],
                                       ACT.Square).then_inc(squared, 1)
                    for c in range(NC):
                        act.wait_ge(var_ready, c + 1)
                        act.activation(sq[:, c * CH:(c + 1) * CH], PS[:, (NC + c) * CH:(NC + c + 1) * CH], ACT.Ln,
                                       bias=ln_eps[:]).then_inc(log_ready, 1)
                        act.wait_ge(log_ready, c + 1)
                        act.activation(sq[:, c * CH:(c + 1) * CH], sq[:, c * CH:(c + 1) * CH], ACT.Exp,
                                       scale=-0.5).then_inc(rstd_ready, 1)
                    for c in range(NC):
                        act.wait_ge(normed, c + 1)
                        act.activation(h[:, c * CH:(c + 1) * CH], xc[:, c * CH:(c + 1) * CH], ACT.Identity,
                                       bias=mod[:, layer, shift_col:shift_col + 1],
                                       scale=mod[:, layer, scale_col:scale_col + 1])

        def route(tag, layer, den_eps, with_bias):
            ctx = ExitStack()
            with ctx:
                lg = sb(f"lg_{tag}", [P, NT, NE], on=ctx)
                pr = sb(f"pr_{tag}", [P, NT, NE], on=ctx)
                eq = sb(f"eq_{tag}", [P, NT, NE], on=ctx)
                oh = sb(f"oh_{tag}", [P, 2, NT, NE], on=ctx)
                rest = sb(f"rest_{tag}", [P, NT, NE], on=ctx)
                order = sb(f"order_{tag}", [P, NE], on=ctx)
                st = sb(f"st_{tag}", [P, 8, NT], on=ctx)
                cwt = sb(f"cwt_{tag}", [NE, T], on=ctx)
                mid = sb(f"mid_{tag}", [NE, T], BF16, on=ctx)
                logits_ready = sem(f"logits_ready_{tag}")
                shifted = sem(f"shifted_{tag}")
                exp_ready = sem(f"exp_ready_{tag}")
                chain = sem(f"route_step_{tag}")
                cw_ready = sem(f"cw_ready_{tag}")
                cwt_psum = sem(f"cwt_psum_{tag}")
                order_ready = sem(f"order_ready_{tag}")
                block = ctx.enter_context(nc.Block())

                @block.tensor
                def _(pe):
                    for t in range(NT):
                        mm = pe.matmul(PS[:, t * NE:(t + 1) * NE], h[:, t * P:(t + 1) * P], wg[:, layer, :],
                                       start=True, stop=True, skip_group_check=True)
                    mm.then_inc(logits_ready, 1)
                    pe.wait_ge(cw_ready, 1)
                    for t in range(NT):
                        mm = pe.transpose(PS[0:NE, (CH + t * P):(CH + (t + 1) * P)], eq[:, t, :], ident[:])
                    mm.then_inc(cwt_psum, 1)

                @block.gpsimd
                def _(pool):
                    for e in range(NE):
                        i = pool.memset(order[:, e:e + 1], float(NE - e))
                    i.then_inc(order_ready, 1)
                    pool.memset(cw_split[:], 0.0).then_inc(order_ready, 1)

                @block.scalar
                def _(act):
                    act.wait_ge(shifted, 1)
                    act.activation(pr[:], lg[:], ACT.Exp).then_inc(exp_ready, 1)

                @block.vector
                def _(dve):
                    steps = [0]

                    def wide(v):
                        return v.unsqueeze(2).broadcast_to([P, NT, NE])

                    def step(ins):
                        steps[0] += 1
                        ins.then_inc(chain, 1)
                        dve.wait_ge(chain, steps[0])

                    dve.wait_ge(logits_ready, 1)
                    psl = PS[:, 0:NT * NE].rearrange("p (t e) -> p t e", e=NE)
                    if with_bias:
                        step(dve.tensor_tensor(lg[:], psl, rb[:].unsqueeze(1).broadcast_to([P, NT, NE]), ALU.add))
                    else:
                        step(dve.tensor_copy(lg[:], psl))
                    step(dve.tensor_reduce(st[:, 0, :], lg[:], axis=AX.X, op=ALU.max))
                    dve.tensor_tensor(lg[:], lg[:], wide(st[:, 0, :]), ALU.subtract).then_inc(shifted, 1)
                    dve.wait_ge(exp_ready, 1)
                    step(dve.tensor_reduce(st[:, 1, :], pr[:], axis=AX.X, op=ALU.add))
                    step(dve.reciprocal(st[:, 2, :], st[:, 1, :]))
                    step(dve.tensor_tensor(pr[:], pr[:], wide(st[:, 2, :]), ALU.mult))
                    dve.wait_ge(order_ready, 2)
                    left = pr
                    for k in range(2):
                        step(dve.tensor_reduce(st[:, 3 + k, :], left[:], axis=AX.X, op=ALU.max))
                        step(dve.tensor_tensor(eq[:], left[:], wide(st[:, 3 + k, :]), ALU.is_equal))
                        step(dve.tensor_tensor(eq[:], eq[:], order[:].unsqueeze(1).broadcast_to([P, NT, NE]),
                                               ALU.mult))
                        step(dve.tensor_reduce(st[:, 5, :], eq[:], axis=AX.X, op=ALU.max))
                        step(dve.tensor_tensor(oh[:, k], eq[:], wide(st[:, 5, :]), ALU.is_equal))
                        if k == 0:
                            step(dve.scalar_tensor_tensor(rest[:], oh[:, 0], -2.0, pr[:], ALU.mult, ALU.add))
                            left = rest
                    step(dve.scalar_tensor_tensor(st[:, 6, :], st[:, 3, :], den_eps, st[:, 4, :], ALU.add, ALU.add))
                    step(dve.reciprocal(st[:, 7, :], st[:, 6, :]))
                    step(dve.tensor_tensor(oh[:, 0], oh[:, 0], oh[:, 1], ALU.add))
                    step(dve.tensor_tensor(oh[:, 0], oh[:, 0], pr[:], ALU.mult))
                    dve.tensor_tensor(eq[:], oh[:, 0], wide(st[:, 7, :]), ALU.mult).then_inc(cw_ready, 1)
                    dve.wait_ge(cwt_psum, 1)
                    step(dve.tensor_copy(cwt[:], PS[0:NE, CH:CH + T]))
                    step(dve.tensor_copy(cw_split[0:NE, :], cwt[:]))
                    step(dve.tensor_tensor(cwt[:], cwt[:], cw_split[0:NE, :], ALU.subtract))
                    step(dve.tensor_copy(mid[:], cwt[:]))
                    step(dve.tensor_copy(cw_split[32:32 + NE, :], mid[:]))
                    step(dve.tensor_tensor(cw_split[64:64 + NE, :], cwt[:], mid[:], ALU.subtract))

        def experts(tag, width, wgate, wup, wdown, gate_col, layer, weights_sem, weights_count):
            ctx = ExitStack()
            with ctx:
                tiles = [(e, j, o, m) for e in range(NE) for j, (o, m) in enumerate(hidden_tiles(width))]
                NI = len(tiles)
                NJ = NI // NE
                LAG = 2
                RG, RU, RH, RW = 2, 3, 3, 2
                sg = sb(f"sg_{tag}", [P, RH, CH], on=ctx)
                sw = sb(f"sw_{tag}", [P, RH, CH], on=ctx)
                hid = sb(f"hid_{tag}", [P, RH, CH], on=ctx)
                cwb = sb(f"cwb_{tag}", [P, RW, CH], on=ctx)
                gate_ready = sem(f"gate_ready_{tag}")
                up_ready = sem(f"up_ready_{tag}")
                spread_ready = sem(f"spread_ready_{tag}")
                silu_ready = sem(f"silu_ready_{tag}")
                cwb_ready = sem(f"cwb_ready_{tag}")
                weighed = sem(f"weighed_{tag}")
                hid_ready = sem(f"hid_ready_{tag}")
                down_done = sem(f"down_done_{tag}")
                added = sem(f"added_{tag}")
                block = ctx.enter_context(nc.Block())
                BW, BO = RG + RU, RG + RU + 1

                @block.tensor
                def _(pe):
                    pe.wait_ge(weights_sem, weights_count)
                    pe.sem_inc(down_done, RH)
                    with pe.Fori(0, NC) as c:
                        hc = h[:, ds(c * CH, CH)]

                        def down(i):
                            e, j, o, m = tiles[i]
                            pe.wait_ge(hid_ready, c * NI + (RU + i + 1))
                            if i == 0:
                                pe.wait_ge(added, c + 1)
                            pe.matmul(bank(BO), wdown[0:m, e * NJ + j, :], hid[0:m, i % RH, :],
                                      start=(i == 0), stop=(i == NI - 1)).then_inc(down_done, 1)

                        for i, (e, j, o, m) in enumerate(tiles):
                            if j == 0:
                                pe.wait_ge(cwb_ready, c * NE + e + 1)
                                pe.matmul(bank(BW), sel[:, e, :], cw_split[:, ds(c * CH, CH)],
                                          start=True, stop=True).then_inc(spread_ready, 1)
                            w0 = e * width + o
                            pe.wait_ge(silu_ready, c * NI + i + 1)
                            pe.matmul(bank(i % RG)[0:m], wgate[:, w0:w0 + m], hc,
                                      start=True, stop=True).then_inc(gate_ready, 1)
                            pe.wait_ge(hid_ready, c * NI + i + 1)
                            pe.matmul(bank(RG + i % RU)[0:m], wup[:, w0:w0 + m], hc,
                                      start=True, stop=True).then_inc(up_ready, 1)
                            if i >= LAG:
                                down(i - LAG)
                        for i in range(NI - LAG, NI):
                            down(i)

                @block.scalar
                def _(act):
                    act.sem_inc(silu_ready, RG)
                    act.sem_inc(cwb_ready, 1)
                    with act.Fori(0, NC) as c:
                        for i, (e, j, o, m) in enumerate(tiles):
                            act.wait_ge(gate_ready, c * NI + i + 1)
                            act.wait_ge(weighed, c * NI + i + 1)
                            act.activation(sg[0:m, i % RH, :], bank(i % RG)[0:m], ACT.Silu).then_inc(silu_ready, 1)
                            if j == 0:
                                act.wait_ge(spread_ready, c * NE + e + 1)
                                act.activation(cwb[:, e % RW, :], bank(BW), ACT.Copy).then_inc(cwb_ready, 1)

                @block.gpsimd
                def _(pool):
                    pool.sem_inc(weighed, RH)
                    with pool.Fori(0, NC) as c:
                        for i, (e, j, o, m) in enumerate(tiles):
                            pool.wait_ge(silu_ready, c * NI + (RG + i + 1))
                            if j == 0:
                                pool.wait_ge(cwb_ready, c * NE + (e + 2))
                            pool.wait_ge(hid_ready, c * NI + i + (RU - RH + 1))
                            pool.tensor_tensor(sw[0:m, i % RH, :], sg[0:m, i % RH, :], cwb[0:m, e % RW, :],
                                               ALU.mult).then_inc(weighed, 1)

                @block.vector
                def _(dve):
                    dve.sem_inc(hid_ready, RU)
                    dve.sem_inc(added, 1)
                    with dve.Fori(0, NC) as c:
                        for i, (e, j, o, m) in enumerate(tiles):
                            dve.wait_ge(up_ready, c * NI + i + 1)
                            dve.wait_ge(weighed, c * NI + (RH + i + 1))
                            dve.wait_ge(down_done, c * NI + i + 1)
                            dve.tensor_tensor(hid[0:m, i % RH, :], sw[0:m, i % RH, :],
                                              bank(RG + i % RU)[0:m], ALU.mult).then_inc(hid_ready, 1)
                        dve.wait_ge(down_done, c * NI + (RH + NI))
                        xc = x[:, ds(c * CH, CH)]
                        dve.scalar_tensor_tensor(xc, bank(BO), mod[:, layer, gate_col:gate_col + 1], xc,
                                                 ALU.mult, ALU.add).then_inc(added, 1)

        ab = ExitStack()
        w_in = sb("w_in", [P, 2 * DI], on=ab)
        b_in = sb("b_in", [P, 2 * HV], on=ab)
        conv_w = sb("conv_w", [P, HV, KW], on=ab)
        conv_b = sb("conv_b", [P, HV], on=ab)
        w_x = sb("w_x", [P, HV, RK + 2 * NS], on=ab)
        w_dt = sb("w_dt", [RK, DI], on=ab)
        b_dt = sb("b_dt", [P, HV], on=ab)
        w_out = sb("w_out", [P, HV, P], on=ab)
        b_out = sb("b_out", [P, 1], on=ab)
        a_neg = sb("a_neg", [P, HV, NS], on=ab)
        ga_b = sb("ga_b", [P, 1], on=ab)

        small_loads = [
            (x[:], a["x"]), (cvec[:], a["c"]), (wmod[:, 0, :], a["wmod0"]), (wmod[:, 1, :], a["wmod1"]),
            (w_in[:], a["w_in"]), (b_in[:], a["b_in"]), (conv_w[:], a["conv_w"]), (conv_b[:], a["conv_b"]),
            (w_x[:], a["w_x"]), (w_dt[:], a["w_dt"]), (b_dt[:], a["b_dt"]), (w_out[:], a["w_out"]),
            (b_out[:], a["b_out"]), (a_neg[:], a["a_log"]), (wg[:], a["wg"]),
            (rb[:], a["router_b"].partition_broadcast(P)),
        ]
        n_small = 16 * len(small_loads)

        s_const = sem("s_const")
        s_silu_c = sem("s_silu_c")
        s_mod = sem("s_mod")
        s_gate = sem("s_gate")
        s_setup = sem("s_setup")
        blk = ExitStack()
        with blk:
            block = blk.enter_context(nc.Block())

            @block.sync
            def _(sp):
                for dst, src in small_loads:
                    sp.dma_start(dst, src).then_inc(s_load, 16)

            @block.gpsimd
            def _(pool):
                pool.memset(ident[:], 0.0).then_inc(s_const, 1)
                pool.memset(ones[:], 1.0).then_inc(s_const, 1)
                pool.memset(mean_w[:], 1.0 / P).then_inc(s_const, 1)
                pool.memset(ln_eps[:], LN_EPS).then_inc(s_const, 1)
                pool.memset(sel[:], 0.0).then_inc(s_const, 1)
                pool.wait_ge(s_const, 5)
                pool.affine_select(out=ident[:], in_=ident[:], compare_op=ALU.not_equal, fill=1.0,
                                   base=0, pattern=[[-1, P]], channel_multiplier=1).then_inc(s_const, 1)
                for g in range(3):
                    pool.affine_select(out=sel[:], in_=sel[:], compare_op=ALU.not_equal, fill=1.0,
                                       base=-32 * g, pattern=[[-1, 32], [0, P]],
                                       channel_multiplier=1).then_inc(s_const, 1)
                    pool.wait_ge(s_const, 7 + g)

            @block.scalar
            def _(act):
                act.wait_ge(s_load, n_small)
                act.activation(cvec[:], cvec[:], ACT.Silu).then_inc(s_silu_c, 1)
                act.activation(a_neg[:], a_neg[:], ACT.Exp).then_inc(s_silu_c, 1)

            @block.tensor
            def _(pe):
                pe.wait_ge(s_silu_c, 1)
                for l in range(2):
                    for k in range(6):
                        mm = pe.matmul(PS[:, 6 * l + k:6 * l + k + 1], wmod[:, l, k * P:(k + 1) * P],
                                       cvec[:, l:l + 1], start=True, stop=True, skip_group_check=True)
                mm.then_inc(s_mod, 1)

            @block.vector
            def _(dve):
                dve.wait_ge(s_mod, 1)
                dve.tensor_copy(mod[:], PS[:, 0:12].rearrange("p (l k) -> p l k", l=2)).then_inc(s_gate, 1)
                dve.wait_ge(s_gate, 1)
                gates = mod[:, :, 2:6:3]
                dve.scalar_tensor_tensor(gtmp[:, 0], gates, -1.0, gates, ALU.mult, ALU.max).then_inc(s_gate, 1)
                dve.tensor_scalar(gtmp[:, 1], gates, 0.0, 2.0, ALU.is_ge, ALU.mult).then_inc(s_gate, 1)
                dve.wait_ge(s_gate, 3)
                dve.tensor_scalar(gtmp[:, 1], gtmp[:, 1], -1.0, None, ALU.add).then_inc(s_gate, 1)
                dve.wait_ge(s_gate, 4)
                dve.scalar_tensor_tensor(gates, gtmp[:, 0], 0.25, gtmp[:, 1], ALU.max, ALU.mult).then_inc(s_gate, 1)
                dve.tensor_scalar(mod[:, :, 1:6:3], mod[:, :, 1:6:3], 1.0, None, ALU.add).then_inc(s_gate, 1)
                dve.wait_ge(s_gate, 6)
                dve.tensor_tensor(ga_b[:], mod[:, 0, 2:3], b_out[:], ALU.mult).then_inc(s_setup, 1)
                dve.wait_ge(s_silu_c, 2)
                dve.tensor_scalar(a_neg[:], a_neg[:], -1.0, None, ALU.mult).then_inc(s_setup, 1)

        layernorm("a0", 0, 0, 1)

        sc = ExitStack()
        u = sb("u", [P, HV, T], on=sc)
        rg = sb("rg", [P, HV, T], on=sc)
        delta = sb("delta", [P, HV, T], on=sc)
        bc_split = sb("bc_split", [96, T], BF16, on=sc)

        def scan_inputs():
            ctx = ExitStack()
            with ctx:
                ur = sb("ur", [P, HV, T + KW - 1], on=ctx)
                cv = sb("cv", [P, HV, CH], on=ctx)
                taps = sb("taps", [P, HV, CH], on=ctx)
                dt = sb("dt", [RK, T], on=ctx)
                bc = sb("bc", [2 * NS, T], on=ctx)
                bc_mid = sb("bc_mid", [2 * NS, T], BF16, on=ctx)
                soft = sb("soft", [P, 2, HV, CH], on=ctx)
                pad_ready = sem("pad_ready")
                xr_ready = sem("xr_ready")
                ur_ready = sem("ur_ready")
                rg_ready = sem("rg_ready")
                conv_step = sem("conv_step")
                conv_ready = sem("conv_ready")
                u_ready = sem("u_ready")
                xp_ready = sem("xp_ready")
                xp_read = sem("xp_read")
                split_step = sem("split_step")
                v_ready = sem("v_ready")
                v_abs = sem("v_abs")
                v_max = sem("v_max")
                soft_exp = sem("soft_exp")
                soft_ln = sem("soft_ln")
                delta_ready = sem("delta_ready")
                block = ctx.enter_context(nc.Block())

                @block.gpsimd
                def _(pool):
                    pool.memset(ur[:, :, 0:KW - 1], 0.0).then_inc(pad_ready, 1)

                @block.tensor
                def _(pe):
                    with pe.Fori(0, NC) as c:
                        for j in range(2 * HV):
                            if j < HV:
                                pe.wait_ge(ur_ready, c * HV + (j + 1))
                            else:
                                pe.wait_ge(rg_ready, c * HV + (j - HV + 1))
                            pe.matmul(bank(j), w_in[:, j * P:(j + 1) * P], h[:, ds(c * CH, CH)],
                                      start=True, stop=True).then_inc(xr_ready, 1)
                        pe.wait_ge(xp_read, 2 * c + 2)
                        for j in range(HV):
                            pe.wait_ge(u_ready, c * HV + (HV + j + 1))
                            mm = pe.matmul(bank(4)[0:RK + 2 * NS], w_x[:, j, :], u[:, j, ds(c * CH, CH)],
                                           start=(j == 0), stop=(j == HV - 1))
                        mm.then_inc(xp_ready, 1)
                    for c in range(NC):
                        for j in range(HV):
                            pe.wait_ge(xp_read, 2 * NC + 2)
                            pe.wait_ge(v_max, c * HV + (j + 1))
                            pe.wait_ge(v_abs, c * HV + (j + 1))
                            pe.matmul(bank(5 + j), w_dt[:, j * P:(j + 1) * P], dt[:, c * CH:(c + 1) * CH],
                                      start=True, stop=True).then_inc(v_ready, 1)

                @block.scalar
                def _(act):
                    act.sem_inc(ur_ready, HV)
                    act.sem_inc(rg_ready, HV)
                    act.sem_inc(u_ready, HV)
                    act.sem_inc(xp_read, 2)
                    act.sem_inc(v_abs, HV)
                    with act.Fori(0, NC) as c:
                        for j in range(HV):
                            act.wait_ge(xr_ready, c * 2 * HV + (j + 1))
                            act.activation(ur[:, j, ds(c * CH + (KW - 1), CH)], bank(j), ACT.Identity,
                                           bias=b_in[:, j:j + 1]).then_inc(ur_ready, 1)
                        for j in range(HV):
                            act.wait_ge(xr_ready, c * 2 * HV + (HV + j + 1))
                            act.activation(rg[:, j, ds(c * CH, CH)], bank(HV + j), ACT.Silu,
                                           bias=b_in[:, HV + j:HV + j + 1]).then_inc(rg_ready, 1)
                        for j in range(HV):
                            act.wait_ge(conv_ready, c * HV + (j + 1))
                            act.activation(u[:, j, ds(c * CH, CH)], cv[:, j, :], ACT.Silu).then_inc(u_ready, 1)
                        act.wait_ge(xp_ready, c + 1)
                        act.activation(dt[:, ds(c * CH, CH)], bank(4)[0:RK], ACT.Copy).then_inc(xp_read, 1)
                        act.activation(bc[:, ds(c * CH, CH)], bank(4)[RK:RK + 2 * NS], ACT.Copy).then_inc(xp_read, 1)
                    with act.Fori(0, NC) as c:
                        for j in range(HV):
                            act.wait_ge(v_ready, c * HV + (j + 1))
                            act.wait_ge(delta_ready, c * HV + (j + 1))
                            act.activation(soft[:, 0, j, :], bank(5 + j), ACT.Abs,
                                           bias=b_dt[:, j:j + 1]).then_inc(v_abs, 1)
                            act.wait_ge(v_abs, c * HV + (HV + j + 1))
                            act.activation(soft[:, 0, j, :], soft[:, 0, j, :], ACT.Exp,
                                           scale=-1.0).then_inc(soft_exp, 1)
                            act.wait_ge(soft_exp, c * HV + (j + 1))
                            act.activation(soft[:, 0, j, :], soft[:, 0, j, :], ACT.Ln,
                                           bias=ones[:, 0:1]).then_inc(soft_ln, 1)

                @block.vector
                def _(dve):
                    dve.sem_inc(v_max, HV)
                    dve.sem_inc(delta_ready, HV)
                    dve.wait_ge(pad_ready, 1)
                    with dve.Fori(0, NC) as c:
                        for j in range(HV):
                            dve.wait_ge(ur_ready, c * HV + (HV + j + 1))
                            dve.tensor_scalar(taps[:, j, :], ur[:, j, ds(c * CH, CH)], conv_w[:, j, 0:1],
                                              conv_b[:, j:j + 1], ALU.mult, ALU.add).then_inc(conv_step, 1)
                            dve.wait_ge(conv_step, c * 2 * HV + (2 * j + 1))
                            dve.scalar_tensor_tensor(taps[:, j, :], ur[:, j, ds(c * CH + 1, CH)],
                                                     conv_w[:, j, 1:2], taps[:, j, :],
                                                     ALU.mult, ALU.add).then_inc(conv_step, 1)
                            dve.wait_ge(conv_step, c * 2 * HV + (2 * j + 2))
                            dve.wait_ge(u_ready, c * HV + (j + 1))
                            dve.scalar_tensor_tensor(cv[:, j, :], ur[:, j, ds(c * CH + 2, CH)], conv_w[:, j, 2:3],
                                                     taps[:, j, :], ALU.mult, ALU.add).then_inc(conv_ready, 1)
                            dve.wait_ge(conv_ready, c * HV + (j + 1))
                    dve.wait_ge(xp_read, 2 * NC + 2)
                    dve.tensor_copy(bc_split[0:2 * NS, :], bc[:]).then_inc(split_step, 1)
                    dve.wait_ge(split_step, 1)
                    dve.tensor_tensor(bc[:], bc[:], bc_split[0:2 * NS, :], ALU.subtract).then_inc(split_step, 1)
                    dve.wait_ge(split_step, 2)
                    dve.tensor_copy(bc_mid[:], bc[:]).then_inc(split_step, 1)
                    dve.wait_ge(split_step, 3)
                    dve.tensor_copy(bc_split[32:32 + 2 * NS, :], bc_mid[:])
                    dve.tensor_tensor(bc_split[64:64 + 2 * NS, :], bc[:], bc_mid[:], ALU.subtract)
                    with dve.Fori(0, NC) as c:
                        for j in range(HV):
                            dve.wait_ge(v_abs, c * HV + (HV + j + 1))
                            dve.tensor_scalar(soft[:, 1, j, :], bank(5 + j), b_dt[:, j:j + 1], 0.0,
                                              ALU.add, ALU.max).then_inc(v_max, 1)
                        for j in range(HV):
                            dve.wait_ge(soft_ln, c * HV + (j + 1))
                            dve.wait_ge(v_max, c * HV + (HV + j + 1))
                            dve.tensor_tensor(delta[:, j, ds(c * CH, CH)], soft[:, 0, j, :], soft[:, 1, j, :],
                                              ALU.add).then_inc(delta_ready, 1)
                            dve.wait_ge(delta_ready, c * HV + (HV + j + 1))
                            dve.tensor_tensor(u[:, j, ds(c * CH, CH)], u[:, j, ds(c * CH, CH)],
                                              delta[:, j, ds(c * CH, CH)], ALU.mult)

        def scan():
            ctx = ExitStack()
            with ctx:
                RB, RP = 2, 2
                st = sb("st", [P, NS, HV, CH], on=ctx)
                da = sb("da", [P, RB, HV, CH], on=ctx)
                db = sb("db", [P, RB, HV, CH], on=ctx)
                cs = sb("cs", [P, RB, CH], on=ctx)
                prod = sb("prod", [P, RP, HV, CH], on=ctx)
                yg = sb("yg", [P, HV, CH], on=ctx)
                ob = sb("ob", [P, CH], on=ctx)
                dl = sb("dl", [P, HV, CH], on=ctx)
                dl_ready = sem("dl_ready")
                st_zero = sem("st_zero")
                b_spread = sem("b_spread")
                c_spread = sem("c_spread")
                cs_ready = sem("cs_ready")
                da_ready = sem("da_ready")
                db_ready = sem("db_ready")
                st_ready = sem("st_ready")
                prod_ready = sem("prod_ready")
                y_added = sem("y_added")
                yg_ready = sem("yg_ready")
                o_ready = sem("o_ready")
                ob_ready = sem("ob_ready")
                x_added = sem("x_added")
                block = ctx.enter_context(nc.Block())
                B_BANK, C_BANK, Y_BANK, O_BANK = 0, 2, 4, 6

                @block.tensor
                def _(pe):
                    pe.sem_inc(y_added, RP)
                    with pe.Fori(0, NC) as c:
                        def add_y(n):
                            pe.wait_ge(prod_ready, c * NS + (NS + n + 1))
                            if n == 0:
                                pe.wait_ge(yg_ready, c + 1)
                            for j in range(HV):
                                mm = pe.matmul(bank(Y_BANK + j), ident[:], prod[:, n % RP, j, :],
                                               start=(n == 0), stop=(n == NS - 1))
                            mm.then_inc(y_added, 1)

                        for n in range(NS):
                            pe.wait_ge(db_ready, c * NS + (n + 1))
                            pe.matmul(bank(B_BANK + n % RB), sel[:, n, :], bc_split[:, ds(c * CH, CH)],
                                      start=True, stop=True).then_inc(b_spread, 1)
                            pe.wait_ge(cs_ready, c * NS + (n + 1))
                            pe.matmul(bank(C_BANK + n % RB), sel[:, NS + n, :], bc_split[:, ds(c * CH, CH)],
                                      start=True, stop=True).then_inc(c_spread, 1)
                            if n > 0:
                                add_y(n - 1)
                        add_y(NS - 1)
                        pe.wait_ge(yg_ready, c + 2)
                        pe.wait_ge(ob_ready, c + 1)
                        for j in range(HV):
                            mm = pe.matmul(bank(O_BANK), w_out[:, j, :], yg[:, j, :],
                                           start=(j == 0), stop=(j == HV - 1))
                        mm.then_inc(o_ready, 1)

                @block.scalar
                def _(act):
                    act.sem_inc(cs_ready, RB)
                    act.sem_inc(ob_ready, 1)
                    with act.Fori(0, NC) as c:
                        act.activation(dl[:], delta[:, :, ds(c * CH, CH)], ACT.Copy).then_inc(dl_ready, 1)
                        act.wait_ge(dl_ready, c + 1)
                        for n in range(NS):
                            act.wait_ge(st_ready, (c * NS + n) * HV + HV)
                            for j in range(HV):
                                act.activation(da[:, n % RB, j, :], dl[:, j, :], ACT.Exp,
                                               scale=a_neg[:, j, n:n + 1]).then_inc(da_ready, 1)
                            act.wait_ge(c_spread, c * NS + (n + 1))
                            act.wait_ge(prod_ready, c * NS + (n + NS - RB + 1))
                            act.activation(cs[:, n % RB, :], bank(C_BANK + n % RB), ACT.Copy).then_inc(cs_ready, 1)
                        act.wait_ge(o_ready, c + 1)
                        act.wait_ge(x_added, c + 1)
                        act.activation(ob[:], bank(O_BANK), ACT.Identity, bias=ga_b[:],
                                       scale=mod[:, 0, 2:3]).then_inc(ob_ready, 1)

                @block.gpsimd
                def _(pool):
                    for n in range(NS):
                        i = pool.memset(st[:, n, :, CH - 1:CH], 0.0)
                    i.then_inc(st_zero, 1)
                    pool.sem_inc(prod_ready, NS)
                    with pool.Fori(0, NC) as c:
                        for n in range(NS):
                            pool.wait_ge(st_ready, (c * NS + (n + RB)) * HV + HV)
                            pool.wait_ge(cs_ready, c * NS + (RB + n + 1))
                            pool.wait_ge(y_added, c * NS + (n + 1))
                            pool.tensor_tensor(prod[:, n % RP], st[:, n],
                                               cs[:, n % RB, :].unsqueeze(1).broadcast_to([P, HV, CH]),
                                               ALU.mult).then_inc(prod_ready, 1)

                @block.vector
                def _(dve):
                    dve.sem_inc(db_ready, RB)
                    dve.sem_inc(st_ready, RB * HV)
                    dve.sem_inc(yg_ready, 1)
                    dve.sem_inc(x_added, 1)
                    dve.wait_ge(st_zero, 1)
                    with dve.Fori(0, NC) as c:
                        for n in range(NS):
                            dve.wait_ge(b_spread, c * NS + (n + 1))
                            dve.wait_ge(st_ready, (c * NS + n) * HV + HV)
                            dve.tensor_tensor(db[:, n % RB], u[:, :, ds(c * CH, CH)],
                                              bank(B_BANK + n % RB).unsqueeze(1).broadcast_to([P, HV, CH]),
                                              ALU.mult).then_inc(db_ready, 1)
                            dve.wait_ge(db_ready, c * NS + (RB + n + 1))
                            dve.wait_ge(prod_ready, c * NS + (n + 1))
                            for j in range(HV):
                                dve.wait_ge(da_ready, (c * NS + n) * HV + (j + 1))
                                dve.tensor_tensor_scan(st[:, n, j, :], da[:, n % RB, j, :], db[:, n % RB, j, :],
                                                       initial=st[:, n, j, CH - 1:CH],
                                                       op0=ALU.mult, op1=ALU.add).then_inc(st_ready, 1)
                        dve.wait_ge(y_added, c * NS + (RP + NS))
                        dve.tensor_tensor(yg[:], bank(Y_BANK, 2).rearrange("p (j t) -> p j t", j=HV),
                                          rg[:, :, ds(c * CH, CH)], ALU.mult).then_inc(yg_ready, 1)
                        dve.wait_ge(ob_ready, c + 2)
                        dve.tensor_tensor(x[:, ds(c * CH, CH)], x[:, ds(c * CH, CH)], ob[:],
                                          ALU.add).then_inc(x_added, 1)

        scan_inputs()
        scan()
        sc.close()
        ab.close()

        eb = ExitStack()
        w1_0 = sb("w1_0", [P, NE * H0], on=eb)
        w3_0 = sb("w3_0", [P, NE * H0], on=eb)
        nj0 = len(hidden_tiles(H0))
        w2_0 = sb("w2_0", [P, NE * nj0, P], on=eb)
        full = (H0 // P) * P
        ld = ExitStack()
        with ld:
            block = ld.enter_context(nc.Block())

            @block.sync
            def _(sp):
                sp.dma_start(w1_0[:], a["w1_0"]).then_inc(s_w0, 16)
                sp.dma_start(w3_0[:], a["w3_0"]).then_inc(s_w0, 16)
                for e in range(NE):
                    sp.dma_start(w2_0[:, e * nj0:(e + 1) * nj0 - 1, :],
                                 a["w2_0"][e, 0:full, :].rearrange("(j p) d -> p j d", p=P)).then_inc(s_w0, 16)
                    sp.dma_start(w2_0[0:H0 - full, (e + 1) * nj0 - 1, :],
                                 a["w2_0"][e, full:H0, :]).then_inc(s_w0, 16)
        layernorm("f0", 0, 3, 4)
        route("f0", 0, 1e-20, False)
        experts("f0", H0, w1_0, w3_0, w2_0, 5, 0, s_w0, 16 * (2 + 2 * NE))
        eb.close()

        wb = ExitStack()
        w1_1 = sb("w1_1", [P, NE * H1], on=wb)
        w3_1 = sb("w3_1", [P, NE * H1], on=wb)
        nj1 = H1 // P
        w2_1 = sb("w2_1", [P, NE * nj1, P], on=wb)
        tb = ExitStack()
        wq = sb("wq", [P, NH * DH], on=tb)
        wk = sb("wk", [P, NH * DH], on=tb)
        wv = sb("wv", [P, NH * DH], on=tb)
        wo = sb("wo", [P, NP, P], on=tb)
        wqt = sb("wqt", [P, NP, P], on=tb)
        wkt = sb("wkt", [P, NP, P], on=tb)
        bo = sb("bo", [P, 1], on=tb)
        pt2 = sb("pt2", [P, 2 * M], on=tb)
        wqp = sb("wqp", [P, FE], on=tb)
        wkp = sb("wkp", [P, FE], on=tb)
        pair_ones = sb("pair_ones", [P, 2], on=tb)
        ga_bo = sb("ga_bo", [P, 1], on=tb)
        attn_loads = [(wq[:], a["wq"]), (wk[:], a["wk"]), (wv[:], a["wv"]), (bo[:], a["bo"]),
                      (wo[:], a["wo"].rearrange("(j p) d -> p j d", p=P)),
                      (wqt[:], a["wqt"].rearrange("(j p) d -> p j d", p=P)),
                      (wkt[:], a["wkt"].rearrange("(j p) d -> p j d", p=P)),
                      (pt2[0:DH, 0:M], a["pt"]), (pt2[DH:P, M:2 * M], a["pt"])]
        zero_ready = sem("zero_ready")
        feat_w_ready = sem("feat_w_ready")
        ld = ExitStack()
        with ld:
            block = ld.enter_context(nc.Block())

            @block.sync
            def _(sp):
                sp.wait_ge(zero_ready, 1)
                for dst, src in attn_loads:
                    sp.dma_start(dst, src).then_inc(s_wa, 16)
                sp.dma_start(w1_1[:], a["w1_1"]).then_inc(s_w1, 16)
                sp.dma_start(w3_1[:], a["w3_1"]).then_inc(s_w1, 16)
                sp.dma_start(w2_1[:], a["w2_1"].rearrange("(j p) d -> p j d", p=P)).then_inc(s_w1, 16)

            @block.gpsimd
            def _(pool):
                pool.memset(pt2[:], 0.0).then_inc(zero_ready, 1)
                pool.memset(pair_ones[:], 0.0).then_inc(zero_ready, 1)
                pool.wait_ge(zero_ready, 2)
                pool.memset(pair_ones[0:DH, 0:1], 1.0)
                pool.memset(pair_ones[DH:P, 1:2], 1.0)

            @block.tensor
            def _(pe):
                pe.wait_ge(s_wa, 16 * len(attn_loads))
                for b, wt in enumerate((wqt, wkt)):
                    for p in range(NP):
                        mm = pe.matmul(PS[:, b * CH + p * 2 * M:b * CH + (p + 1) * 2 * M], wt[:, p, :], pt2[:],
                                       start=True, stop=True, skip_group_check=True)
                    mm.then_inc(feat_w_ready, 1)

            @block.scalar
            def _(act):
                for b, w in enumerate((wqp, wkp)):
                    act.wait_ge(feat_w_ready, b + 1)
                    act.activation(w[:], bank(b), ACT.Copy, scale=DN)

            @block.vector
            def _(dve):
                dve.wait_ge(s_wa, 16 * len(attn_loads))
                dve.tensor_tensor(ga_bo[:], mod[:, 1, 2:3], bo[:], ALU.mult)

        layernorm("a1", 1, 0, 1)

        fb = ExitStack()
        hx = sb("hx", [P, NT, P], on=fb)
        fk = sb("fk", [P, NT, FE], on=fb)
        fq = sb("fq", [P, NT, FE], on=fb)
        kmax = sb("kmax", [P, NT], on=fb)

        def heads(v):
            return v.rearrange("p (h m) -> p h m", m=M)

        def wide_m(v):
            return v.unsqueeze(2).broadcast_to([P, NH, M])

        def features():
            ctx = ExitStack()
            with ctx:
                hs = sb("hs", [P, CH], on=ctx)
                sq = sb("sq", [P, 2, NP, CH], on=ctx)
                dg = sb("dg", [P, 2, 2, NH], on=ctx)
                mq = sb("mq", [P, 2, NH], on=ctx)
                bq = sb("bq", [P, 2, NH], on=ctx)
                hs_ready = sem("hs_ready")
                proj_ready = sem("proj_ready")
                sq_ready = sem("sq_ready")
                dd_ready = sem("dd_ready")
                dg_ready = sem("dg_ready")
                dg_read = sem("dg_read")
                k_read = sem("k_read")
                hx_psum = sem("hx_psum")
                hx_ready = sem("hx_ready")
                q_max = sem("q_max")
                q_bias = sem("q_bias")
                q_shift = sem("q_shift")
                q_exp = sem("q_exp")
                block = ctx.enter_context(nc.Block())
                OPS = 2 * NP

                @block.vector
                def _(dve):
                    dve.sem_inc(k_read, 2)
                    dve.sem_inc(q_shift, 2)
                    with dve.Fori(0, NC) as c:
                        dve.wait_ge(dd_ready, c * TPC + 1)
                        dve.tensor_copy(hs[:], h[:, ds(c * CH, CH)]).then_inc(hs_ready, 1)
                        for t in range(TPC):
                            r = t % 2
                            dve.wait_ge(dd_ready, c * TPC + (t + 2))
                            dve.wait_ge(dg_read, c * TPC + (t + 2))
                            dve.tensor_reduce(kmax[:, ds(c * TPC + t, 1)], bank(2 + r), axis=AX.X, op=ALU.max)
                            dve.tensor_tensor(fk[:, ds(c * TPC + t, 1), :].rearrange("p a (h m) -> p (a h) m", m=M),
                                              heads(bank(2 + r)), wide_m(dg[:, r, 0, :]),
                                              ALU.subtract).then_inc(k_read, 1)
                            dve.tensor_reduce(mq[:, r, :], heads(bank(4 + r)), axis=AX.X,
                                              op=ALU.max).then_inc(q_max, 1)
                            dve.wait_ge(q_max, c * TPC + (t + 1))
                            dve.tensor_tensor(bq[:, r, :], mq[:, r, :], dg[:, r, 1, :], ALU.add).then_inc(q_bias, 1)
                            dve.wait_ge(q_bias, c * TPC + (t + 1))
                            dve.tensor_tensor(fq[:, ds(c * TPC + t, 1), :].rearrange("p a (h m) -> p (a h) m", m=M),
                                              heads(bank(4 + r)), wide_m(bq[:, r, :]),
                                              ALU.subtract).then_inc(q_shift, 1)

                @block.tensor
                def _(pe):
                    pe.sem_inc(dd_ready, 1)
                    with pe.Fori(0, NC) as c:
                        for i in range(OPS):
                            w = (wk, wq)[i // NP]
                            p = i % NP
                            pe.wait_ge(sq_ready, c * OPS + (i + 1))
                            pe.matmul(bank(i % 2), w[:, p * P:(p + 1) * P], h[:, ds(c * CH, CH)],
                                      start=True, stop=True).then_inc(proj_ready, 1)
                        pe.wait_ge(hs_ready, c + 1)
                        pe.wait_ge(sq_ready, c * OPS + (OPS + 2))
                        for t in range(TPC):
                            r = t % 2
                            tok = slice(t * P, (t + 1) * P)
                            pe.wait_ge(dg_read, c * TPC + (t + 1))
                            for s in range(2):
                                for p in range(NP):
                                    col = 6 * CH + s * NH + 2 * p
                                    mm = pe.matmul(PS[:, col:col + 2], sq[:, s, p, tok], pair_ones[:],
                                                   start=True, stop=True, skip_group_check=True)
                            mm.then_inc(dg_ready, 1)
                            pe.wait_ge(hx_ready, c * TPC + (t + 1))
                            pe.transpose(PS[:, 7 * CH:7 * CH + P], hs[:, tok],
                                         ident[:]).then_inc(hx_psum, 1)
                            pe.wait_ge(k_read, c * TPC + (t + 1))
                            pe.matmul(bank(2 + r), hs[:, tok], wkp[:], start=True, stop=True)
                            pe.wait_ge(q_shift, c * TPC + (t + 1))
                            pe.matmul(bank(4 + r), hs[:, tok], wqp[:], start=True, stop=True).then_inc(dd_ready, 1)

                @block.scalar
                def _(act):
                    act.sem_inc(sq_ready, 2)
                    act.sem_inc(dg_read, 1)
                    act.sem_inc(hx_ready, 1)
                    with act.Fori(0, NC) as c:
                        for i in range(OPS):
                            act.wait_ge(proj_ready, c * OPS + (i + 1))
                            act.activation(sq[:, i // NP, i % NP, :], bank(i % 2), ACT.Square,
                                           scale=DN * math.sqrt(0.5)).then_inc(sq_ready, 1)
                        for t in range(TPC):
                            r = t % 2
                            act.wait_ge(dg_ready, c * TPC + (t + 1))
                            act.wait_ge(q_shift, c * TPC + (t + 1))
                            act.activation(dg[:, r].rearrange("p s h -> p (s h)"),
                                           PS[:, 6 * CH:6 * CH + 2 * NH],
                                           ACT.Copy).then_inc(dg_read, 1)
                            act.wait_ge(hx_psum, c * TPC + (t + 1))
                            act.activation(hx[:, ds(c * TPC + t, 1), :].rearrange("p a d -> p (a d)"),
                                           PS[:, 7 * CH:7 * CH + P],
                                           ACT.Copy).then_inc(hx_ready, 1)
                    with act.Fori(0, NT) as t:
                        act.wait_ge(q_shift, t + 3)
                        q = fq[:, ds(t, 1), :].rearrange("p a f -> p (a f)")
                        act.activation(q, q, ACT.Exp).then_inc(q_exp, 1)

                @block.gpsimd
                def _(pool):
                    for t in range(NT):
                        pool.wait_ge(q_exp, t + 1)
                        pool.tensor_scalar(fq[:, t, :], fq[:, t, :], FEAT_EPS, RATIO, ALU.add, ALU.mult)

        def context():
            ctx = ExitStack()
            with ctx:
                km = sb("km", [P, 4], on=ctx)
                gt = sb("gt", [P, FE], on=ctx)
                ctxt = sb("ctxt", [P, NP, P], on=ctx)
                k_step = sem("k_step")
                km_t = sem("km_t")
                km_row = sem("km_row")
                km_b = sem("km_b")
                kneg = sem("kneg")
                k_exp = sem("k_exp")
                fk_ready = sem("fk_ready")
                gt_psum = sem("gt_psum")
                gt_ready = sem("gt_ready")
                ks_ready = sem("ks_ready")
                ctx_psum = sem("ctx_psum")
                ctxt_ready = sem("ctxt_ready")
                ctxt_zero = sem("ctxt_zero")
                cwo_psum = sem("cwo_psum")
                block = ctx.enter_context(nc.Block())

                @block.gpsimd
                def _(pool):
                    pool.memset(ctxt[:], 0.0).then_inc(ctxt_zero, 1)

                @block.vector
                def _(dve):
                    dve.tensor_reduce(km[:, 0:1], kmax[:], axis=AX.X, op=ALU.max).then_inc(k_step, 1)
                    dve.wait_ge(km_t, 1)
                    dve.tensor_reduce(km[0:1, 1:2], PS[0:1, 0:P], axis=AX.X, op=ALU.max).then_inc(km_row, 1)
                    dve.wait_ge(km_b, 1)
                    dve.tensor_scalar(km[:, 2:3], PS[:, CH:CH + 1], -1.0, None, ALU.mult).then_inc(kneg, 1)
                    with dve.Fori(0, NT) as t:
                        dve.wait_ge(k_exp, t + 1)
                        k = fk[:, ds(t, 1), :].rearrange("p a f -> p (a f)")
                        dve.tensor_scalar(k, k, FEAT_EPS, RATIO, ALU.add, ALU.mult).then_inc(fk_ready, 1)
                    dve.wait_ge(gt_psum, 1)
                    dve.tensor_copy(ksum[:], bank(3)).then_inc(ks_ready, 1)
                    dve.wait_ge(ctxt_zero, 1)
                    dve.wait_ge(ctx_psum, NP)
                    for p in range(NP):
                        for i in range(2):
                            o = (p % 2) * 2 * M + i * M
                            dve.tensor_copy(ctxt[i * DH:(i + 1) * DH, p, o:o + M],
                                            PS[i * DH:(i + 1) * DH,
                                               4 * CH + p * 2 * M + i * M:4 * CH + p * 2 * M + (i + 1) * M]
                                            ).then_inc(ctxt_ready, 1)

                @block.scalar
                def _(act):
                    act.wait_ge(kneg, 1)
                    with act.Fori(0, NT) as t:
                        k = fk[:, ds(t, 1), :].rearrange("p a f -> p (a f)")
                        act.activation(k, k, ACT.Exp, bias=km[:, 2:3]).then_inc(k_exp, 1)
                    act.wait_ge(gt_psum, 1)
                    act.activation(gt[:], bank(2), ACT.Copy).then_inc(gt_ready, 1)
                    act.wait_ge(cwo_psum, 1)
                    act.activation(cwo[:].rearrange("p g d -> p (g d)"), bank(5), ACT.Copy)

                @block.tensor
                def _(pe):
                    pe.wait_ge(k_step, 1)
                    pe.transpose(PS[0:1, 0:P], km[:, 0:1], ident[:]).then_inc(km_t, 1)
                    pe.wait_ge(km_row, 1)
                    pe.matmul(PS[:, CH:CH + 1], ones[0:1, :], km[0:1, 1:2], start=True, stop=True).then_inc(km_b, 1)
                    for t in range(NT):
                        pe.wait_ge(fk_ready, t + 1)
                        pe.matmul(bank(2), hx[:, t, :], fk[:, t, :], start=(t == 0), stop=(t == NT - 1))
                        mm = pe.matmul(bank(3), ones[:], fk[:, t, :], start=(t == 0), stop=(t == NT - 1))
                    mm.then_inc(gt_psum, 1)
                    pe.wait_ge(gt_ready, 1)
                    for p in range(NP):
                        pe.matmul(PS[:, 4 * CH + p * 2 * M:4 * CH + (p + 1) * 2 * M], wv[:, p * P:(p + 1) * P],
                                  gt[:, p * 2 * M:(p + 1) * 2 * M], start=True, stop=True,
                                  skip_group_check=True).then_inc(ctx_psum, 1)
                    pe.wait_ge(ctxt_ready, 2 * NP)
                    for p in range(NP):
                        g = p // 2
                        mm = pe.matmul(PS[:, 5 * CH + g * P:5 * CH + (g + 1) * P], ctxt[:, p, :], wo[:, p, :],
                                       start=(p % 2 == 0), stop=(p % 2 == 1), skip_group_check=True)
                    mm.then_inc(cwo_psum, 1)

        ksum = sb("ksum", [P, FE], on=fb)
        cwo = sb("cwo", [P, FE // P, P], on=fb)

        def attend():
            ctx = ExitStack()
            with ctx:
                G = FE // P
                qk = sb("qk", [P, 2, FE], on=ctx)
                den = sb("den", [P, 2, 2, NH], on=ctx)
                qs = sb("qs", [P, 2, FE], on=ctx)
                qt = sb("qt", [P, G, CH], on=ctx)
                ob = sb("ob1", [P, CH], on=ctx)
                qk_ready = sem("qk_ready")
                den_step = sem("den_step")
                qs_ready = sem("qs_ready")
                qt_psum = sem("qt_psum")
                qt_ready = sem("qt_ready")
                o1_ready = sem("o1_ready")
                ob1_ready = sem("ob1_ready")
                x1_added = sem("x1_added")
                block = ctx.enter_context(nc.Block())

                @block.gpsimd
                def _(pool):
                    pool.sem_inc(qk_ready, 2)
                    with pool.Fori(0, NC) as c:
                        for t in range(TPC):
                            q = fq[:, ds(c * TPC + t, 1), :].rearrange("p a f -> p (a f)")
                            pool.wait_ge(qs_ready, c * TPC + (t + 1))
                            pool.tensor_tensor(qk[:, t % 2, :], q, ksum[:], ALU.mult).then_inc(qk_ready, 1)

                @block.vector
                def _(dve):
                    dve.sem_inc(qs_ready, 2)
                    dve.sem_inc(x1_added, 1)
                    with dve.Fori(0, NC) as c:
                        for t in range(TPC):
                            r = t % 2
                            dve.wait_ge(qk_ready, c * TPC + (t + 3))
                            dve.tensor_reduce(den[:, r, 0, :], heads(qk[:, r, :]), axis=AX.X,
                                              op=ALU.add).then_inc(den_step, 1)
                            dve.wait_ge(den_step, 2 * (c * TPC) + (2 * t + 1))
                            dve.reciprocal(den[:, r, 1, :], den[:, r, 0, :]).then_inc(den_step, 1)
                            dve.wait_ge(den_step, 2 * (c * TPC) + (2 * t + 2))
                            dve.wait_ge(qt_psum, c * TPC + (t + 1))
                            dve.tensor_tensor(heads(qs[:, r, :]),
                                              fq[:, ds(c * TPC + t, 1), :].rearrange("p a (h m) -> p (a h) m", m=M),
                                              wide_m(den[:, r, 1, :]), ALU.mult).then_inc(qs_ready, 1)
                        dve.wait_ge(ob1_ready, c + 2)
                        dve.tensor_tensor(x[:, ds(c * CH, CH)], x[:, ds(c * CH, CH)], ob[:],
                                          ALU.add).then_inc(x1_added, 1)

                @block.tensor
                def _(pe):
                    pe.sem_inc(qt_psum, 2)
                    with pe.Fori(0, NC) as c:
                        for t in range(TPC):
                            r = t % 2
                            pe.wait_ge(qs_ready, c * TPC + (t + 3))
                            pe.wait_ge(qt_ready, c * TPC + (t + 1))
                            for g in range(G):
                                mm = pe.transpose(PS[:, r * CH + g * P:r * CH + (g + 1) * P],
                                                  qs[:, r, g * P:(g + 1) * P], ident[:])
                            mm.then_inc(qt_psum, 1)
                        pe.wait_ge(qt_ready, c * TPC + (TPC + 2))
                        pe.wait_ge(ob1_ready, c + 1)
                        for g in range(G):
                            mm = pe.matmul(bank(2), cwo[:, g, :], qt[:, g, :], start=(g == 0), stop=(g == G - 1))
                        mm.then_inc(o1_ready, 1)

                @block.scalar
                def _(act):
                    act.sem_inc(qt_ready, 2)
                    act.sem_inc(ob1_ready, 1)
                    with act.Fori(0, NC) as c:
                        for t in range(TPC):
                            r = t % 2
                            act.wait_ge(qt_psum, c * TPC + (t + 3))
                            act.activation(qt[:, :, t * P:(t + 1) * P],
                                           bank(r).rearrange("p (g t) -> p g t", g=G), ACT.Copy).then_inc(qt_ready, 1)
                        act.wait_ge(o1_ready, c + 1)
                        act.wait_ge(x1_added, c + 1)
                        act.activation(ob[:], bank(2), ACT.Identity, bias=ga_bo[:],
                                       scale=mod[:, 1, 2:3]).then_inc(ob1_ready, 1)

        features()
        context()
        attend()
        fb.close()
        tb.close()

        layernorm("f1", 1, 3, 4)
        route("f1", 1, 1e-9, True)
        experts("f1", H1, w1_1, w3_1, w2_1, 5, 1, s_w1, 16 * 3)
        wb.close()

        s_out = sem("s_out")
        fin = ExitStack()
        with fin:
            block = fin.enter_context(nc.Block())

            @block.sync
            def _(sp):
                sp.dma_start(out, x[:]).then_inc(s_out, 16)
                sp.wait_ge(s_out, 16)


def kernel(**inputs):
    import numpy as np
    import concourse.bacc as bacc
    from concourse.bass_utils import run_bass_kernel_spmd

    def lay(v):
        return np.ascontiguousarray(v)

    def cols(v, n):
        return lay(np.reshape(v, (n, P)).T)

    i = {k: np.asarray(v) for k, v in inputs.items()}
    arrays = {
        "x": lay(i["L0_attn_x"][0].T),
        "c": lay(np.concatenate([i["L0_c"], i["L1_c"]], axis=0).T),
        "wmod0": i["L0_wmod"], "wmod1": i["L1_wmod"],
        "w_in": i["L0_attn_W_in"], "b_in": cols(i["L0_attn_b_in"], 2 * HV),
        "conv_w": lay(i["L0_attn_conv_w"].reshape(HV, P, KW).transpose(1, 0, 2)),
        "conv_b": cols(i["L0_attn_conv_b"], HV),
        "w_x": lay(i["L0_attn_W_x"].reshape(HV, P, RK + 2 * NS).transpose(1, 0, 2)),
        "w_dt": i["L0_attn_W_dt"], "b_dt": cols(i["L0_attn_b_dt"], HV),
        "w_out": lay(i["L0_attn_W_out"].reshape(HV, P, P).transpose(1, 0, 2)),
        "b_out": cols(i["L0_attn_b_out"], 1),
        "a_log": lay(i["L0_attn_A_log"].reshape(HV, P, NS).transpose(1, 0, 2)),
        "wg": lay(np.stack([i["L0_ffn_Wg"].T, i["L1_ffn_router_w"].T], axis=1)),
        "router_b": i["L1_ffn_router_b"],
        "w1_0": lay(i["L0_ffn_W1"].transpose(2, 0, 1).reshape(P, NE * H0)),
        "w3_0": lay(i["L0_ffn_W3"].transpose(2, 0, 1).reshape(P, NE * H0)),
        "w2_0": lay(i["L0_ffn_W2"].transpose(0, 2, 1)),
        "wq": i["L1_attn_Wq"], "wk": i["L1_attn_Wk"], "wv": i["L1_attn_Wv"], "wo": i["L1_attn_Wo"],
        "wqt": lay(i["L1_attn_Wq"].T), "wkt": lay(i["L1_attn_Wk"].T),
        "bo": cols(i["L1_attn_bo"], 1), "pt": lay(i["L1_attn_P"].T),
        "w1_1": lay(i["L1_ffn_w_gate"].transpose(2, 0, 1).reshape(P, NE * H1)),
        "w3_1": lay(i["L1_ffn_w_up"].transpose(2, 0, 1).reshape(P, NE * H1)),
        "w2_1": lay(i["L1_ffn_w_down"].transpose(0, 2, 1).reshape(NE * H1, P)),
    }
    nc = bacc.Bacc("TRN2", target_bir_lowering=False, num_devices=1)
    arrays = {f"in_{k}": lay(v) for k, v in arrays.items()}
    aps = {k[3:]: nc.dram_tensor(k, v.shape, mybir.dt.from_np(v.dtype), kind="ExternalInput").ap()
           for k, v in arrays.items()}
    out = nc.dram_tensor("out", (P, T), F32, kind="ExternalOutput").ap()
    build(nc, aps, out)
    r = run_bass_kernel_spmd(nc, [arrays], core_ids=[0])
    return lay(r.results[0]["out"].T)[None]
```

```python
import math
from contextlib import ExitStack

import concourse.bass as bass
from concourse import mybir

F32 = mybir.dt.float32
F32R = mybir.dt.float32r
BF16 = mybir.dt.bfloat16
ALU = mybir.AluOpType
ACT = mybir.ActivationFunctionType
AX = mybir.AxisListType
ds = bass.ds

P = 128
T = 2048
CH = 512
NC = T // CH
TPC = CH // P
NT = T // P
DI = 256
HV = DI // P
NS = 16
RK = 64
KW = 3
NE = 8
H0 = 352
H1 = 256
NH, DH, M = 16, 64, 32
NP = NH // 2
FE = NH * M
LN_EPS = 1e-5
FEAT_EPS = 1e-4
DN = DH ** -0.25
RATIO = M ** -0.5


def hidden_tiles(width):
    return [(j, min(P, width - j)) for j in range(0, width, P)]


def build(nc, a, out):
    top = ExitStack()
    with top:
        def sb(name, shape, dt=F32, on=top):
            return on.enter_context(nc.sbuf_tensor(name, shape, dt))

        live = []

        def sem(name):
            live.append(nc.alloc_semaphore(name))
            return live[-1]

        PS = top.enter_context(nc.psum_tensor("PS", [P, 8 * CH], F32))

        def bank(b, n=1):
            return PS[:, b * CH:(b + n) * CH]

        def product(pe, into, w, v, start=True, stop=True):
            pe.matmul(into, w[0], v[0], start=start, stop=False)
            pe.matmul(into, w[0], v[1], start=False, stop=False)
            return pe.matmul(into, w[1], v[0], start=False, stop=stop)

        x = sb("x", [P, T])
        h = sb("h", [P, T])
        ident = sb("ident", [P, P])
        mean_w = sb("mean_w", [P, P])
        ones = sb("ones", [P, P])
        ln_eps = sb("ln_eps", [P, 1])
        sel = sb("sel", [96, 32, P], BF16)
        cvec = sb("cvec", [P, 2])
        wmod = sb("wmod", [P, 2, 6 * P])
        mod = sb("mod", [P, 2, 6])
        hot = sb("hot", [96, 32])
        gtmp = sb("gtmp", [P, 2, 2, 2])
        wg = sb("wg", [P, 2, NE])
        rb = sb("rb", [P, NE])
        cw_split = sb("cw_split", [96, T], BF16)

        s_load = sem("s_load")
        s_w0 = [[sem(f"s_w0_{e}_{k}") for k in range(3)] for e in range(0, NE, 2)]
        s_pad0 = sem("s_pad0")

        def layernorm(tag, layer, shift_col, scale_col, parts=None):
            ctx = ExitStack()
            with ctx:
                xc = sb(f"xc_{tag}", [P, T], on=ctx)
                sq = sb(f"sq_{tag}", [P, T], on=ctx)
                mean_ready = sem(f"mean_ready_{tag}")
                centred = sem(f"centred_{tag}")
                squared = sem(f"squared_{tag}")
                var_ready = sem(f"var_ready_{tag}")
                log_ready = sem(f"log_ready_{tag}")
                rstd_ready = sem(f"rstd_ready_{tag}")
                normed = sem(f"normed_{tag}")
                h_ready = sem(f"h_ready_{tag}")
                h_high = sem(f"h_high_{tag}")

                block = ctx.enter_context(nc.Block())

                @block.tensor
                def _(pe):
                    for c in range(NC):
                        pe.matmul(PS[:, c * CH:(c + 1) * CH], mean_w[:], x[:, c * CH:(c + 1) * CH],
                                  start=True, stop=True).then_inc(mean_ready, 1)
                    for c in range(NC):
                        pe.wait_ge(squared, c + 1)
                        pe.matmul(PS[:, (NC + c) * CH:(NC + c + 1) * CH], mean_w[:], sq[:, c * CH:(c + 1) * CH],
                                  start=True, stop=True).then_inc(var_ready, 1)

                @block.vector
                def _(dve):
                    for c in range(NC):
                        dve.wait_ge(mean_ready, c + 1)
                        dve.tensor_tensor(xc[:, c * CH:(c + 1) * CH], x[:, c * CH:(c + 1) * CH], PS[:, c * CH:(c + 1) * CH],
                                          ALU.subtract).then_inc(centred, 1)
                    for c in range(NC):
                        dve.wait_ge(rstd_ready, c + 1)
                        dve.tensor_tensor(xc[:, c * CH:(c + 1) * CH], xc[:, c * CH:(c + 1) * CH], sq[:, c * CH:(c + 1) * CH],
                                          ALU.mult).then_inc(normed, 1)
                    for c in range(NC if parts else 0):
                        tok = slice(c * CH, (c + 1) * CH)
                        dve.wait_ge(h_ready, c + 1)
                        dve.tensor_copy(parts[:, 0, tok], h[:, tok]).then_inc(h_high, 1)
                        dve.wait_ge(h_high, c + 1)
                        dve.tensor_tensor(parts[:, 1, tok], h[:, tok], parts[:, 0, tok].bitcast(F32), ALU.subtract)

                @block.scalar
                def _(act):
                    for c in range(NC):
                        act.wait_ge(centred, c + 1)
                        act.activation(sq[:, c * CH:(c + 1) * CH], xc[:, c * CH:(c + 1) * CH],
                                       ACT.Square).then_inc(squared, 1)
                    for c in range(NC):
                        act.wait_ge(var_ready, c + 1)
                        act.activation(sq[:, c * CH:(c + 1) * CH], PS[:, (NC + c) * CH:(NC + c + 1) * CH], ACT.Ln,
                                       bias=ln_eps[:]).then_inc(log_ready, 1)
                    for c in range(NC):
                        act.wait_ge(log_ready, c + 1)
                        act.activation(sq[:, c * CH:(c + 1) * CH], sq[:, c * CH:(c + 1) * CH], ACT.Exp,
                                       scale=-0.5).then_inc(rstd_ready, 1)
                    for c in range(NC):
                        act.wait_ge(normed, c + 1)
                        act.activation(h[:, c * CH:(c + 1) * CH], xc[:, c * CH:(c + 1) * CH], ACT.Identity,
                                       bias=mod[:, layer, shift_col:shift_col + 1],
                                       scale=mod[:, layer, scale_col:scale_col + 1]).then_inc(h_ready, 1)

        def route(tag, layer, den_eps, with_bias, cuts):
            ctx = ExitStack()
            with ctx:
                lg = sb(f"lg_{tag}", [P, NT, NE], on=ctx)
                pr = sb(f"pr_{tag}", [P, NT, NE], on=ctx)
                eq = sb(f"eq_{tag}", [P, NT, NE], on=ctx)
                oh = sb(f"oh_{tag}", [P, 2, NT, NE], on=ctx)
                rest = sb(f"rest_{tag}", [P, NT, NE], on=ctx)
                order = sb(f"order_{tag}", [P, NE], on=ctx)
                st = sb(f"st_{tag}", [P, 8, NT], on=ctx)
                cwt = sb(f"cwt_{tag}", [NE, T], on=ctx)
                mid = sb(f"mid_{tag}", [NE, T], BF16, on=ctx)
                logits_ready = sem(f"logits_ready_{tag}")
                shifted = sem(f"shifted_{tag}")
                exp_ready = sem(f"exp_ready_{tag}")
                chain = sem(f"route_step_{tag}")
                cw_ready = sem(f"cw_ready_{tag}")
                cwt_psum = sem(f"cwt_psum_{tag}")
                order_ready = sem(f"order_ready_{tag}")
                high_ready = sem(f"high_ready_{tag}")
                block = ctx.enter_context(nc.Block())

                @block.tensor
                def _(pe):
                    for t in range(NT):
                        mm = pe.matmul(PS[:, t * NE:(t + 1) * NE], h[:, t * P:(t + 1) * P], wg[:, layer, :],
                                       start=True, stop=True, skip_group_check=True)
                    mm.then_inc(logits_ready, 1)
                    pe.wait_ge(cw_ready, 1)
                    for t in range(NT):
                        mm = pe.transpose(PS[0:NE, (CH + t * P):(CH + (t + 1) * P)], eq[:, t, :], ident[:])
                    mm.then_inc(cwt_psum, 1)

                @block.gpsimd
                def _(pool):
                    for e in range(NE):
                        i = pool.memset(order[:, e:e + 1], float(NE - e))
                    i.then_inc(order_ready, 1)
                    pool.memset(cw_split[:], 0.0).then_inc(order_ready, 1)
                    for k, (whole, high, low, _) in enumerate(cuts):
                        pool.wait_ge(high_ready, k + 1)
                        pool.tensor_tensor(low, whole, high.bitcast(F32), ALU.subtract)

                @block.scalar
                def _(act):
                    for k, (whole, high, _, n) in enumerate(cuts):
                        if k == 3:
                            act.wait_ge(shifted, 1)
                            act.activation(pr[:], lg[:], ACT.Exp).then_inc(exp_ready, 1)
                        act.wait_ge(*n)
                        act.activation(high, whole, ACT.Copy).then_inc(high_ready, 1)

                @block.vector
                def _(dve):
                    steps = [0]

                    def wide(v):
                        return v.unsqueeze(2).broadcast_to([P, NT, NE])

                    def step(ins):
                        steps[0] += 1
                        ins.then_inc(chain, 1)
                        dve.wait_ge(chain, steps[0])

                    dve.wait_ge(logits_ready, 1)
                    psl = PS[:, 0:NT * NE].rearrange("p (t e) -> p t e", e=NE)
                    if with_bias:
                        step(dve.tensor_tensor(lg[:], psl, rb[:].unsqueeze(1).broadcast_to([P, NT, NE]), ALU.add))
                    else:
                        step(dve.tensor_copy(lg[:], psl))
                    step(dve.tensor_reduce(st[:, 0, :], lg[:], axis=AX.X, op=ALU.max))
                    dve.tensor_tensor(lg[:], lg[:], wide(st[:, 0, :]), ALU.subtract).then_inc(shifted, 1)
                    dve.wait_ge(exp_ready, 1)
                    step(dve.tensor_reduce(st[:, 1, :], pr[:], axis=AX.X, op=ALU.add))
                    step(dve.reciprocal(st[:, 2, :], st[:, 1, :]))
                    step(dve.tensor_tensor(pr[:], pr[:], wide(st[:, 2, :]), ALU.mult))
                    dve.wait_ge(order_ready, 2)
                    left = pr
                    for k in range(2):
                        step(dve.tensor_reduce(st[:, 3 + k, :], left[:], axis=AX.X, op=ALU.max))
                        step(dve.tensor_tensor(eq[:], left[:], wide(st[:, 3 + k, :]), ALU.is_equal))
                        step(dve.tensor_tensor(eq[:], eq[:], order[:].unsqueeze(1).broadcast_to([P, NT, NE]),
                                               ALU.mult))
                        step(dve.tensor_reduce(st[:, 5, :], eq[:], axis=AX.X, op=ALU.max))
                        step(dve.tensor_tensor(oh[:, k], eq[:], wide(st[:, 5, :]), ALU.is_equal))
                        if k == 0:
                            step(dve.scalar_tensor_tensor(rest[:], oh[:, 0], -2.0, pr[:], ALU.mult, ALU.add))
                            left = rest
                    step(dve.scalar_tensor_tensor(st[:, 6, :], st[:, 3, :], den_eps, st[:, 4, :], ALU.add, ALU.add))
                    step(dve.reciprocal(st[:, 7, :], st[:, 6, :]))
                    step(dve.tensor_tensor(oh[:, 0], oh[:, 0], oh[:, 1], ALU.add))
                    step(dve.tensor_tensor(oh[:, 0], oh[:, 0], pr[:], ALU.mult))
                    dve.tensor_tensor(eq[:], oh[:, 0], wide(st[:, 7, :]), ALU.mult).then_inc(cw_ready, 1)
                    dve.wait_ge(cwt_psum, 1)
                    step(dve.tensor_copy(cwt[:], PS[0:NE, CH:CH + T]))
                    step(dve.tensor_copy(cw_split[0:NE, :], cwt[:]))
                    step(dve.tensor_tensor(cwt[:], cwt[:], cw_split[0:NE, :], ALU.subtract))
                    step(dve.tensor_copy(mid[:], cwt[:]))
                    step(dve.tensor_copy(cw_split[32:32 + NE, :], mid[:]))
                    step(dve.tensor_tensor(cw_split[64:64 + NE, :], cwt[:], mid[:], ALU.subtract))

        def experts(tag, width, wgate, wup, wdown, hp, gate_col, layer):
            ctx = ExitStack()
            with ctx:
                tiles = [(e, j, o, m) for e in range(NE) for j, (o, m) in enumerate(hidden_tiles(width))]
                NI = len(tiles)
                NJ = NI // NE
                HIGH_LAG, LOW_LAG, DOWN_LAG = 1, 2, 4
                RG, RU, RH, RW = 2, 4, 4, 2
                sg = sb(f"sg_{tag}", [P, RH, CH], on=ctx)
                sw = sb(f"sw_{tag}", [P, RH, CH], on=ctx)
                hid = sb(f"hid_{tag}", [P, RH, CH], on=ctx)
                hid_high = sb(f"hid_high_{tag}", [P, RH, CH], F32R, on=ctx)
                hid_low = sb(f"hid_low_{tag}", [P, RH, CH], F32R, on=ctx)
                cwb = sb(f"cwb_{tag}", [P, RW, CH], on=ctx)
                gate_ready = sem(f"gate_ready_{tag}")
                up_ready = sem(f"up_ready_{tag}")
                spread_ready = sem(f"spread_ready_{tag}")
                silu_ready = sem(f"silu_ready_{tag}")
                cwb_ready = sem(f"cwb_ready_{tag}")
                weighed = sem(f"weighed_{tag}")
                hid_ready = sem(f"hid_ready_{tag}")
                high_ready = sem(f"hid_high_ready_{tag}")
                low_ready = sem(f"hid_low_ready_{tag}")
                down_done = sem(f"down_done_{tag}")
                added = sem(f"added_{tag}")
                block = ctx.enter_context(nc.Block())
                BW, BO = RG + RU, RG + RU + 1

                def lagging(i, lag, c, follows, what):
                    if i >= lag:
                        what(c, i - lag)
                    elif follows:
                        what(c - 1, NI + i - lag)

                @block.tensor
                def _(pe):
                    pe.sem_inc(down_done, RH)

                    def down(c, i):
                        e, j, o, m = tiles[i]
                        pe.wait_ge(low_ready, c * NI + (i + 1))
                        if i == 0:
                            pe.wait_ge(added, c + 1)
                        product(pe, bank(BO), [w[0:m, e * NJ + j, :] for w in wdown],
                                [v[0:m, i % RH, :] for v in (hid_high, hid_low)],
                                start=(i == 0), stop=(i == NI - 1)).then_inc(down_done, 1)

                    def chunk(c, follows):
                        hc = [hp[:, k, ds(c * CH, CH)] for k in range(2)]
                        for i, (e, j, o, m) in enumerate(tiles):
                            if j == 0:
                                pe.wait_ge(cwb_ready, c * NE + e + 1)
                                pe.matmul(bank(BW), sel[:, e, :], cw_split[:, ds(c * CH, CH)],
                                          start=True, stop=True).then_inc(spread_ready, 1)
                            w0 = e * width + o
                            pe.wait_ge(silu_ready, c * NI + i + 1)
                            product(pe, bank(i % RG)[0:m], [w[:, w0:w0 + m] for w in wgate],
                                    hc).then_inc(gate_ready, 1)
                            pe.wait_ge(hid_ready, c * NI + i + 1)
                            product(pe, bank(RG + i % RU)[0:m], [w[:, w0:w0 + m] for w in wup],
                                    hc).then_inc(up_ready, 1)
                            lagging(i, DOWN_LAG, c, follows, down)

                    chunk(0, False)
                    with pe.Fori(1, NC) as c:
                        chunk(c, True)
                    for i in range(NI - DOWN_LAG, NI):
                        down(NC - 1, i)

                @block.scalar
                def _(act):
                    act.sem_inc(silu_ready, RG)
                    act.sem_inc(cwb_ready, 1)

                    def high(c, i):
                        m = tiles[i][3]
                        act.wait_ge(hid_ready, c * NI + (RU + i + 1))
                        act.wait_ge(down_done, c * NI + (i + 1))
                        act.activation(hid_high[0:m, i % RH, :], hid[0:m, i % RH, :], ACT.Copy).then_inc(high_ready, 1)

                    def chunk(c, follows):
                        for i, (e, j, o, m) in enumerate(tiles):
                            act.wait_ge(gate_ready, c * NI + i + 1)
                            act.wait_ge(weighed, c * NI + i + 1)
                            act.activation(sg[0:m, i % RH, :], bank(i % RG)[0:m], ACT.Silu).then_inc(silu_ready, 1)
                            if j == 0:
                                act.wait_ge(spread_ready, c * NE + e + 1)
                                act.wait_ge(weighed, c * NI + (RH + i - NJ))
                                act.activation(cwb[:, e % RW, :], bank(BW), ACT.Copy).then_inc(cwb_ready, 1)
                            lagging(i, HIGH_LAG, c, follows, high)

                    chunk(0, False)
                    with act.Fori(1, NC) as c:
                        chunk(c, True)
                    for i in range(NI - HIGH_LAG, NI):
                        high(NC - 1, i)

                @block.gpsimd
                def _(pool):
                    pool.sem_inc(weighed, RH)
                    with pool.Fori(0, NC) as c:
                        for i, (e, j, o, m) in enumerate(tiles):
                            pool.wait_ge(silu_ready, c * NI + (RG + i + 1))
                            if j == 0:
                                pool.wait_ge(cwb_ready, c * NE + (e + 2))
                            pool.wait_ge(hid_ready, c * NI + i + (RU - RH + 1))
                            pool.tensor_tensor(sw[0:m, i % RH, :], sg[0:m, i % RH, :], cwb[0:m, e % RW, :],
                                               ALU.mult).then_inc(weighed, 1)

                @block.vector
                def _(dve):
                    dve.sem_inc(hid_ready, RU)
                    dve.sem_inc(added, 1)

                    def low(c, i):
                        m = tiles[i][3]
                        dve.wait_ge(high_ready, c * NI + (i + 1))
                        dve.tensor_tensor(hid_low[0:m, i % RH, :], hid[0:m, i % RH, :],
                                          hid_high[0:m, i % RH, :].bitcast(F32), ALU.subtract).then_inc(low_ready, 1)

                    def add(c):
                        dve.wait_ge(down_done, c * NI + (RH + NI))
                        xc = x[:, ds(c * CH, CH)]
                        dve.scalar_tensor_tensor(xc, bank(BO), mod[:, layer, gate_col:gate_col + 1], xc,
                                                 ALU.mult, ALU.add).then_inc(added, 1)

                    def chunk(c, follows):
                        for i, (e, j, o, m) in enumerate(tiles):
                            dve.wait_ge(up_ready, c * NI + i + 1)
                            dve.wait_ge(weighed, c * NI + (RH + i + 1))
                            if follows or i >= RH:
                                dve.wait_ge(low_ready, c * NI + (i + 1 - RH))
                            dve.tensor_tensor(hid[0:m, i % RH, :], sw[0:m, i % RH, :],
                                              bank(RG + i % RU)[0:m], ALU.mult).then_inc(hid_ready, 1)
                            lagging(i, LOW_LAG, c, follows, low)
                            if i == DOWN_LAG and follows:
                                add(c - 1)

                    chunk(0, False)
                    with dve.Fori(1, NC) as c:
                        chunk(c, True)
                    for i in range(NI - LOW_LAG, NI):
                        low(NC - 1, i)
                    add(NC - 1)

        ab = ExitStack()
        w_in = sb("w_in", [P, 2 * DI], on=ab)
        b_in = sb("b_in", [P, 2 * HV], on=ab)
        conv_w = sb("conv_w", [P, HV, KW], on=ab)
        conv_b = sb("conv_b", [P, HV], on=ab)
        w_x = sb("w_x", [P, HV, RK + 2 * NS], on=ab)
        w_dt = sb("w_dt", [RK, DI], on=ab)
        b_dt = sb("b_dt", [P, HV], on=ab)
        w_out = sb("w_out", [P, HV, P], on=ab)
        b_out = sb("b_out", [P, 1], on=ab)
        a_neg = sb("a_neg", [P, HV, NS], on=ab)
        ga_b = sb("ga_b", [P, 1], on=ab)

        small_loads = [
            (x[:], a["x"]), (cvec[:], a["c"]), (wmod[:, 0, :], a["wmod0"]), (wmod[:, 1, :], a["wmod1"]),
            (w_in[:], a["w_in"]), (b_in[:], a["b_in"]), (conv_w[:], a["conv_w"]), (conv_b[:], a["conv_b"]),
            (w_x[:], a["w_x"]), (w_dt[:], a["w_dt"]), (b_dt[:], a["b_dt"]), (w_out[:], a["w_out"]),
            (b_out[:], a["b_out"]), (a_neg[:], a["a_log"]), (wg[:], a["wg"]),
            (rb[:], a["router_b"].partition_broadcast(P)),
        ]
        n_small = 16 * len(small_loads)

        s_const = sem("s_const")
        s_silu_c = sem("s_silu_c")
        s_mod = sem("s_mod")
        s_gate = sem("s_gate")
        s_setup = sem("s_setup")
        blk = ExitStack()
        with blk:
            block = blk.enter_context(nc.Block())

            @block.sync
            def _(sp):
                for dst, src in small_loads:
                    sp.dma_start(dst, src).then_inc(s_load, 16)

            @block.gpsimd
            def _(pool):
                pool.memset(ident[:], 0.0).then_inc(s_const, 1)
                pool.memset(ones[:], 1.0).then_inc(s_const, 1)
                pool.memset(mean_w[:], 1.0 / P).then_inc(s_const, 1)
                pool.memset(ln_eps[:], LN_EPS).then_inc(s_const, 1)
                pool.memset(hot[:], 0.0).then_inc(s_const, 1)
                pool.wait_ge(s_const, 5)
                pool.affine_select(out=ident[:], in_=ident[:], compare_op=ALU.not_equal, fill=1.0,
                                   base=0, pattern=[[-1, P]], channel_multiplier=1).then_inc(s_const, 1)
                for g in range(3):
                    pool.affine_select(out=hot[:], in_=hot[:], compare_op=ALU.not_equal, fill=1.0,
                                       base=-32 * g, pattern=[[-1, 32]], channel_multiplier=1).then_inc(s_const, 1)
                    pool.wait_ge(s_const, 7 + g)

            @block.scalar
            def _(act):
                act.wait_ge(s_load, n_small)
                act.activation(cvec[:], cvec[:], ACT.Silu).then_inc(s_silu_c, 1)
                act.activation(a_neg[:], a_neg[:], ACT.Exp).then_inc(s_silu_c, 1)

            @block.tensor
            def _(pe):
                pe.wait_ge(s_silu_c, 1)
                for l in range(2):
                    for k in range(6):
                        mm = pe.matmul(PS[:, 6 * l + k:6 * l + k + 1], wmod[:, l, k * P:(k + 1) * P],
                                       cvec[:, l:l + 1], start=True, stop=True, skip_group_check=True)
                mm.then_inc(s_mod, 1)

            @block.vector
            def _(dve):
                dve.wait_ge(s_mod, 1)
                dve.tensor_copy(mod[:], PS[:, 0:12].rearrange("p (l k) -> p l k", l=2)).then_inc(s_gate, 1)
                dve.wait_ge(s_gate, 1)
                gates = mod[:, :, 2:6:3]
                dve.scalar_tensor_tensor(gtmp[:, 0], gates, -1.0, gates, ALU.mult, ALU.max).then_inc(s_gate, 1)
                dve.tensor_scalar(gtmp[:, 1], gates, 0.0, 2.0, ALU.is_ge, ALU.mult).then_inc(s_gate, 1)
                dve.wait_ge(s_gate, 3)
                dve.tensor_scalar(gtmp[:, 1], gtmp[:, 1], -1.0, None, ALU.add).then_inc(s_gate, 1)
                dve.wait_ge(s_gate, 4)
                dve.scalar_tensor_tensor(gates, gtmp[:, 0], 0.25, gtmp[:, 1], ALU.max, ALU.mult).then_inc(s_gate, 1)
                dve.tensor_scalar(mod[:, :, 1:6:3], mod[:, :, 1:6:3], 1.0, None, ALU.add).then_inc(s_gate, 1)
                dve.wait_ge(s_gate, 6)
                dve.tensor_tensor(ga_b[:], mod[:, 0, 2:3], b_out[:], ALU.mult).then_inc(s_setup, 1)
                dve.wait_ge(s_silu_c, 2)
                dve.tensor_scalar(a_neg[:], a_neg[:], -1.0, None, ALU.mult).then_inc(s_setup, 1)
                dve.wait_ge(s_const, 9)
                dve.tensor_copy(sel[:], hot[:].unsqueeze(2).broadcast_to([96, 32, P]))

        layernorm("a0", 0, 0, 1)

        sc = ExitStack()
        u = sb("u", [P, HV, T], on=sc)
        rg = sb("rg", [P, HV, T], on=sc)
        delta = sb("delta", [P, HV, T], on=sc)
        bc_split = sb("bc_split", [96, T], BF16, on=sc)

        def scan_inputs():
            ctx = ExitStack()
            with ctx:
                ur = sb("ur", [P, HV, T + KW - 1], on=ctx)
                cv = sb("cv", [P, HV, CH], on=ctx)
                taps = sb("taps", [P, HV, CH], on=ctx)
                dt = sb("dt", [RK, CH], on=ctx)
                bc = sb("bc", [2 * NS, CH], on=ctx)
                bc_rest = sb("bc_rest", [2 * NS, CH], on=ctx)
                bc_mid = sb("bc_mid", [2 * NS, CH], BF16, on=ctx)
                vmax = sb("vmax", [P, HV, T], on=ctx)
                pad_ready = sem("pad_ready")
                xr_ready = sem("xr_ready")
                ur_ready = sem("ur_ready")
                rg_ready = sem("rg_ready")
                conv_step = sem("conv_step")
                conv_ready = sem("conv_ready")
                u_ready = sem("u_ready")
                xp_ready = sem("xp_ready")
                dt_ready = sem("dt_ready")
                bc_ready = sem("bc_ready")
                split_step = sem("split_step")
                v_ready = sem("v_ready")
                v_abs = sem("v_abs")
                v_max = sem("v_max")
                soft_exp = sem("soft_exp")
                soft_ln = sem("soft_ln")
                delta_ready = sem("delta_ready")
                block = ctx.enter_context(nc.Block())
                XP_BANK, V_BANK = 2 * HV, 2 * HV + 1

                @block.tensor
                def _(pe):
                    def after(c):
                        pe.wait_ge(dt_ready, c + 1)
                        pe.wait_ge(bc_ready, 2 * c + 2)
                        for j in range(HV):
                            pe.wait_ge(u_ready, c * HV + (HV + j + 1))
                            mm = pe.matmul(bank(XP_BANK)[0:RK + 2 * NS], w_x[:, j, :], u[:, j, ds(c * CH, CH)],
                                           start=(j == 0), stop=(j == HV - 1))
                        mm.then_inc(xp_ready, 1)
                        for j in range(HV):
                            pe.wait_ge(dt_ready, c + 2)
                            pe.wait_ge(v_max, c * HV + (j + 1))
                            pe.matmul(bank(V_BANK + j), w_dt[:, j * P:(j + 1) * P], dt[:],
                                      start=True, stop=True).then_inc(v_ready, 1)

                    def chunk(c, follows):
                        for j in range(2 * HV):
                            if j < HV:
                                pe.wait_ge(ur_ready, c * HV + (j + 1))
                            else:
                                pe.wait_ge(rg_ready, c * HV + (j - HV + 1))
                            pe.matmul(bank(j), w_in[:, j * P:(j + 1) * P], h[:, ds(c * CH, CH)],
                                      start=True, stop=True).then_inc(xr_ready, 1)
                        if follows:
                            after(c - 1)

                    chunk(0, False)
                    with pe.Fori(1, NC) as c:
                        chunk(c, True)
                    after(NC - 1)

                @block.scalar
                def _(act):
                    act.sem_inc(ur_ready, HV)
                    act.sem_inc(rg_ready, HV)
                    act.sem_inc(u_ready, HV)
                    act.sem_inc(dt_ready, 1)
                    act.sem_inc(bc_ready, 2)

                    def after(c):
                        act.wait_ge(xp_ready, c + 1)
                        act.activation(dt[:], bank(XP_BANK)[0:RK], ACT.Copy).then_inc(dt_ready, 1)
                        act.wait_ge(split_step, 4 * c + 4)
                        act.activation(bc[:], bank(XP_BANK)[RK:RK + 2 * NS], ACT.Copy).then_inc(bc_ready, 1)
                        act.activation(bc_split[0:2 * NS, ds(c * CH, CH)], bank(XP_BANK)[RK:RK + 2 * NS],
                                       ACT.Copy).then_inc(bc_ready, 1)
                        for j in range(HV):
                            act.wait_ge(v_ready, c * HV + (j + 1))
                            act.activation(delta[:, j, ds(c * CH, CH)], bank(V_BANK + j), ACT.Abs,
                                           bias=b_dt[:, j:j + 1]).then_inc(v_abs, 1)

                    def chunk(c, follows):
                        for j in range(HV):
                            act.wait_ge(xr_ready, c * 2 * HV + (j + 1))
                            act.activation(ur[:, j, ds(c * CH + (KW - 1), CH)], bank(j), ACT.Identity,
                                           bias=b_in[:, j:j + 1]).then_inc(ur_ready, 1)
                        for j in range(HV):
                            act.wait_ge(xr_ready, c * 2 * HV + (HV + j + 1))
                            act.activation(rg[:, j, ds(c * CH, CH)], bank(HV + j), ACT.Silu,
                                           bias=b_in[:, HV + j:HV + j + 1]).then_inc(rg_ready, 1)
                        if follows:
                            after(c - 1)
                        for j in range(HV):
                            act.wait_ge(conv_ready, c * HV + (j + 1))
                            act.activation(u[:, j, ds(c * CH, CH)], cv[:, j, :], ACT.Silu).then_inc(u_ready, 1)

                    chunk(0, False)
                    with act.Fori(1, NC) as c:
                        chunk(c, True)
                    after(NC - 1)
                    for step, (func, kw) in enumerate(((ACT.Exp, dict(scale=-1.0)), (ACT.Ln, dict(bias=ones[:, 0:1])))):
                        for j in range(HV):
                            act.wait_ge(*((v_abs, HV * NC) if step == 0 else (soft_exp, j + 1)))
                            act.activation(delta[:, j, :], delta[:, j, :], func,
                                           **kw).then_inc(soft_exp if step == 0 else soft_ln, 1)

                @block.gpsimd
                def _(pool):
                    pool.memset(ur[:, :, 0:KW - 1], 0.0).then_inc(pad_ready, 1)
                    pool.sem_inc(split_step, 4)
                    with pool.Fori(0, NC) as c:
                        tok = ds(c * CH, CH)
                        pool.wait_ge(bc_ready, 2 * c + 4)
                        pool.tensor_tensor(bc_rest[:], bc[:], bc_split[0:2 * NS, tok],
                                           ALU.subtract).then_inc(split_step, 1)
                        pool.wait_ge(split_step, 4 * c + 5)
                        one = ones[0:2 * NS, 0:1].broadcast_to([2 * NS, CH])
                        pool.tensor_tensor(bc_mid[:], bc_rest[:], one, ALU.mult).then_inc(split_step, 1)
                        pool.tensor_tensor(bc_split[32:32 + 2 * NS, tok], bc_rest[:], one,
                                           ALU.mult).then_inc(split_step, 1)
                        pool.wait_ge(split_step, 4 * c + 7)
                        pool.tensor_tensor(bc_split[64:64 + 2 * NS, tok], bc_rest[:], bc_mid[:],
                                           ALU.subtract).then_inc(split_step, 1)
                        pool.wait_ge(split_step, 4 * c + 8)
                    pool.wait_ge(delta_ready, 1)
                    pool.tensor_tensor(u[:, 0, :], u[:, 0, :], delta[:, 0, :], ALU.mult)

                @block.vector
                def _(dve):
                    dve.sem_inc(v_max, HV)
                    dve.wait_ge(pad_ready, 1)

                    def after(c):
                        for j in range(HV):
                            dve.wait_ge(v_abs, c * HV + (j + 1))
                            dve.tensor_scalar(vmax[:, j, ds(c * CH, CH)], bank(V_BANK + j), b_dt[:, j:j + 1], 0.0,
                                              ALU.add, ALU.max).then_inc(v_max, 1)

                    def chunk(c, follows):
                        for j in range(HV):
                            dve.wait_ge(ur_ready, c * HV + (HV + j + 1))
                            dve.tensor_scalar(taps[:, j, :], ur[:, j, ds(c * CH, CH)], conv_w[:, j, 0:1],
                                              conv_b[:, j:j + 1], ALU.mult, ALU.add).then_inc(conv_step, 1)
                            dve.wait_ge(conv_step, c * 2 * HV + (2 * j + 1))
                            dve.scalar_tensor_tensor(taps[:, j, :], ur[:, j, ds(c * CH + 1, CH)],
                                                     conv_w[:, j, 1:2], taps[:, j, :],
                                                     ALU.mult, ALU.add).then_inc(conv_step, 1)
                            dve.wait_ge(conv_step, c * 2 * HV + (2 * j + 2))
                            dve.wait_ge(u_ready, c * HV + (j + 1))
                            dve.scalar_tensor_tensor(cv[:, j, :], ur[:, j, ds(c * CH + 2, CH)], conv_w[:, j, 2:3],
                                                     taps[:, j, :], ALU.mult, ALU.add).then_inc(conv_ready, 1)
                        if follows:
                            after(c - 1)
                        dve.wait_ge(conv_ready, (c + 1) * HV)

                    chunk(0, False)
                    with dve.Fori(1, NC) as c:
                        chunk(c, True)
                    after(NC - 1)
                    dve.wait_ge(v_max, HV * NC + HV)
                    for j in range(HV):
                        dve.wait_ge(soft_ln, j + 1)
                        dve.tensor_tensor(delta[:, j, :], delta[:, j, :], vmax[:, j, :], ALU.add).then_inc(delta_ready, 1)
                    dve.wait_ge(delta_ready, HV)
                    dve.tensor_tensor(u[:, 1, :], u[:, 1, :], delta[:, 1, :], ALU.mult)

        def scan():
            ctx = ExitStack()
            with ctx:
                RB, RC, RP = 2, 4, 4
                LAG = 3
                YG_AT, OB_AT, X_AT = 2, 4, 5
                st = sb("st", [P, NS, HV, CH], on=ctx)
                da = sb("da", [P, RB, HV, CH], on=ctx)
                db = sb("db", [P, RB, HV, CH], on=ctx)
                cs = sb("cs", [P, RC, CH], on=ctx)
                prod = sb("prod", [P, RP, HV, CH], on=ctx)
                yg = sb("yg", [P, HV, CH], on=ctx)
                ob = sb("ob", [P, CH], on=ctx)
                dl = sb("dl", [P, HV, CH], on=ctx)
                dl_ready = sem("dl_ready")
                st_zero = sem("st_zero")
                b_spread = sem("b_spread")
                c_spread = sem("c_spread")
                cs_ready = sem("cs_ready")
                da_ready = sem("da_ready")
                db_ready = sem("db_ready")
                st_ready = sem("st_ready")
                prod_ready = sem("prod_ready")
                y_added = sem("y_added")
                yg_ready = sem("yg_ready")
                o_ready = sem("o_ready")
                ob_ready = sem("ob_ready")
                x_added = sem("x_added")
                block = ctx.enter_context(nc.Block())
                B_BANK, C_BANK, Y_BANK, O_BANK = 0, 2, 4, 6

                @block.tensor
                def _(pe):
                    pe.sem_inc(y_added, RP)

                    def add_y(c, n):
                        pe.wait_ge(prod_ready, c * NS + (NS + n + 1))
                        if n == 0:
                            pe.wait_ge(yg_ready, c + 1)
                        for j in range(HV):
                            mm = pe.matmul(bank(Y_BANK + j), ident[:], prod[:, n % RP, j, :],
                                           start=(n == 0), stop=(n == NS - 1))
                        mm.then_inc(y_added, 1)

                    def project(c):
                        pe.wait_ge(yg_ready, c + 2)
                        pe.wait_ge(ob_ready, c + 1)
                        for j in range(HV):
                            mm = pe.matmul(bank(O_BANK), w_out[:, j, :], yg[:, j, :],
                                           start=(j == 0), stop=(j == HV - 1))
                        mm.then_inc(o_ready, 1)

                    def chunk(c, follows):
                        for n in range(NS):
                            pe.wait_ge(db_ready, c * NS + (n + 1))
                            pe.matmul(bank(B_BANK + n % RB), sel[:, n, :], bc_split[:, ds(c * CH, CH)],
                                      start=True, stop=True).then_inc(b_spread, 1)
                            pe.wait_ge(cs_ready, c * NS + (n + 1))
                            pe.matmul(bank(C_BANK + n % RB), sel[:, NS + n, :], bc_split[:, ds(c * CH, CH)],
                                      start=True, stop=True).then_inc(c_spread, 1)
                            if n == LAG and follows:
                                project(c - 1)
                            if n >= LAG:
                                add_y(c, n - LAG)
                            elif follows:
                                add_y(c - 1, NS - LAG + n)

                    chunk(0, False)
                    with pe.Fori(1, NC) as c:
                        chunk(c, True)
                    for n in range(NS - LAG, NS):
                        add_y(NC - 1, n)
                    project(NC - 1)

                @block.scalar
                def _(act):
                    act.sem_inc(cs_ready, RB)
                    act.sem_inc(ob_ready, 1)

                    def project_out(c):
                        act.wait_ge(x_added, c + 1)
                        act.wait_ge(o_ready, c + 1)
                        act.activation(ob[:], bank(O_BANK), ACT.Identity, bias=ga_b[:],
                                       scale=mod[:, 0, 2:3]).then_inc(ob_ready, 1)

                    def chunk(c, follows):
                        if follows:
                            act.wait_ge(da_ready, c * NS * HV)
                        act.activation(dl[:], delta[:, :, ds(c * CH, CH)], ACT.Copy).then_inc(dl_ready, 1)
                        act.wait_ge(dl_ready, c + 1)
                        for n in range(NS):
                            act.wait_ge(st_ready, (c * NS + n) * HV + HV)
                            for j in range(HV):
                                act.activation(da[:, n % RB, j, :], dl[:, j, :], ACT.Exp,
                                               scale=a_neg[:, j, n:n + 1]).then_inc(da_ready, 1)
                            act.wait_ge(c_spread, c * NS + (n + 1))
                            act.wait_ge(prod_ready, c * NS + (n + NS - RC + 1))
                            act.activation(cs[:, n % RC, :],
                                           bank(C_BANK + n % RB), ACT.Copy).then_inc(cs_ready, 1)
                            if n == OB_AT and follows:
                                project_out(c - 1)

                    chunk(0, False)
                    with act.Fori(1, NC) as c:
                        chunk(c, True)
                    project_out(NC - 1)

                @block.gpsimd
                def _(pool):
                    for n in range(NS):
                        i = pool.memset(st[:, n, :, CH - 1:CH], 0.0)
                    i.then_inc(st_zero, 1)
                    pool.sem_inc(prod_ready, NS)
                    with pool.Fori(0, NC) as c:
                        for n in range(NS):
                            pool.wait_ge(st_ready, (c * NS + (n + RB)) * HV + HV)
                            pool.wait_ge(cs_ready, c * NS + (RB + n + 1))
                            pool.wait_ge(y_added, c * NS + (n + 1))
                            pool.tensor_tensor(prod[:, n % RP], st[:, n],
                                               cs[:, n % RC, :].unsqueeze(1).broadcast_to([P, HV, CH]),
                                               ALU.mult).then_inc(prod_ready, 1)

                @block.vector
                def _(dve):
                    dve.sem_inc(db_ready, RB)
                    dve.sem_inc(st_ready, RB * HV)
                    dve.sem_inc(yg_ready, 1)
                    dve.sem_inc(x_added, 1)
                    dve.wait_ge(st_zero, 1)

                    def gate_y(c):
                        dve.wait_ge(y_added, c * NS + (RP + NS))
                        dve.tensor_tensor(yg[:], bank(Y_BANK, 2).rearrange("p (j t) -> p j t", j=HV),
                                          rg[:, :, ds(c * CH, CH)], ALU.mult).then_inc(yg_ready, 1)

                    def add_x(c):
                        dve.wait_ge(ob_ready, c + 2)
                        dve.tensor_tensor(x[:, ds(c * CH, CH)], x[:, ds(c * CH, CH)], ob[:],
                                          ALU.add).then_inc(x_added, 1)

                    def chunk(c, follows):
                        for n in range(NS):
                            dve.wait_ge(b_spread, c * NS + (n + 1))
                            dve.wait_ge(st_ready, (c * NS + n) * HV + HV)
                            dve.tensor_tensor(db[:, n % RB], u[:, :, ds(c * CH, CH)],
                                              bank(B_BANK + n % RB).unsqueeze(1).broadcast_to([P, HV, CH]),
                                              ALU.mult).then_inc(db_ready, 1)
                            dve.wait_ge(db_ready, c * NS + (RB + n + 1))
                            dve.wait_ge(prod_ready, c * NS + (n + 1))
                            for j in range(HV):
                                dve.wait_ge(da_ready, (c * NS + n) * HV + (j + 1))
                                dve.tensor_tensor_scan(st[:, n, j, :], da[:, n % RB, j, :], db[:, n % RB, j, :],
                                                       initial=st[:, n, j, CH - 1:CH],
                                                       op0=ALU.mult, op1=ALU.add).then_inc(st_ready, 1)
                            if n == YG_AT and follows:
                                gate_y(c - 1)
                            if n == X_AT and follows:
                                add_x(c - 1)

                    chunk(0, False)
                    with dve.Fori(1, NC) as c:
                        chunk(c, True)
                    gate_y(NC - 1)
                    add_x(NC - 1)

        scan_inputs()
        scan()
        sc.close()
        ab.close()

        def expert_weights(on, layer, width):
            nj = len(hidden_tiles(width))
            whole = [sb(f"w{k}_{layer}", [P, NE * width], on=on) for k in (1, 3)]
            whole.append(sb(f"w2_{layer}", [P, NE * nj, P], on=on))
            high = [sb(f"{w.name}_high", list(w.shape), F32R, on=on) for w in whole]
            low = [sb(f"{w.name}_low", list(w.shape), F32R, on=on) for w in whole]
            return nj, whole, high, low

        def expert_pieces(nj, whole, high, low, width, loaded):
            cuts = []
            for e in range(0, NE, 2):
                for k, unit in enumerate((width, width, nj)):
                    span = slice(e * unit, (e + 2) * unit)
                    cuts.append((whole[k][:, span], high[k][:, span], low[k][:, span], loaded(e, k)))
            return cuts

        eb = ExitStack()
        nj0, whole0, high0, low0 = expert_weights(eb, 0, H0)
        hp0 = sb("hp0", [P, 2, T], F32R, on=eb)
        full = (H0 // P) * P
        ld = ExitStack()
        with ld:
            block = ld.enter_context(nc.Block())

            @block.gpsimd
            def _(pool):
                for e in range(NE):
                    i = pool.memset(whole0[2][H0 - full:P, (e + 1) * nj0 - 1, :], 0.0)
                i.then_inc(s_pad0, 1)

            @block.sync
            def _(sp):
                for e in range(0, NE, 2):
                    span = slice(e * H0, (e + 2) * H0)
                    sp.dma_start(whole0[0][:, span], a["w1_0"][:, span]).then_inc(s_w0[e // 2][0], 16)
                    sp.dma_start(whole0[1][:, span], a["w3_0"][:, span]).then_inc(s_w0[e // 2][1], 16)
                    for f in (e, e + 1):
                        sp.dma_start(whole0[2][:, f * nj0:(f + 1) * nj0 - 1, :],
                                     a["w2_0"][f, 0:full, :].rearrange("(j p) d -> p j d", p=P)
                                     ).then_inc(s_w0[e // 2][2], 16)
                        sp.dma_start(whole0[2][0:H0 - full, (f + 1) * nj0 - 1, :],
                                     a["w2_0"][f, full:H0, :]).then_inc(s_w0[e // 2][2], 16)
        layernorm("f0", 0, 3, 4, hp0)
        route("f0", 0, 1e-20, False, expert_pieces(
            nj0, whole0, high0, low0, H0, lambda e, k: (s_w0[e // 2][k], 64 if k == 2 else 16)))
        experts("f0", H0, *[(high0[k], low0[k]) for k in range(3)], hp0, 5, 0)
        eb.close()
        nc.clear_and_free_semaphores(live)
        nc.all_engine_barrier()
        live.clear()

        tb = ExitStack()
        wv = sb("wv", [P, NH * DH], on=tb)
        wo = sb("wo", [P, NP, P], on=tb)
        bo = sb("bo", [P, 1], on=tb)
        ga_bo = sb("ga_bo", [P, 1], on=tb)
        wq2, wk2, wqp2, wkp2 = ([sb(f"{n}_{k}", [P, m], F32R, on=tb) for k in ("high", "low")]
                                for n, m in (("wq", NH * DH), ("wk", NH * DH), ("wqp", FE), ("wkp", FE)))

        def attention_weights():
            ctx = ExitStack()
            with ctx:
                wq = sb("wq", [P, NH * DH], on=ctx)
                wk = sb("wk", [P, NH * DH], on=ctx)
                wqt = sb("wqt", [P, NP, P], on=ctx)
                wkt = sb("wkt", [P, NP, P], on=ctx)
                pt2 = sb("pt2", [P, 2 * M], on=ctx)
                wp = sb("wp", [P, 2, FE], on=ctx)
                zero_ready = sem("zero_ready")
                pt_loaded = sem("pt_loaded")
                t_loaded = [sem(f"wt_loaded_{k}") for k in "kq"]
                w_loaded = [sem(f"w_loaded_{k}") for k in "kq"]
                rest_loaded = sem("rest_loaded")
                wp_psum = sem("wp_psum")
                wp_ready = sem("wp_ready")
                wp_high = sem("wp_high")
                high_ready = sem("w_high_ready")
                block = ctx.enter_context(nc.Block())

                @block.sync
                def _(sp):
                    sp.wait_ge(zero_ready, 1)
                    sp.dma_start(pt2[0:DH, 0:M], a["pt"]).then_inc(pt_loaded, 16)
                    sp.dma_start(pt2[DH:P, M:2 * M], a["pt"]).then_inc(pt_loaded, 16)
                    for k, (t, n) in enumerate(((wkt, "wkt"), (wqt, "wqt"))):
                        sp.dma_start(t[:], a[n].rearrange("(j p) d -> p j d", p=P)).then_inc(t_loaded[k], 16)
                    for k, (t, n) in enumerate(((wk, "wk"), (wq, "wq"))):
                        sp.dma_start(t[:], a[n]).then_inc(w_loaded[k], 16)
                    sp.dma_start(bo[:], a["bo"]).then_inc(rest_loaded, 16)
                    sp.dma_start(wv[:], a["wv"]).then_inc(rest_loaded, 16)
                    sp.dma_start(wo[:], a["wo"].rearrange("(j p) d -> p j d", p=P)).then_inc(rest_loaded, 16)

                @block.tensor
                def _(pe):
                    pe.wait_ge(pt_loaded, 32)
                    for b, wt in enumerate((wkt, wqt)):
                        pe.wait_ge(t_loaded[b], 16)
                        for p in range(NP):
                            mm = pe.matmul(PS[:, b * CH + p * 2 * M:b * CH + (p + 1) * 2 * M], wt[:, p, :], pt2[:],
                                           start=True, stop=True, skip_group_check=True)
                        mm.then_inc(wp_psum, 1)

                @block.scalar
                def _(act):
                    for b, (w, w2) in enumerate(((wk, wk2), (wq, wq2))):
                        act.wait_ge(wp_psum, b + 1)
                        act.activation(wp[:, b, :], bank(b), ACT.Copy, scale=DN).then_inc(wp_ready, 1)
                        act.wait_ge(w_loaded[b], 16)
                        act.activation(w2[0][:], w[:], ACT.Copy).then_inc(high_ready, 1)

                @block.gpsimd
                def _(pool):
                    pool.memset(pt2[:], 0.0).then_inc(zero_ready, 1)
                    for b, (w, w2) in enumerate(((wk, wk2), (wq, wq2))):
                        pool.wait_ge(high_ready, b + 1)
                        pool.tensor_tensor(w2[1][:], w[:], w2[0][:].bitcast(F32), ALU.subtract)

                @block.vector
                def _(dve):
                    for b, w2 in enumerate((wkp2, wqp2)):
                        dve.wait_ge(wp_ready, b + 1)
                        dve.tensor_copy(w2[0][:], wp[:, b, :]).then_inc(wp_high, 1)
                        dve.wait_ge(wp_high, b + 1)
                        dve.tensor_tensor(w2[1][:], wp[:, b, :], w2[0][:].bitcast(F32), ALU.subtract)
                    dve.wait_ge(rest_loaded, 48)
                    dve.tensor_tensor(ga_bo[:], mod[:, 1, 2:3], bo[:], ALU.mult)

        attention_weights()
        layernorm("a1", 1, 0, 1)

        fb = ExitStack()
        hx = sb("hx", [P, NT, P], on=fb)
        fk = sb("fk", [P, NT, FE], on=fb)
        fq = sb("fq", [P, NT, FE], on=fb)
        kmax = sb("kmax", [P, NT], on=fb)

        def heads(v):
            return v.rearrange("p (h m) -> p h m", m=M)

        def wide_m(v):
            return v.unsqueeze(2).broadcast_to([P, NH, M])

        def features():
            ctx = ExitStack()
            with ctx:
                HS = 2
                hs = sb("hs", [P, HS, CH], on=ctx)
                hs_high = sb("hs_high", [P, HS, CH], F32R, on=ctx)
                hs_low = sb("hs_low", [P, HS, CH], F32R, on=ctx)
                sq = sb("sq", [P, 2, NH, DH], on=ctx)
                half = sb("half", [P, 2, NH, DH // 2], on=ctx)
                dg = sb("dg", [P, 2, NH], on=ctx)
                mq = sb("mq", [P, 2, NH], on=ctx)
                hs_copied = sem("hs_copied")
                hs_ready = sem("hs_ready")
                hx_psum = sem("hx_psum")
                hx_ready = sem("hx_ready")
                dd_ready = [sem(f"dd_ready_{k}") for k in "kq"]
                proj_ready = [sem(f"proj_ready_{k}") for k in "kq"]
                sq_ready = [sem(f"sq_ready_{k}") for k in "kq"]
                half_ready = [sem(f"half_ready_{k}") for k in "kq"]
                dg_ready = [sem(f"dg_ready_{k}") for k in "kq"]
                q_max = sem("q_max")
                q_bias = sem("q_bias")
                shifted = [sem(f"shifted_{k}") for k in "kq"]
                q_exp = sem("q_exp")
                block = ctx.enter_context(nc.Block())
                DD, PR, HX = (0, 3), (1, 4), 6
                weights = ((wkp2, wk2), (wqp2, wq2))

                @block.tensor
                def _(pe):
                    def tile(c, g, t):
                        k1 = c * TPC + t
                        tok = slice(t * P, (t + 1) * P)
                        stat = [v[:, g, tok] for v in (hs_high, hs_low)]
                        for s, (wd, wp) in enumerate(weights):
                            if s == 0:
                                pe.wait_ge(hs_ready, c + 1)
                            else:
                                pe.wait_ge(hx_ready, k1 + 1)
                                pe.transpose(PS[:, HX * CH:HX * CH + P], hs[:, g, tok], ident[:]).then_inc(hx_psum, 1)
                            pe.wait_ge(shifted[s], k1 + 1)
                            product(pe, bank(DD[s]), stat, [w[:] for w in wd]).then_inc(dd_ready[s], 1)
                            pe.wait_ge(sq_ready[s], k1 + 1)
                            for b in range(2):
                                mm = product(pe, bank(PR[s] + b), stat, [w[:, b * CH:(b + 1) * CH] for w in wp])
                            mm.then_inc(proj_ready[s], 1)

                    with pe.Fori(0, NC, HS) as c:
                        for g in range(HS):
                            for t in range(TPC):
                                tile(c + g, g, t)

                @block.scalar
                def _(act):
                    for k in sq_ready:
                        act.sem_inc(k, 1)
                    act.sem_inc(hx_ready, 1)
                    with act.Fori(0, NC) as c:
                        for t in range(TPC):
                            k1 = c * TPC + t
                            for s in range(2):
                                act.wait_ge(half_ready[s], k1 + 1)
                                act.wait_ge(proj_ready[s], k1 + 1)
                                act.activation(sq[:, s].rearrange("p h e -> p (h e)"), bank(PR[s], 2), ACT.Square,
                                               scale=DN * math.sqrt(0.5)).then_inc(sq_ready[s], 1)
                            act.wait_ge(hx_psum, k1 + 1)
                            act.activation(hx[:, ds(k1, 1), :].rearrange("p a d -> p (a d)"),
                                           PS[:, HX * CH:HX * CH + P], ACT.Copy).then_inc(hx_ready, 1)
                            act.wait_ge(shifted[1], k1 + 2)
                            q = fq[:, ds(k1, 1), :].rearrange("p a f -> p (a f)")
                            act.activation(q, q, ACT.Exp)

                @block.gpsimd
                def _(pool):
                    for k in half_ready:
                        pool.sem_inc(k, 1)
                    with pool.Fori(0, NT) as t:
                        for s in range(2):
                            pool.wait_ge(sq_ready[s], t + 2)
                            pool.wait_ge(dg_ready[s], t + 1)
                            pool.tensor_tensor(half[:, s], sq[:, s, :, 0:DH // 2], sq[:, s, :, DH // 2:DH],
                                               ALU.add).then_inc(half_ready[s], 1)

                @block.vector
                def _(dve):
                    for k in (*shifted, *dg_ready):
                        dve.sem_inc(k, 1)

                    def take(c, g):
                        dve.tensor_copy(hs[:, g, :], h[:, ds(c * CH, CH)]).then_inc(hs_copied, 1)
                        dve.tensor_copy(hs_high[:, g, :], h[:, ds(c * CH, CH)]).then_inc(hs_copied, 1)
                        dve.wait_ge(hs_copied, 2 * c + 2)
                        dve.tensor_tensor(hs_low[:, g, :], hs[:, g, :], hs_high[:, g, :].bitcast(F32),
                                          ALU.subtract).then_inc(hs_ready, 1)

                    def tile(k1):
                        dve.wait_ge(dd_ready[0], k1 + 1)
                        dve.tensor_reduce(kmax[:, ds(k1, 1)], bank(DD[0]), axis=AX.X, op=ALU.max)
                        dve.wait_ge(dd_ready[1], k1 + 1)
                        dve.tensor_reduce(mq[:, 0, :], heads(bank(DD[1])), axis=AX.X, op=ALU.max).then_inc(q_max, 1)
                        dve.wait_ge(half_ready[0], k1 + 2)
                        dve.tensor_reduce(dg[:, 0, :], half[:, 0], axis=AX.X, op=ALU.add).then_inc(dg_ready[0], 1)
                        dve.wait_ge(dg_ready[0], k1 + 2)
                        dve.tensor_tensor(fk[:, ds(k1, 1), :].rearrange("p a (h m) -> p (a h) m", m=M),
                                          heads(bank(DD[0])), wide_m(dg[:, 0, :]), ALU.subtract).then_inc(shifted[0], 1)
                        dve.wait_ge(half_ready[1], k1 + 2)
                        dve.tensor_reduce(dg[:, 1, :], half[:, 1], axis=AX.X, op=ALU.add).then_inc(dg_ready[1], 1)
                        dve.wait_ge(dg_ready[1], k1 + 2)
                        dve.wait_ge(q_max, k1 + 1)
                        dve.tensor_tensor(mq[:, 1, :], mq[:, 0, :], dg[:, 1, :], ALU.add).then_inc(q_bias, 1)
                        dve.wait_ge(q_bias, k1 + 1)
                        dve.tensor_tensor(fq[:, ds(k1, 1), :].rearrange("p a (h m) -> p (a h) m", m=M),
                                          heads(bank(DD[1])), wide_m(mq[:, 1, :]), ALU.subtract).then_inc(shifted[1], 1)

                    take(0, 0)
                    with dve.Fori(0, NC - HS, HS) as c:
                        for g in range(HS):
                            take(c + (g + 1), (g + 1) % HS)
                            for t in range(TPC):
                                tile((c + g) * TPC + t)
                    take(NC - 1, 1)
                    for t in range(TPC * HS):
                        tile((NC - HS) * TPC + t)

        def context():
            ctx = ExitStack()
            with ctx:
                km = sb("km", [P, 4], on=ctx)
                gt = sb("gt", [P, FE], on=ctx)
                kacc = sb("kacc", [P, FE], on=ctx)
                kacc_step = sem("kacc_step")
                ks_psum = sem("ks_psum")
                ctxt = sb("ctxt", [P, NP, P], on=ctx)
                k_step = sem("k_step")
                km_t = sem("km_t")
                km_row = sem("km_row")
                km_b = sem("km_b")
                kneg = sem("kneg")
                k_exp = sem("k_exp")
                fk_ready = sem("fk_ready")
                gt_psum = sem("gt_psum")
                gt_ready = sem("gt_ready")
                ctx_psum = sem("ctx_psum")
                ctxt_ready = sem("ctxt_ready")
                ctxt_zero = sem("ctxt_zero")
                cwo_psum = sem("cwo_psum")
                block = ctx.enter_context(nc.Block())

                @block.gpsimd
                def _(pool):
                    pool.memset(ctxt[:], 0.0).then_inc(ctxt_zero, 1)
                    pool.memset(kacc[:], 0.0).then_inc(kacc_step, 1)
                    with pool.Fori(0, NT) as t:
                        pool.wait_ge(kacc_step, t + 1)
                        pool.wait_ge(fk_ready, t + 1)
                        pool.tensor_tensor(kacc[:], kacc[:], fk[:, ds(t, 1), :].rearrange("p a f -> p (a f)"),
                                           ALU.add).then_inc(kacc_step, 1)

                @block.vector
                def _(dve):
                    dve.tensor_reduce(km[:, 0:1], kmax[:], axis=AX.X, op=ALU.max).then_inc(k_step, 1)
                    dve.wait_ge(km_t, 1)
                    dve.tensor_reduce(km[0:1, 1:2], PS[0:1, 0:P], axis=AX.X, op=ALU.max).then_inc(km_row, 1)
                    dve.wait_ge(km_b, 1)
                    dve.tensor_scalar(km[:, 2:3], PS[:, CH:CH + 1], -1.0, None, ALU.mult).then_inc(kneg, 1)
                    with dve.Fori(0, NT) as t:
                        dve.wait_ge(k_exp, t + 1)
                        k = fk[:, ds(t, 1), :].rearrange("p a f -> p (a f)")
                        dve.tensor_scalar(k, k, FEAT_EPS, RATIO, ALU.add, ALU.mult).then_inc(fk_ready, 1)
                    with dve.Fori(0, NT) as t:
                        q = fq[:, ds(t, 1), :].rearrange("p a f -> p (a f)")
                        dve.tensor_scalar(q, q, FEAT_EPS, RATIO, ALU.add, ALU.mult)
                    dve.wait_ge(ctxt_zero, 1)
                    dve.wait_ge(ctx_psum, NP)
                    for p in range(NP):
                        for i in range(2):
                            o = (p % 2) * 2 * M + i * M
                            dve.tensor_copy(ctxt[i * DH:(i + 1) * DH, p, o:o + M],
                                            PS[i * DH:(i + 1) * DH,
                                               4 * CH + p * 2 * M + i * M:4 * CH + p * 2 * M + (i + 1) * M]
                                            ).then_inc(ctxt_ready, 1)

                @block.scalar
                def _(act):
                    act.wait_ge(kneg, 1)
                    with act.Fori(0, NT) as t:
                        k = fk[:, ds(t, 1), :].rearrange("p a f -> p (a f)")
                        act.activation(k, k, ACT.Exp, bias=km[:, 2:3]).then_inc(k_exp, 1)
                    act.wait_ge(gt_psum, 1)
                    act.activation(gt[:], bank(2), ACT.Copy).then_inc(gt_ready, 1)
                    act.wait_ge(ks_psum, 1)
                    act.activation(ksum[:], bank(3), ACT.Copy)
                    act.wait_ge(cwo_psum, 1)
                    act.activation(cwo[:].rearrange("p g d -> p (g d)"), bank(5), ACT.Copy)

                @block.tensor
                def _(pe):
                    pe.wait_ge(k_step, 1)
                    pe.transpose(PS[0:1, 0:P], km[:, 0:1], ident[:]).then_inc(km_t, 1)
                    pe.wait_ge(km_row, 1)
                    pe.matmul(PS[:, CH:CH + 1], ones[0:1, :], km[0:1, 1:2], start=True, stop=True).then_inc(km_b, 1)
                    for t in range(NT):
                        pe.wait_ge(fk_ready, t + 1)
                        mm = pe.matmul(bank(2), hx[:, t, :], fk[:, t, :], start=(t == 0), stop=(t == NT - 1))
                    mm.then_inc(gt_psum, 1)
                    pe.wait_ge(gt_ready, 1)
                    for p in range(NP):
                        pe.matmul(PS[:, 4 * CH + p * 2 * M:4 * CH + (p + 1) * 2 * M], wv[:, p * P:(p + 1) * P],
                                  gt[:, p * 2 * M:(p + 1) * 2 * M], start=True, stop=True,
                                  skip_group_check=True).then_inc(ctx_psum, 1)
                    pe.wait_ge(kacc_step, NT + 1)
                    pe.matmul(bank(3), ones[:], kacc[:], start=True, stop=True).then_inc(ks_psum, 1)
                    pe.wait_ge(ctxt_ready, 2 * NP)
                    for p in range(NP):
                        g = p // 2
                        mm = pe.matmul(PS[:, 5 * CH + g * P:5 * CH + (g + 1) * P], ctxt[:, p, :], wo[:, p, :],
                                       start=(p % 2 == 0), stop=(p % 2 == 1), skip_group_check=True)
                    mm.then_inc(cwo_psum, 1)

        ksum = sb("ksum", [P, FE], on=fb)
        cwo = sb("cwo", [P, FE // P, P], on=fb)

        def attend():
            ctx = ExitStack()
            with ctx:
                G = FE // P
                qk = sb("qk", [P, 2, FE], on=ctx)
                den = sb("den", [P, 2, 2, NH], on=ctx)
                qs = sb("qs", [P, 2, FE], on=ctx)
                qt = sb("qt", [P, G, CH], on=ctx)
                ob = sb("ob1", [P, CH], on=ctx)
                qk_ready = sem("qk_ready")
                den_step = sem("den_step")
                qs_ready = sem("qs_ready")
                qt_psum = sem("qt_psum")
                qt_ready = sem("qt_ready")
                o1_ready = sem("o1_ready")
                ob1_ready = sem("ob1_ready")
                x1_added = sem("x1_added")
                block = ctx.enter_context(nc.Block())

                @block.gpsimd
                def _(pool):
                    pool.sem_inc(qk_ready, 2)
                    with pool.Fori(0, NC) as c:
                        for t in range(TPC):
                            q = fq[:, ds(c * TPC + t, 1), :].rearrange("p a f -> p (a f)")
                            pool.wait_ge(qs_ready, c * TPC + (t + 1))
                            pool.tensor_tensor(qk[:, t % 2, :], q, ksum[:], ALU.mult).then_inc(qk_ready, 1)

                @block.vector
                def _(dve):
                    dve.sem_inc(qs_ready, 2)
                    dve.sem_inc(x1_added, 1)
                    def add_x(c):
                        dve.wait_ge(ob1_ready, c + 2)
                        dve.tensor_tensor(x[:, ds(c * CH, CH)], x[:, ds(c * CH, CH)], ob[:],
                                          ALU.add).then_inc(x1_added, 1)

                    def chunk(c, follows):
                        for t in range(TPC):
                            r = t % 2
                            dve.wait_ge(qk_ready, c * TPC + (t + 3))
                            dve.tensor_reduce(den[:, r, 0, :], heads(qk[:, r, :]), axis=AX.X,
                                              op=ALU.add).then_inc(den_step, 1)
                            dve.wait_ge(den_step, 2 * (c * TPC) + (2 * t + 1))
                            dve.reciprocal(den[:, r, 1, :], den[:, r, 0, :]).then_inc(den_step, 1)
                            dve.wait_ge(den_step, 2 * (c * TPC) + (2 * t + 2))
                            dve.wait_ge(qt_psum, c * TPC + (t + 1))
                            dve.tensor_tensor(heads(qs[:, r, :]),
                                              fq[:, ds(c * TPC + t, 1), :].rearrange("p a (h m) -> p (a h) m", m=M),
                                              wide_m(den[:, r, 1, :]), ALU.mult).then_inc(qs_ready, 1)
                            if t == 1 and follows:
                                add_x(c - 1)

                    chunk(0, False)
                    with dve.Fori(1, NC) as c:
                        chunk(c, True)
                    add_x(NC - 1)

                @block.tensor
                def _(pe):
                    pe.sem_inc(qt_psum, 2)
                    with pe.Fori(0, NC) as c:
                        for t in range(TPC):
                            r = t % 2
                            pe.wait_ge(qs_ready, c * TPC + (t + 3))
                            pe.wait_ge(qt_ready, c * TPC + (t + 1))
                            for g in range(G):
                                mm = pe.transpose(PS[:, r * CH + g * P:r * CH + (g + 1) * P],
                                                  qs[:, r, g * P:(g + 1) * P], ident[:])
                            mm.then_inc(qt_psum, 1)
                        pe.wait_ge(qt_ready, c * TPC + (TPC + 2))
                        pe.wait_ge(ob1_ready, c + 1)
                        for g in range(G):
                            mm = pe.matmul(bank(2), cwo[:, g, :], qt[:, g, :], start=(g == 0), stop=(g == G - 1))
                        mm.then_inc(o1_ready, 1)

                @block.scalar
                def _(act):
                    act.sem_inc(qt_ready, 2)
                    act.sem_inc(ob1_ready, 1)
                    with act.Fori(0, NC) as c:
                        for t in range(TPC):
                            r = t % 2
                            act.wait_ge(qt_psum, c * TPC + (t + 3))
                            act.activation(qt[:, :, t * P:(t + 1) * P],
                                           bank(r).rearrange("p (g t) -> p g t", g=G), ACT.Copy).then_inc(qt_ready, 1)
                        act.wait_ge(o1_ready, c + 1)
                        act.wait_ge(x1_added, c + 1)
                        act.activation(ob[:], bank(2), ACT.Identity, bias=ga_bo[:],
                                       scale=mod[:, 1, 2:3]).then_inc(ob1_ready, 1)

        features()
        context()
        attend()
        fb.close()
        tb.close()

        wb = ExitStack()
        nj1, whole1, high1, low1 = expert_weights(wb, 1, H1)
        hp1 = sb("hp1", [P, 2, T], F32R, on=wb)
        s_w1 = [sem(f"s_w1_{k}") for k in range(3)]
        ld = ExitStack()
        with ld:
            block = ld.enter_context(nc.Block())

            @block.sync
            def _(sp):
                sp.dma_start(whole1[0][:], a["w1_1"]).then_inc(s_w1[0], 16)
                sp.dma_start(whole1[1][:], a["w3_1"]).then_inc(s_w1[1], 16)
                sp.dma_start(whole1[2][:], a["w2_1"].rearrange("(j p) d -> p j d", p=P)).then_inc(s_w1[2], 16)
        layernorm("f1", 1, 3, 4, hp1)
        route("f1", 1, 1e-9, True, expert_pieces(nj1, whole1, high1, low1, H1, lambda e, k: (s_w1[k], 16)))
        experts("f1", H1, *[(high1[k], low1[k]) for k in range(3)], hp1, 5, 1)
        wb.close()

        s_out = sem("s_out")
        fin = ExitStack()
        with fin:
            block = fin.enter_context(nc.Block())

            @block.sync
            def _(sp):
                sp.dma_start(out, x[:]).then_inc(s_out, 16)
                sp.wait_ge(s_out, 16)


def kernel(**inputs):
    import numpy as np
    import concourse.bacc as bacc
    from concourse.bass_utils import run_bass_kernel_spmd

    def lay(v):
        return np.ascontiguousarray(v)

    def cols(v, n):
        return lay(np.reshape(v, (n, P)).T)

    i = {k: np.asarray(v) for k, v in inputs.items()}
    arrays = {
        "x": lay(i["L0_attn_x"][0].T),
        "c": lay(np.concatenate([i["L0_c"], i["L1_c"]], axis=0).T),
        "wmod0": i["L0_wmod"], "wmod1": i["L1_wmod"],
        "w_in": i["L0_attn_W_in"], "b_in": cols(i["L0_attn_b_in"], 2 * HV),
        "conv_w": lay(i["L0_attn_conv_w"].reshape(HV, P, KW).transpose(1, 0, 2)),
        "conv_b": cols(i["L0_attn_conv_b"], HV),
        "w_x": lay(i["L0_attn_W_x"].reshape(HV, P, RK + 2 * NS).transpose(1, 0, 2)),
        "w_dt": i["L0_attn_W_dt"], "b_dt": cols(i["L0_attn_b_dt"], HV),
        "w_out": lay(i["L0_attn_W_out"].reshape(HV, P, P).transpose(1, 0, 2)),
        "b_out": cols(i["L0_attn_b_out"], 1),
        "a_log": lay(i["L0_attn_A_log"].reshape(HV, P, NS).transpose(1, 0, 2)),
        "wg": lay(np.stack([i["L0_ffn_Wg"].T, i["L1_ffn_router_w"].T], axis=1)),
        "router_b": i["L1_ffn_router_b"],
        "w1_0": lay(i["L0_ffn_W1"].transpose(2, 0, 1).reshape(P, NE * H0)),
        "w3_0": lay(i["L0_ffn_W3"].transpose(2, 0, 1).reshape(P, NE * H0)),
        "w2_0": lay(i["L0_ffn_W2"].transpose(0, 2, 1)),
        "wq": i["L1_attn_Wq"], "wk": i["L1_attn_Wk"], "wv": i["L1_attn_Wv"], "wo": i["L1_attn_Wo"],
        "wqt": lay(i["L1_attn_Wq"].T), "wkt": lay(i["L1_attn_Wk"].T),
        "bo": cols(i["L1_attn_bo"], 1), "pt": lay(i["L1_attn_P"].T),
        "w1_1": lay(i["L1_ffn_w_gate"].transpose(2, 0, 1).reshape(P, NE * H1)),
        "w3_1": lay(i["L1_ffn_w_up"].transpose(2, 0, 1).reshape(P, NE * H1)),
        "w2_1": lay(i["L1_ffn_w_down"].transpose(0, 2, 1).reshape(NE * H1, P)),
    }
    nc = bacc.Bacc("TRN2", target_bir_lowering=False, num_devices=1)
    arrays = {f"in_{k}": lay(v) for k, v in arrays.items()}
    aps = {k[3:]: nc.dram_tensor(k, v.shape, mybir.dt.from_np(v.dtype), kind="ExternalInput").ap()
           for k, v in arrays.items()}
    out = nc.dram_tensor("out", (P, T), F32, kind="ExternalOutput").ap()
    build(nc, aps, out)
    r = run_bass_kernel_spmd(nc, [arrays], core_ids=[0])
    return lay(r.results[0]["out"].T)[None]
```

```python
import math
from contextlib import ExitStack

import concourse.bass as bass
from concourse import mybir

F32 = mybir.dt.float32
F32R = mybir.dt.float32r
BF16 = mybir.dt.bfloat16
ALU = mybir.AluOpType
ACT = mybir.ActivationFunctionType
AX = mybir.AxisListType
ds = bass.ds

P = 128
T = 2048
CH = 512
NC = T // CH
TPC = CH // P
NT = T // P
DI = 256
HV = DI // P
NS = 16
RK = 64
KW = 3
NE = 8
H0 = 352
H1 = 256
NH, DH, M = 16, 64, 32
NP = NH // 2
FE = NH * M
LN_EPS = 1e-5
FEAT_EPS = 1e-4
QW = 4
DN = DH ** -0.25
RATIO = M ** -0.5


def build(nc, a, out):
    top = ExitStack()
    with top:
        def sb(name, shape, dt=F32, on=top, **kw):
            return on.enter_context(nc.sbuf_tensor(name, shape, dt, **kw))

        live = []

        def sem(name):
            live.append(nc.alloc_semaphore(name))
            return live[-1]

        PS = top.enter_context(nc.psum_tensor("PS", [P, 8 * CH], F32))

        def bank(b, n=1):
            return PS[:, b * CH:(b + n) * CH]

        def product(pe, into, w, v, start=True, stop=True):
            pe.matmul(into, w[0], v[0], start=start, stop=False)
            pe.matmul(into, w[0], v[1], start=False, stop=False)
            return pe.matmul(into, w[1], v[0], start=False, stop=stop)

        x = sb("x", [P, T])
        h = sb("h", [P, T])
        ident = sb("ident", [P, P])
        ident_bf = sb("ident_bf", [P, P], BF16)
        mean_w = sb("mean_w", [P, P])
        ones = sb("ones", [P, P])
        ln_eps = sb("ln_eps", [P, 1])
        spare = sb("spare", [P, 1])
        sel = sb("sel", [96, 32, P], BF16)
        cvec = sb("cvec", [P, 2])
        wmod = sb("wmod", [P, 2, 6 * P])
        mod = sb("mod", [P, 2, 6])
        hot = sb("hot", [96, 32])
        gtmp = sb("gtmp", [P, 2, 2, 2])
        wg = sb("wg", [P, 2, NE])
        rb = sb("rb", [P, NE])
        cw_split = sb("cw_split", [96, T], BF16)

        s_load = sem("s_load")
        s_c, s_wmod, s_x = sem("s_c"), [sem(f"s_wmod{l}") for l in range(2)], sem("s_x")
        s_w0 = [[sem(f"s_w0_{q}_{k}") for k in range(3)] for q in range(QW)]
        s_wt = [nc.alloc_semaphore(f"wt_loaded_{k}") for k in "kq"]
        s_wkq = [nc.alloc_semaphore(f"w_loaded_{k}") for k in "kq"]
        s_rest = nc.alloc_semaphore("rest_loaded")
        s_pt = nc.alloc_semaphore("pt_loaded")

        def issue(sp, loads):
            for dst, src, done in loads:
                sp.dma_start(dst, src).then_inc(done, 16)

        def layernorm(tag, layer, shift_col, scale_col, parts=None, loads=(), beside=None):
            ctx = ExitStack()
            with ctx:
                xc = sb(f"xc_{tag}", [P, T], on=ctx)
                sq = sb(f"sq_{tag}", [P, T], on=ctx)
                mean_ready = sem(f"mean_ready_{tag}")
                centred = sem(f"centred_{tag}")
                squared = sem(f"squared_{tag}")
                var_ready = sem(f"var_ready_{tag}")
                log_ready = sem(f"log_ready_{tag}")
                rstd_ready = sem(f"rstd_ready_{tag}")
                normed = sem(f"normed_{tag}")
                h_ready = sem(f"h_ready_{tag}")
                h_high = sem(f"h_high_{tag}")


                def also(key, *args):
                    if beside and key in beside:
                        beside[key](*args)

                block = ctx.enter_context(nc.Block())

                @block.sync
                def _(sp):
                    issue(sp, loads)
                    also("sp", sp)

                @block.gpsimd
                def _(pool):
                    also("pool", pool)

                @block.tensor
                def _(pe):
                    for c in range(NC):
                        pe.matmul(PS[:, c * CH:(c + 1) * CH], mean_w[:], x[:, c * CH:(c + 1) * CH],
                                  start=True, stop=True).then_inc(mean_ready, 1)
                    if beside and "pe_mid" in beside:
                        pe.wait_ge(centred, 2)
                        beside["pe_mid"](pe)
                    for c in range(NC):
                        pe.wait_ge(squared, c + 1)
                        pe.matmul(PS[:, (NC + c) * CH:(NC + c + 1) * CH], mean_w[:], sq[:, c * CH:(c + 1) * CH],
                                  start=True, stop=True).then_inc(var_ready, 1)
                    also("pe_end", pe, h_ready)

                @block.vector
                def _(dve):
                    for c in range(NC):
                        dve.wait_ge(mean_ready, c + 1)
                        dve.tensor_tensor(xc[:, c * CH:(c + 1) * CH], x[:, c * CH:(c + 1) * CH], PS[:, c * CH:(c + 1) * CH],
                                          ALU.subtract).then_inc(centred, 1)
                    also("dve_mid", dve)
                    for c in range(NC):
                        dve.wait_ge(rstd_ready, c + 1)
                        dve.tensor_tensor(xc[:, c * CH:(c + 1) * CH], xc[:, c * CH:(c + 1) * CH], sq[:, c * CH:(c + 1) * CH],
                                          ALU.mult).then_inc(normed, 1)
                    for c in range(NC if parts else 0):
                        tok = slice(c * CH, (c + 1) * CH)
                        dve.wait_ge(h_ready, c + 1)
                        dve.tensor_copy(parts[:, 0, tok], h[:, tok]).then_inc(h_high, 1)
                        dve.wait_ge(h_high, c + 1)
                        dve.tensor_tensor(parts[:, 1, tok], h[:, tok], parts[:, 0, tok].bitcast(F32), ALU.subtract)
                    also("dve_end", dve)

                @block.scalar
                def _(act):
                    act.activation(spare[:], ones[:, 0:1], ACT.Ln)
                    for c in range(NC):
                        act.wait_ge(centred, c + 1)
                        act.activation(sq[:, c * CH:(c + 1) * CH], xc[:, c * CH:(c + 1) * CH],
                                       ACT.Square).then_inc(squared, 1)
                    for c in range(NC):
                        act.wait_ge(var_ready, c + 1)
                        act.activation(sq[:, c * CH:(c + 1) * CH], PS[:, (NC + c) * CH:(NC + c + 1) * CH], ACT.Ln,
                                       bias=ln_eps[:]).then_inc(log_ready, 1)
                    for c in range(NC + 2):
                        if c < NC:
                            act.wait_ge(log_ready, c + 1)
                            act.activation(sq[:, c * CH:(c + 1) * CH], sq[:, c * CH:(c + 1) * CH], ACT.Exp,
                                           scale=-0.5).then_inc(rstd_ready, 1)
                        if c >= 2:
                            act.wait_ge(normed, c - 1)
                            tok = slice((c - 2) * CH, (c - 1) * CH)
                            act.activation(h[:, tok], xc[:, tok], ACT.Identity,
                                           bias=mod[:, layer, shift_col:shift_col + 1],
                                           scale=mod[:, layer, scale_col:scale_col + 1]).then_inc(h_ready, 1)
                    also("act_end", act)

        def logits(pe, h_ready, layer):
            for t in range(NT):
                if t % TPC == 0:
                    pe.wait_ge(h_ready, t // TPC + 1)
                pe.matmul(PS[:, t * NE:(t + 1) * NE], h[:, t * P:(t + 1) * P], wg[:, layer, :],
                          start=True, stop=True, skip_group_check=True)

        def cut_high(act, cuts, done):
            for whole, high, _, loaded in cuts:
                act.wait_ge(loaded, 16)
                act.activation(high, whole, ACT.Copy).then_inc(done, 1)

        def copy_high(dve, cuts, done):
            for whole, high, _, loaded in cuts:
                dve.wait_ge(loaded, 16)
                dve.tensor_copy(high, whole).then_inc(done, 1)

        def cut_low(pool, cuts, high_ready):
            for k, (whole, high, low, _) in enumerate(cuts):
                pool.wait_ge(high_ready, k + 1)
                pool.tensor_tensor(low, whole, high.bitcast(F32), ALU.subtract)

        def route(tag, layer, den_eps, with_bias, cuts):
            ctx = ExitStack()
            with ctx:
                lg = sb(f"lg_{tag}", [P, NT, NE], on=ctx)
                pr = sb(f"pr_{tag}", [P, NT, NE], on=ctx)
                eq = sb(f"eq_{tag}", [P, NT, NE], on=ctx)
                cw = sb(f"cw_{tag}", [P, NT, NE], on=ctx)
                cw3 = sb(f"cw3_{tag}", [P, NT, 96], BF16, on=ctx)
                oh = sb(f"oh_{tag}", [P, 2, NT, NE], on=ctx)
                rest = sb(f"rest_{tag}", [P, NT, NE], on=ctx)
                order = sb(f"order_{tag}", [P, NE], on=ctx)
                st = sb(f"st_{tag}", [P, 8, NT], on=ctx)
                shifted = sem(f"shifted_{tag}")
                exp_ready = sem(f"exp_ready_{tag}")
                chain = sem(f"route_step_{tag}")
                cw_ready = sem(f"cw_ready_{tag}")
                cwt_psum = sem(f"cwt_psum_{tag}")
                order_ready = sem(f"order_ready_{tag}")
                high_ready = sem(f"high_ready_{tag}")
                block = ctx.enter_context(nc.Block())

                @block.tensor
                def _(pe):
                    pe.wait_ge(cw_ready, 1)
                    for c in range(NC):
                        for t in range(c * TPC, (c + 1) * TPC):
                            mm = pe.matmul(PS[0:96, (CH + t * P):(CH + (t + 1) * P)], cw3[:, t, :], ident_bf[:],
                                           start=True, stop=True, skip_group_check=True)
                        mm.then_inc(cwt_psum, 1)

                @block.gpsimd
                def _(pool):
                    for e in range(NE):
                        i = pool.memset(order[:, e:e + 1], float(NE - e))
                    i.then_inc(order_ready, 1)
                    pool.memset(cw3[:], 0.0).then_inc(order_ready, 1)
                    cut_low(pool, cuts[:-2], high_ready)

                @block.scalar
                def _(act):
                    cut_high(act, cuts[:3], high_ready)
                    act.wait_ge(shifted, 1)
                    act.activation(pr[:], lg[:], ACT.Exp).then_inc(exp_ready, 1)
                    cut_high(act, cuts[3:], high_ready)
                    act.wait_ge(cwt_psum, NC)
                    act.activation(cw_split[:, T // 2:T], PS[0:96, CH + T // 2:CH + T], ACT.Copy)

                @block.vector
                def _(dve):
                    steps = [0]

                    def wide(v):
                        return v.unsqueeze(2).broadcast_to([P, NT, NE])

                    def step(ins):
                        steps[0] += 1
                        ins.then_inc(chain, 1)
                        dve.wait_ge(chain, steps[0])

                    psl = PS[:, 0:NT * NE].rearrange("p (t e) -> p t e", e=NE)
                    if with_bias:
                        step(dve.tensor_tensor(lg[:], psl, rb[:].unsqueeze(1).broadcast_to([P, NT, NE]), ALU.add))
                    else:
                        step(dve.tensor_copy(lg[:], psl))
                    step(dve.tensor_reduce(st[:, 0, :], lg[:], axis=AX.X, op=ALU.max))
                    dve.tensor_tensor(lg[:], lg[:], wide(st[:, 0, :]), ALU.subtract).then_inc(shifted, 1)
                    dve.wait_ge(exp_ready, 1)
                    step(dve.tensor_reduce(st[:, 1, :], pr[:], axis=AX.X, op=ALU.add))
                    step(dve.reciprocal(st[:, 2, :], st[:, 1, :]))
                    step(dve.tensor_tensor(pr[:], pr[:], wide(st[:, 2, :]), ALU.mult))
                    dve.wait_ge(order_ready, 2)
                    left = pr
                    for k in range(2):
                        step(dve.tensor_reduce(st[:, 3 + k, :], left[:], axis=AX.X, op=ALU.max))
                        step(dve.tensor_tensor(eq[:], left[:], wide(st[:, 3 + k, :]), ALU.is_equal))
                        step(dve.tensor_tensor(eq[:], eq[:], order[:].unsqueeze(1).broadcast_to([P, NT, NE]),
                                               ALU.mult))
                        step(dve.tensor_reduce(st[:, 5, :], eq[:], axis=AX.X, op=ALU.max))
                        step(dve.tensor_tensor(oh[:, k], eq[:], wide(st[:, 5, :]), ALU.is_equal))
                        if k == 0:
                            step(dve.scalar_tensor_tensor(rest[:], oh[:, 0], -2.0, pr[:], ALU.mult, ALU.add))
                            left = rest
                    step(dve.scalar_tensor_tensor(st[:, 6, :], st[:, 3, :], den_eps, st[:, 4, :], ALU.add, ALU.add))
                    step(dve.reciprocal(st[:, 7, :], st[:, 6, :]))
                    step(dve.tensor_tensor(oh[:, 0], oh[:, 0], oh[:, 1], ALU.add))
                    step(dve.tensor_tensor(oh[:, 0], oh[:, 0], pr[:], ALU.mult))
                    step(dve.tensor_tensor(cw[:], oh[:, 0], wide(st[:, 7, :]), ALU.mult))
                    step(dve.tensor_copy(cw3[:, :, 0:NE], cw[:]))
                    step(dve.tensor_tensor(cw[:], cw[:], cw3[:, :, 0:NE], ALU.subtract))
                    step(dve.tensor_copy(cw3[:, :, 32:32 + NE], cw[:]))
                    dve.tensor_tensor(cw3[:, :, 64:64 + NE], cw[:], cw3[:, :, 32:32 + NE],
                                      ALU.subtract).then_inc(cw_ready, 1)
                    for k, (whole, high, low, _) in list(enumerate(cuts))[-2:]:
                        dve.wait_ge(high_ready, k + 1)
                        dve.tensor_tensor(low, whole, high.bitcast(F32), ALU.subtract)
                    dve.wait_ge(cwt_psum, NC // 2)
                    dve.tensor_copy(cw_split[:, 0:T // 2], PS[0:96, CH:CH + T // 2])

        def experts(tag, width, wgate, wup, wdown, hp, gate_col, layer, loads=(), store=None):
            ctx = ExitStack()
            with ctx:
                NI = NE * width // P

                def spread_column(i):
                    e = i * P // width
                    return (e + 1) * P - min(P, (e + 1) * width - i * P)

                firsts = [i for i in range(NI) if i == 0 or spread_column(i) != spread_column(i - 1)]
                NSP = len(firsts)
                HIGH_LAG, LOW_LAG, DOWN_LAG = 1, 2, 4
                RG, RU, RS, RH, RW = 2, 4, 4, 6, 2
                CREDIT = 8
                sg = sb(f"sg_{tag}", [P, RS, CH], on=ctx)
                sw = sb(f"sw_{tag}", [P, RS, CH], on=ctx)
                hid = sb(f"hid_{tag}", [P, RH, CH], on=ctx)
                hid_high = sb(f"hid_high_{tag}", [P, RH, CH], F32R, on=ctx)
                hid_low = sb(f"hid_low_{tag}", [P, RH, CH], F32R, on=ctx)
                cwb = sb(f"cwb_{tag}", [P, RW, CH], on=ctx)
                gate_ready = sem(f"gate_ready_{tag}")
                up_ready = sem(f"up_ready_{tag}")
                spread_ready = sem(f"spread_ready_{tag}")
                silu_ready = sem(f"silu_ready_{tag}")
                cwb_ready = sem(f"cwb_ready_{tag}")
                weighed = sem(f"weighed_{tag}")
                hid_ready = sem(f"hid_ready_{tag}")
                high_ready = sem(f"hid_high_ready_{tag}")
                low_ready = sem(f"hid_low_ready_{tag}")
                down_done = sem(f"down_done_{tag}")
                added = sem(f"added_{tag}")
                block = ctx.enter_context(nc.Block())
                BW, BO = RG + RU, RG + RU + 1

                def lagging(i, lag, c, follows, what):
                    if i >= lag:
                        what(c, i - lag)
                    elif follows:
                        what(c - 1, NI + i - lag)

                def done(c, i):
                    return c * NI + (CREDIT + i + 1)

                def slot_free(c, i, ring):
                    last = i - ring if i >= ring else max(t for t in range(NI) if t % ring == i) - NI
                    return done(c, last)

                @block.sync
                def _(sp):
                    issue(sp, loads)
                    if store is not None:
                        for c in range(NC):
                            tok = slice(c * CH, (c + 1) * CH)
                            sp.wait_ge(added, c + 2)
                            sp.dma_start(store[:, tok], x[:, tok]).then_inc(s_out, 16)
                        sp.wait_ge(s_out, 16 * NC)

                @block.tensor
                def _(pe):
                    pe.sem_inc(down_done, CREDIT)

                    def down(c, i):
                        pe.wait_ge(low_ready, c * NI + (i + 1))
                        if i == 0:
                            pe.wait_ge(added, c + 1)
                        product(pe, bank(BO), [w[:, i, :] for w in wdown],
                                [v[:, i % RH, :] for v in (hid_high, hid_low)],
                                start=(i == 0), stop=(i == NI - 1)).then_inc(down_done, 1)

                    def chunk(c, follows):
                        hc = [hp[:, k, ds(c * CH, CH)] for k in range(2)]
                        for i in range(NI):
                            if i in firsts:
                                k, col = firsts.index(i), spread_column(i)
                                pe.wait_ge(cwb_ready, c * NSP + k + 1)
                                pe.matmul(bank(BW), sel[:].rearrange("k j p -> k (j p)")[:, col:col + P],
                                          cw_split[:, ds(c * CH, CH)], start=True, stop=True).then_inc(spread_ready, 1)
                            rows = slice(i * P, (i + 1) * P)
                            pe.wait_ge(silu_ready, slot_free(c, i, RG))
                            product(pe, bank(i % RG), [w[:, rows] for w in wgate], hc).then_inc(gate_ready, 1)
                            pe.wait_ge(hid_ready, slot_free(c, i, RU))
                            product(pe, bank(RG + i % RU), [w[:, rows] for w in wup], hc).then_inc(up_ready, 1)
                            if i == DOWN_LAG + 1:
                                down(c, 0)
                            if i != DOWN_LAG:
                                lagging(i, DOWN_LAG, c, follows, down)

                    chunk(0, False)
                    with pe.Fori(1, NC) as c:
                        chunk(c, True)
                    for i in range(NI - DOWN_LAG, NI):
                        down(NC - 1, i)

                @block.scalar
                def _(act):
                    act.sem_inc(silu_ready, CREDIT)
                    act.sem_inc(cwb_ready, 1)

                    def high(c, i):
                        act.wait_ge(hid_ready, done(c, i))
                        act.wait_ge(down_done, slot_free(c, i, RH))
                        act.activation(hid_high[:, i % RH, :], hid[:, i % RH, :], ACT.Copy).then_inc(high_ready, 1)

                    def chunk(c, follows):
                        for i in range(NI):
                            act.wait_ge(gate_ready, c * NI + i + 1)
                            act.wait_ge(weighed, slot_free(c, i, RS))
                            act.activation(sg[:, i % RS, :], bank(i % RG), ACT.Silu).then_inc(silu_ready, 1)
                            if i in firsts:
                                k = firsts.index(i)
                                act.wait_ge(spread_ready, c * NSP + k + 1)
                                between = firsts[k - 1] - (NI if k == 0 else 0)
                                act.wait_ge(weighed, done(c, between - 1))
                                act.activation(cwb[:, k % RW, :], bank(BW), ACT.Copy).then_inc(cwb_ready, 1)
                            lagging(i, HIGH_LAG, c, follows, high)

                    chunk(0, False)
                    with act.Fori(1, NC) as c:
                        chunk(c, True)
                    for i in range(NI - HIGH_LAG, NI):
                        high(NC - 1, i)

                @block.gpsimd
                def _(pool):
                    pool.sem_inc(weighed, CREDIT)
                    with pool.Fori(0, NC) as c:
                        for i in range(NI):
                            pool.wait_ge(silu_ready, done(c, i))
                            k = sum(f <= i for f in firsts) - 1
                            if i in firsts:
                                pool.wait_ge(cwb_ready, c * NSP + (k + 2))
                            pool.wait_ge(hid_ready, slot_free(c, i, RS))
                            pool.tensor_tensor(sw[:, i % RS, :], sg[:, i % RS, :], cwb[:, k % RW, :],
                                               ALU.mult).then_inc(weighed, 1)

                @block.vector
                def _(dve):
                    dve.sem_inc(hid_ready, CREDIT)
                    dve.sem_inc(added, 1)

                    def low(c, i):
                        dve.wait_ge(high_ready, c * NI + (i + 1))
                        dve.tensor_tensor(hid_low[:, i % RH, :], hid[:, i % RH, :],
                                          hid_high[:, i % RH, :].bitcast(F32), ALU.subtract).then_inc(low_ready, 1)

                    def add(c):
                        dve.wait_ge(down_done, done(c, NI - 1))
                        xc = x[:, ds(c * CH, CH)]
                        dve.scalar_tensor_tensor(xc, bank(BO), mod[:, layer, gate_col:gate_col + 1], xc,
                                                 ALU.mult, ALU.add).then_inc(added, 1)

                    def chunk(c, follows):
                        for i in range(NI):
                            dve.wait_ge(up_ready, c * NI + i + 1)
                            dve.wait_ge(weighed, done(c, i))
                            if follows or i >= RH:
                                dve.wait_ge(low_ready, slot_free(c, i, RH) - CREDIT)
                            dve.tensor_tensor(hid[:, i % RH, :], sw[:, i % RS, :], bank(RG + i % RU),
                                              ALU.mult).then_inc(hid_ready, 1)
                            lagging(i, LOW_LAG, c, follows, low)
                            if i == DOWN_LAG - 1 and follows:
                                add(c - 1)

                    chunk(0, False)
                    with dve.Fori(1, NC) as c:
                        chunk(c, True)
                    for i in range(NI - LOW_LAG, NI):
                        low(NC - 1, i)
                    add(NC - 1)

        ab = ExitStack()
        w_in = sb("w_in", [P, 2 * DI], on=ab)
        b_in = sb("b_in", [P, 2 * HV], on=ab)
        conv_w = sb("conv_w", [P, HV, KW], on=ab)
        conv_b = sb("conv_b", [P, HV], on=ab)
        w_x = sb("w_x", [P, HV, RK + 2 * NS], on=ab)
        w_dt = sb("w_dt", [RK, DI], on=ab)
        b_dt = sb("b_dt", [P, HV], on=ab)
        w_out = sb("w_out", [P, HV, P], on=ab)
        b_out = sb("b_out", [P, 1], on=ab)
        a_neg = sb("a_neg", [P, HV, NS], on=ab)
        ga_b = sb("ga_b", [P, 1], on=ab)

        small_loads = [
            (cvec[:], a["c"], s_c), (wmod[:, 0, :], a["wmod0"], s_wmod[0]), (x[:], a["x"], s_x),
            (wmod[:, 1, :], a["wmod1"], s_wmod[1]),
        ] + [(dst, src, s_load) for dst, src in (
            (a_neg[:], a["a_log"]), (b_out[:], a["b_out"]),
            (w_in[:], a["w_in"]), (b_in[:], a["b_in"]), (conv_w[:], a["conv_w"]), (conv_b[:], a["conv_b"]),
            (w_x[:], a["w_x"]), (w_dt[:], a["w_dt"]), (b_dt[:], a["b_dt"]), (w_out[:], a["w_out"]),
            (wg[:], a["wg"]), (rb[:], a["router_b"].partition_broadcast(P)),
        )]
        n_load = 16 * sum(done is s_load for _, _, done in small_loads)

        def modulation_products(pe, layer, col):
            pe.wait_ge(s_wmod[layer], 16)
            for k in range(6):
                mm = pe.matmul(PS[:, col + k:col + k + 1], wmod[:, layer, k * P:(k + 1) * P],
                               cvec[:, layer:layer + 1], start=True, stop=True, skip_group_check=True)
            mm.then_inc(s_mod, 1)

        def modulation_vectors(dve, layer, col):
            m = mod[:, layer]
            t = gtmp[:, layer]
            step0 = 4 * layer
            dve.wait_ge(s_mod, layer + 1)
            dve.tensor_copy(m, PS[:, col:col + 6]).then_inc(s_gate, 1)
            dve.wait_ge(s_gate, step0 + 1)
            gates = m[:, 2:6:3]
            dve.scalar_tensor_tensor(t[:, 0], gates, -1.0, gates, ALU.mult, ALU.max).then_inc(s_gate, 1)
            dve.tensor_scalar(t[:, 1], gates, 0.0, 2.0, ALU.is_ge, ALU.mult).then_inc(s_gate, 1)
            dve.wait_ge(s_gate, step0 + 3)
            dve.tensor_scalar(t[:, 1], t[:, 1], -1.0, None, ALU.add).then_inc(s_gate, 1)
            dve.wait_ge(s_gate, step0 + 4)
            dve.scalar_tensor_tensor(gates, t[:, 0], 0.25, t[:, 1], ALU.max, ALU.mult)
            dve.tensor_scalar(m[:, 1:6:3], m[:, 1:6:3], 1.0, None, ALU.add)

        s_const = sem("s_const")
        s_silu_c = sem("s_silu_c")
        s_mod = sem("s_mod")
        s_gate = sem("s_gate")
        blk = ExitStack()
        with blk:
            block = blk.enter_context(nc.Block())

            @block.sync
            def _(sp):
                issue(sp, small_loads[:3])

            @block.gpsimd
            def _(pool):
                pool.memset(hot[:], 0.0).then_inc(s_const, 1)
                pool.memset(ident[:], 0.0).then_inc(s_const, 1)
                pool.memset(ones[:], 1.0)
                pool.memset(mean_w[:], 1.0 / P)
                pool.memset(ln_eps[:], LN_EPS)
                pool.wait_ge(s_const, 2)
                for g in range(3):
                    pool.affine_select(out=hot[:], in_=hot[:], compare_op=ALU.not_equal, fill=1.0,
                                       base=-32 * g, pattern=[[-1, 32]], channel_multiplier=1).then_inc(s_const, 1)
                    pool.wait_ge(s_const, 3 + g)
                pool.affine_select(out=ident[:], in_=ident[:], compare_op=ALU.not_equal, fill=1.0,
                                   base=0, pattern=[[-1, P]], channel_multiplier=1).then_inc(s_const, 1)

            @block.scalar
            def _(act):
                act.wait_ge(s_c, 16)
                act.activation(cvec[:], cvec[:], ACT.Silu).then_inc(s_silu_c, 1)

            @block.tensor
            def _(pe):
                pe.wait_ge(s_silu_c, 1)
                modulation_products(pe, 0, 0)
                pe.wait_ge(s_x, 16)

            @block.vector
            def _(dve):
                dve.wait_ge(s_const, 5)
                dve.tensor_copy(sel[:], hot[:].unsqueeze(2).broadcast_to([96, 32, P]))
                dve.wait_ge(s_const, 6)
                dve.tensor_copy(ident_bf[:], ident[:])
                modulation_vectors(dve, 0, 0)

        a_exp = sem("a_exp")

        def decay(act):
            act.wait_ge(s_load, n_load)
            act.activation(a_neg[:], a_neg[:], ACT.Exp).then_inc(a_exp, 1)

        def scan_constants(dve):
            dve.wait_ge(a_exp, 1)
            dve.tensor_scalar(a_neg[:], a_neg[:], -1.0, None, ALU.mult)
            dve.tensor_tensor(ga_b[:], mod[:, 0, 2:3], b_out[:], ALU.mult)
            modulation_vectors(dve, 1, 0)

        layernorm("a0", 0, 0, 1, loads=small_loads[3:],
                  beside=dict(act_end=decay, pe_end=lambda pe, _: modulation_products(pe, 1, 0),
                              dve_end=scan_constants))

        sc = ExitStack()
        u = sb("u", [P, HV, T], on=sc)
        rg = sb("rg", [P, HV, T], on=sc)
        delta = sb("delta", [P, HV, T], on=sc)
        bc_split = sb("bc_split", [96, T], BF16, on=sc)

        def scan_inputs():
            ctx = ExitStack()
            with ctx:
                ur = sb("ur", [P, HV, T + KW - 1], on=ctx)
                cv = sb("cv", [P, HV, CH], on=ctx)
                taps = sb("taps", [P, HV, CH], on=ctx)
                dt = sb("dt", [RK, CH], on=ctx)
                bc = sb("bc", [2 * NS, CH], on=ctx)
                bc_rest = sb("bc_rest", [2 * NS, CH], on=ctx)
                bc_mid = sb("bc_mid", [2 * NS, CH], BF16, on=ctx)
                vmax = sb("vmax", [P, HV, T], on=ctx)
                pad_ready = sem("pad_ready")
                xr_ready = sem("xr_ready")
                ur_ready = sem("ur_ready")
                rg_ready = sem("rg_ready")
                conv_step = sem("conv_step")
                conv_ready = sem("conv_ready")
                u_ready = sem("u_ready")
                xp_ready = sem("xp_ready")
                dt_ready = sem("dt_ready")
                bc_ready = sem("bc_ready")
                split_step = sem("split_step")
                v_ready = sem("v_ready")
                v_abs = sem("v_abs")
                v_max = sem("v_max")
                soft_exp = sem("soft_exp")
                soft_ln = sem("soft_ln")
                delta_ready = sem("delta_ready")
                block = ctx.enter_context(nc.Block())
                XP_BANK, V_BANK = 2 * HV, 2 * HV + 1
                pieces = [lambda v, j=j, t=t: v[:, j, t:t + T // 2] for j in range(HV) for t in (0, T // 2)]
                POOL_SHARE = 2

                @block.tensor
                def _(pe):
                    def after(c):
                        pe.wait_ge(dt_ready, c + 1)
                        pe.wait_ge(bc_ready, 2 * c + 2)
                        for j in range(HV):
                            pe.wait_ge(u_ready, c * HV + (HV + j + 1))
                            mm = pe.matmul(bank(XP_BANK)[0:RK + 2 * NS], w_x[:, j, :], u[:, j, ds(c * CH, CH)],
                                           start=(j == 0), stop=(j == HV - 1))
                        mm.then_inc(xp_ready, 1)
                        for j in range(HV):
                            pe.wait_ge(dt_ready, c + 2)
                            pe.wait_ge(v_max, c * HV + (j + 1))
                            pe.matmul(bank(V_BANK + j), w_dt[:, j * P:(j + 1) * P], dt[:],
                                      start=True, stop=True).then_inc(v_ready, 1)

                    def chunk(c, follows):
                        for j in range(2 * HV):
                            if j < HV:
                                pe.wait_ge(ur_ready, c * HV + (j + 1))
                            else:
                                pe.wait_ge(rg_ready, c * HV + (j - HV + 1))
                            pe.matmul(bank(j), w_in[:, j * P:(j + 1) * P], h[:, ds(c * CH, CH)],
                                      start=True, stop=True).then_inc(xr_ready, 1)
                        if follows:
                            after(c - 1)

                    chunk(0, False)
                    with pe.Fori(1, NC) as c:
                        chunk(c, True)
                    after(NC - 1)

                @block.scalar
                def _(act):
                    act.sem_inc(ur_ready, HV)
                    act.sem_inc(rg_ready, HV)
                    act.sem_inc(u_ready, HV)
                    act.sem_inc(dt_ready, 1)
                    act.sem_inc(bc_ready, 2)

                    def after(c):
                        act.wait_ge(xp_ready, c + 1)
                        act.activation(dt[:], bank(XP_BANK)[0:RK], ACT.Copy).then_inc(dt_ready, 1)
                        act.wait_ge(split_step, 4 * c + 4)
                        act.activation(bc[:], bank(XP_BANK)[RK:RK + 2 * NS], ACT.Copy).then_inc(bc_ready, 1)
                        act.activation(bc_split[0:2 * NS, ds(c * CH, CH)], bank(XP_BANK)[RK:RK + 2 * NS],
                                       ACT.Copy).then_inc(bc_ready, 1)
                        for j in range(HV):
                            act.wait_ge(v_ready, c * HV + (j + 1))
                            act.activation(delta[:, j, ds(c * CH, CH)], bank(V_BANK + j), ACT.Abs,
                                           bias=b_dt[:, j:j + 1]).then_inc(v_abs, 1)

                    def chunk(c, follows):
                        for j in range(HV):
                            act.wait_ge(xr_ready, c * 2 * HV + (j + 1))
                            act.activation(ur[:, j, ds(c * CH + (KW - 1), CH)], bank(j), ACT.Identity,
                                           bias=b_in[:, j:j + 1]).then_inc(ur_ready, 1)
                        for j in range(HV):
                            act.wait_ge(xr_ready, c * 2 * HV + (HV + j + 1))
                            act.activation(rg[:, j, ds(c * CH, CH)], bank(HV + j), ACT.Silu,
                                           bias=b_in[:, HV + j:HV + j + 1]).then_inc(rg_ready, 1)
                        if follows:
                            after(c - 1)
                        for j in range(HV):
                            act.wait_ge(conv_ready, c * HV + (j + 1))
                            act.activation(u[:, j, ds(c * CH, CH)], cv[:, j, :], ACT.Silu).then_inc(u_ready, 1)

                    chunk(0, False)
                    with act.Fori(1, NC) as c:
                        chunk(c, True)
                    after(NC - 1)
                    for step, (func, kw) in enumerate(((ACT.Exp, dict(scale=-1.0)), (ACT.Ln, dict(bias=ones[:, 0:1])))):
                        for k, piece in enumerate(pieces):
                            act.wait_ge(*((v_abs, HV * NC) if step == 0 else (soft_exp, k + 1)))
                            act.activation(piece(delta), piece(delta), func,
                                           **kw).then_inc(soft_exp if step == 0 else soft_ln, 1)

                @block.gpsimd
                def _(pool):
                    pool.memset(ur[:, :, 0:KW - 1], 0.0).then_inc(pad_ready, 1)
                    pool.sem_inc(split_step, 4)
                    with pool.Fori(0, NC) as c:
                        tok = ds(c * CH, CH)
                        pool.wait_ge(bc_ready, 2 * c + 4)
                        pool.tensor_tensor(bc_rest[:], bc[:], bc_split[0:2 * NS, tok],
                                           ALU.subtract).then_inc(split_step, 1)
                        pool.wait_ge(split_step, 4 * c + 5)
                        one = ones[0:2 * NS, 0:1].broadcast_to([2 * NS, CH])
                        pool.tensor_tensor(bc_mid[:], bc_rest[:], one, ALU.mult).then_inc(split_step, 1)
                        pool.tensor_tensor(bc_split[32:32 + 2 * NS, tok], bc_rest[:], one,
                                           ALU.mult).then_inc(split_step, 1)
                        pool.wait_ge(split_step, 4 * c + 7)
                        pool.tensor_tensor(bc_split[64:64 + 2 * NS, tok], bc_rest[:], bc_mid[:],
                                           ALU.subtract).then_inc(split_step, 1)
                        pool.wait_ge(split_step, 4 * c + 8)
                    for k, piece in enumerate(pieces[:POOL_SHARE]):
                        pool.wait_ge(delta_ready, k + 1)
                        pool.tensor_tensor(piece(u), piece(u), piece(delta), ALU.mult)

                @block.vector
                def _(dve):
                    dve.sem_inc(v_max, HV)
                    dve.wait_ge(pad_ready, 1)

                    def after(c):
                        for j in range(HV):
                            dve.wait_ge(v_abs, c * HV + (j + 1))
                            dve.tensor_scalar(vmax[:, j, ds(c * CH, CH)], bank(V_BANK + j), b_dt[:, j:j + 1], 0.0,
                                              ALU.add, ALU.max).then_inc(v_max, 1)

                    def chunk(c, follows):
                        for j in range(HV):
                            dve.wait_ge(ur_ready, c * HV + (HV + j + 1))
                            dve.tensor_scalar(taps[:, j, :], ur[:, j, ds(c * CH, CH)], conv_w[:, j, 0:1],
                                              conv_b[:, j:j + 1], ALU.mult, ALU.add).then_inc(conv_step, 1)
                            dve.wait_ge(conv_step, c * 2 * HV + (2 * j + 1))
                            dve.scalar_tensor_tensor(taps[:, j, :], ur[:, j, ds(c * CH + 1, CH)],
                                                     conv_w[:, j, 1:2], taps[:, j, :],
                                                     ALU.mult, ALU.add).then_inc(conv_step, 1)
                            dve.wait_ge(conv_step, c * 2 * HV + (2 * j + 2))
                            dve.wait_ge(u_ready, c * HV + (j + 1))
                            dve.scalar_tensor_tensor(cv[:, j, :], ur[:, j, ds(c * CH + 2, CH)], conv_w[:, j, 2:3],
                                                     taps[:, j, :], ALU.mult, ALU.add).then_inc(conv_ready, 1)
                        if follows:
                            after(c - 1)
                        dve.wait_ge(conv_ready, (c + 1) * HV)

                    chunk(0, False)
                    with dve.Fori(1, NC) as c:
                        chunk(c, True)
                    after(NC - 1)
                    dve.wait_ge(v_max, HV * NC + HV)
                    for k, piece in enumerate(pieces):
                        dve.wait_ge(soft_ln, k + 1)
                        dve.tensor_tensor(piece(delta), piece(delta), piece(vmax), ALU.add).then_inc(delta_ready, 1)
                    for k, piece in list(enumerate(pieces))[POOL_SHARE:]:
                        dve.wait_ge(delta_ready, k + 1)
                        dve.tensor_tensor(piece(u), piece(u), piece(delta), ALU.mult)

        def scan():
            ctx = ExitStack()
            with ctx:
                RB, RC, RP = 2, 4, 4
                LAG = 4
                YG_AT, PROJECT_AT, OB_AT, X_AT = 1, 4, 5, 7
                st = sb("st", [P, NS, HV, CH], on=ctx)
                da = sb("da", [P, RB, HV, CH], on=ctx)
                db = sb("db", [P, RB, HV, CH], on=ctx)
                cs = sb("cs", [P, RC, CH], on=ctx)
                prod = sb("prod", [P, RP, HV, CH], on=ctx)
                yg = sb("yg", [P, HV, CH], on=ctx)
                ob = sb("ob", [P, CH], on=ctx)
                dl = sb("dl", [P, HV, CH], on=ctx)
                dl_ready = sem("dl_ready")
                st_zero = sem("st_zero")
                b_spread = sem("b_spread")
                c_spread = sem("c_spread")
                cs_ready = sem("cs_ready")
                da_ready = sem("da_ready")
                db_ready = sem("db_ready")
                st_ready = sem("st_ready")
                prod_ready = sem("prod_ready")
                y_added = sem("y_added")
                yg_ready = sem("yg_ready")
                o_ready = sem("o_ready")
                ob_ready = sem("ob_ready")
                x_added = sem("x_added")
                block = ctx.enter_context(nc.Block())
                B_BANK, C_BANK, Y_BANK, O_BANK = 0, 2, 4, 6

                @block.tensor
                def _(pe):
                    pe.sem_inc(y_added, RP)

                    def add_y(c, n):
                        pe.wait_ge(prod_ready, c * NS + (NS + n + 1))
                        if n == 0:
                            pe.wait_ge(yg_ready, c + 1)
                        for j in range(HV):
                            mm = pe.matmul(bank(Y_BANK + j), ident[:], prod[:, n % RP, j, :],
                                           start=(n == 0), stop=(n == NS - 1))
                        mm.then_inc(y_added, 1)

                    def project(c):
                        pe.wait_ge(yg_ready, c + 2)
                        pe.wait_ge(ob_ready, c + 1)
                        for j in range(HV):
                            mm = pe.matmul(bank(O_BANK), w_out[:, j, :], yg[:, j, :],
                                           start=(j == 0), stop=(j == HV - 1))
                        mm.then_inc(o_ready, 1)

                    def chunk(c, follows):
                        for n in range(NS):
                            pe.wait_ge(db_ready, c * NS + (n + 1))
                            pe.matmul(bank(B_BANK + n % RB), sel[:, n, :], bc_split[:, ds(c * CH, CH)],
                                      start=True, stop=True).then_inc(b_spread, 1)
                            pe.wait_ge(cs_ready, c * NS + (n + 1))
                            pe.matmul(bank(C_BANK + n % RB), sel[:, NS + n, :], bc_split[:, ds(c * CH, CH)],
                                      start=True, stop=True).then_inc(c_spread, 1)
                            if n >= LAG:
                                add_y(c, n - LAG)
                            elif follows:
                                add_y(c - 1, NS - LAG + n)
                            if n == PROJECT_AT and follows:
                                project(c - 1)

                    chunk(0, False)
                    with pe.Fori(1, NC) as c:
                        chunk(c, True)
                    for n in range(NS - LAG, NS):
                        add_y(NC - 1, n)
                    project(NC - 1)

                @block.scalar
                def _(act):
                    act.sem_inc(cs_ready, RB)
                    act.sem_inc(ob_ready, 1)

                    def project_out(c):
                        act.wait_ge(x_added, c + 1)
                        act.wait_ge(o_ready, c + 1)
                        act.activation(ob[:], bank(O_BANK), ACT.Identity, bias=ga_b[:],
                                       scale=mod[:, 0, 2:3]).then_inc(ob_ready, 1)

                    def chunk(c, follows):
                        if follows:
                            act.wait_ge(da_ready, c * NS * HV)
                        act.activation(dl[:], delta[:, :, ds(c * CH, CH)], ACT.Copy).then_inc(dl_ready, 1)
                        act.wait_ge(dl_ready, c + 1)
                        for n in range(NS):
                            act.wait_ge(st_ready, (c * NS + n) * HV + HV)
                            for j in range(HV):
                                act.activation(da[:, n % RB, j, :], dl[:, j, :], ACT.Exp,
                                               scale=a_neg[:, j, n:n + 1]).then_inc(da_ready, 1)
                            act.wait_ge(c_spread, c * NS + (n + 1))
                            act.wait_ge(prod_ready, c * NS + (n + NS - RC + 1))
                            act.activation(cs[:, n % RC, :],
                                           bank(C_BANK + n % RB), ACT.Copy).then_inc(cs_ready, 1)
                            if n == OB_AT and follows:
                                project_out(c - 1)

                    chunk(0, False)
                    with act.Fori(1, NC) as c:
                        chunk(c, True)
                    project_out(NC - 1)

                @block.gpsimd
                def _(pool):
                    for n in range(NS):
                        i = pool.memset(st[:, n, :, CH - 1:CH], 0.0)
                    i.then_inc(st_zero, 1)
                    pool.sem_inc(prod_ready, NS)
                    with pool.Fori(0, NC) as c:
                        for n in range(NS):
                            pool.wait_ge(st_ready, (c * NS + (n + RB)) * HV + HV)
                            pool.wait_ge(cs_ready, c * NS + (RB + n + 1))
                            pool.wait_ge(y_added, c * NS + (n + 1))
                            pool.tensor_tensor(prod[:, n % RP], st[:, n],
                                               cs[:, n % RC, :].unsqueeze(1).broadcast_to([P, HV, CH]),
                                               ALU.mult).then_inc(prod_ready, 1)

                @block.vector
                def _(dve):
                    dve.sem_inc(db_ready, RB)
                    dve.sem_inc(st_ready, RB * HV)
                    dve.sem_inc(yg_ready, 1)
                    dve.sem_inc(x_added, 1)
                    dve.wait_ge(st_zero, 1)

                    def gate_y(c):
                        dve.wait_ge(y_added, c * NS + (RP + NS))
                        dve.tensor_tensor(yg[:], bank(Y_BANK, 2).rearrange("p (j t) -> p j t", j=HV),
                                          rg[:, :, ds(c * CH, CH)], ALU.mult).then_inc(yg_ready, 1)

                    def add_x(c):
                        dve.wait_ge(ob_ready, c + 2)
                        dve.tensor_tensor(x[:, ds(c * CH, CH)], x[:, ds(c * CH, CH)], ob[:],
                                          ALU.add).then_inc(x_added, 1)

                    def input_term(c, n):
                        dve.wait_ge(b_spread, c * NS + (n + 1))
                        dve.wait_ge(st_ready, (c * NS + n) * HV + HV)
                        dve.tensor_tensor(db[:, n % RB], u[:, :, ds(c * CH, CH)],
                                          bank(B_BANK + n % RB).unsqueeze(1).broadcast_to([P, HV, CH]),
                                          ALU.mult).then_inc(db_ready, 1)

                    def chunk(c, follows):
                        input_term(c, 0)
                        for n in range(NS):
                            dve.wait_ge(db_ready, c * NS + (RB + n + 1))
                            dve.wait_ge(prod_ready, c * NS + (n + 1))
                            for j in range(HV):
                                dve.wait_ge(da_ready, (c * NS + n) * HV + (j + 1))
                                dve.tensor_tensor_scan(st[:, n, j, :], da[:, n % RB, j, :], db[:, n % RB, j, :],
                                                       initial=st[:, n, j, CH - 1:CH],
                                                       op0=ALU.mult, op1=ALU.add).then_inc(st_ready, 1)
                                if j == 0 and n + 1 < NS:
                                    input_term(c, n + 1)
                            if n == YG_AT and follows:
                                gate_y(c - 1)
                            if n == X_AT and follows:
                                add_x(c - 1)

                    chunk(0, False)
                    with dve.Fori(1, NC) as c:
                        chunk(c, True)
                    gate_y(NC - 1)
                    add_x(NC - 1)

        scan_inputs()
        scan()
        sc.close()
        ab.close()

        def expert_tensors(name, width, dt, on, **kw):
            return [sb(f"{name}_{k}", shape, dt, on=on, **kw)
                    for k, shape in (("w1", [P, NE * width]), ("w3", [P, NE * width]), ("w2", [P, NE * width // P, P]))]

        def expert_pieces(width):
            unit = (NE * width, NE * width, NE * width // P)
            return [[slice(n * q // QW, n * (q + 1) // QW) for n in unit] for q in range(QW)]

        def expert_loads(whole, names, width, done):
            sources = [a[names[0]], a[names[1]], a[names[2]].rearrange("(j p) d -> p j d", p=P)]
            return [(whole[k][:, span], sources[k][:, span], done[q][k])
                    for q, spans in enumerate(expert_pieces(width)) for k, span in enumerate(spans)]

        def expert_cuts(whole, high, low, width, done):
            return [(whole[k][:, span], high[k][:, span], low[k][:, span], done[q][k])
                    for q, spans in enumerate(expert_pieces(width)) for k, span in enumerate(spans)]

        eb = ExitStack()
        high0 = expert_tensors("high0", H0, F32R, eb)
        low0 = expert_tensors("low0", H0, F32R, eb)
        hp0 = sb("hp0", [P, 2, T], F32R, on=eb)
        with ExitStack() as raw:
            whole0 = expert_tensors("whole0", H0, F32, raw, side="right")
            cuts0 = expert_cuts(whole0, high0, low0, H0, s_w0)
            first = cuts0[:3]
            first_high = sem("first_high")
            layernorm("f0", 0, 3, 4, hp0, loads=expert_loads(whole0, ("w1_0", "w3_0", "w2_0"), H0, s_w0),
                      beside=dict(pe_end=lambda pe, h_ready: logits(pe, h_ready, 0),
                                  dve_mid=lambda dve: copy_high(dve, first, first_high),
                                  pool=lambda pool: cut_low(pool, first, first_high)))
            route("f0", 0, 1e-20, False, cuts0[3:])

        rw, rq = ExitStack(), ExitStack()
        wv = sb("wv", [P, NH * DH], on=rw, side="right")
        wo = sb("wo", [P, NP, P], on=rw, side="right")
        bo = sb("bo", [P, 1], on=rw, side="right")
        wqkt = [sb(f"w{n}t", [P, NP, P], on=rq, side="right") for n in "kq"]
        wqk = [sb(f"w{n}", [P, NH * DH], on=rq, side="right") for n in "kq"]
        attention_loads = [
            (wqkt[0][:], a["wkt"].rearrange("(j p) d -> p j d", p=P), s_wt[0]),
            (wqkt[1][:], a["wqt"].rearrange("(j p) d -> p j d", p=P), s_wt[1]),
            (wqk[0][:], a["wk"], s_wkq[0]),
            (wqk[1][:], a["wq"], s_wkq[1]),
            (bo[:], a["bo"], s_rest),
            (wv[:], a["wv"], s_rest),
            (wo[:], a["wo"].rearrange("(j p) d -> p j d", p=P), s_rest),
        ]
        experts("f0", H0, *[(high0[k], low0[k]) for k in range(3)], hp0, 5, 0, loads=attention_loads)
        eb.close()
        nc.clear_and_free_semaphores(live)
        nc.all_engine_barrier()
        live.clear()

        whole1 = expert_tensors("whole1", H1, F32, top)
        tb = ExitStack()
        ga_bo = sb("ga_bo", [P, 1], on=tb)
        fq = sb("fq", [P, NT, FE], on=tb)
        kmax = sb("kmax", [P, NT], on=tb)
        ksum = sb("ksum", [P, FE], on=tb)
        cwo = sb("cwo", [P, FE // P, P], on=tb)
        fb = ExitStack()
        wq2, wk2, wqp2, wkp2 = ([sb(f"{n}_{k}", [P, m], F32R, on=fb) for k in ("high", "low")]
                                for n, m in (("wq", NH * DH), ("wk", NH * DH), ("wqp", FE), ("wkp", FE)))

        def attention_weights(ctx):
            pt2 = sb("pt2", [P, 2 * M], on=ctx)
            wp = sb("wp", [P, 2, FE], on=ctx)
            zero_ready = sem("zero_ready")
            wp_psum = sem("wp_psum")
            wp_ready = sem("wp_ready")
            wp_high = sem("wp_high")
            high_ready = sem("w_high_ready")

            def sp_part(sp):
                sp.wait_ge(zero_ready, 1)
                sp.dma_start(pt2[0:DH, 0:M], a["pt"]).then_inc(s_pt, 16)
                sp.dma_start(pt2[DH:P, M:2 * M], a["pt"]).then_inc(s_pt, 16)

            def pe_part(pe):
                pe.wait_ge(s_pt, 32)
                for b, wt in enumerate(wqkt):
                    pe.wait_ge(s_wt[b], 16)
                    for p in range(NP):
                        mm = pe.matmul(PS[:, b * CH + p * 2 * M:b * CH + (p + 1) * 2 * M], wt[:, p, :], pt2[:],
                                       start=True, stop=True, skip_group_check=True)
                    mm.then_inc(wp_psum, 1)

            def pool_part(pool):
                pool.memset(pt2[:], 0.0).then_inc(zero_ready, 1)
                for b, w2 in enumerate((wk2, wq2)):
                    pool.wait_ge(high_ready, b + 1)
                    pool.tensor_tensor(w2[1][:], wqk[b][:], w2[0][:].bitcast(F32), ALU.subtract)

            def dve_part(dve):
                for b, w2 in enumerate((wk2, wq2)):
                    dve.wait_ge(s_wkq[b], 16)
                    dve.tensor_copy(w2[0][:], wqk[b][:]).then_inc(high_ready, 1)
                for b in range(2):
                    dve.wait_ge(wp_psum, b + 1)
                    dve.tensor_scalar(wp[:, b, :], bank(b), DN, None, ALU.mult).then_inc(wp_ready, 1)

            def dve_end(dve):
                dve.wait_ge(wp_ready, 2)
                for b, w2 in enumerate((wkp2, wqp2)):
                    dve.tensor_copy(w2[0][:], wp[:, b, :]).then_inc(wp_high, 1)
                for b, w2 in enumerate((wkp2, wqp2)):
                    dve.wait_ge(wp_high, b + 1)
                    dve.tensor_tensor(w2[1][:], wp[:, b, :], w2[0][:].bitcast(F32), ALU.subtract)
                dve.wait_ge(s_rest, 48)
                dve.tensor_tensor(ga_bo[:], mod[:, 1, 2:3], bo[:], ALU.mult)

            return dict(sp=sp_part, pe_mid=pe_part, pool=pool_part, dve_mid=dve_part, dve_end=dve_end)

        with ExitStack() as aw:
            layernorm("a1", 1, 0, 1, beside=attention_weights(aw))
        rq.close()

        s_w1 = [[sem(f"s_w1_{q}_{k}") for k in range(3)] for q in range(QW)]

        hx = sb("hx", [P, NT, P], on=fb)
        fk = sb("fk", [P, NT, FE], on=fb)

        def heads(v):
            return v.rearrange("p (h m) -> p h m", m=M)

        def wide_m(v):
            return v.unsqueeze(2).broadcast_to([P, NH, M])

        def features():
            ctx = ExitStack()
            with ctx:
                HS = 2
                hs = sb("hs", [P, HS, CH], on=ctx)
                hs_high = sb("hs_high", [P, HS, CH], F32R, on=ctx)
                hs_low = sb("hs_low", [P, HS, CH], F32R, on=ctx)
                sq = sb("sq", [P, 2, NH, DH], on=ctx)
                half = sb("half", [P, 2, NH, DH // 2], on=ctx)
                dg = sb("dg", [P, 2, NH], on=ctx)
                mq = sb("mq", [P, 2, NH], on=ctx)
                hs_step = sem("hs_step")
                first_copied = sem("first_copied")
                first_ready = sem("first_ready")
                hs_ready = sem("hs_ready")
                hx_psum = sem("hx_psum")
                hx_ready = sem("hx_ready")
                dd_ready = [sem(f"dd_ready_{k}") for k in "kq"]
                proj_ready = [sem(f"proj_ready_{k}") for k in "kq"]
                sq_ready = [sem(f"sq_ready_{k}") for k in "kq"]
                half_ready = [sem(f"half_ready_{k}") for k in "kq"]
                dg_ready = [sem(f"dg_ready_{k}") for k in "kq"]
                q_max = sem("q_max")
                q_bias = sem("q_bias")
                shifted = [sem(f"shifted_{k}") for k in "kq"]
                q_exp = sem("q_exp")
                block = ctx.enter_context(nc.Block())
                PR, HX = (1, 4), 6
                DD = ((0, 0), (3, 7))
                RD = (1, 2)
                weights = ((wkp2, wk2), (wqp2, wq2))

                @block.sync
                def _(sp):
                    issue(sp, expert_loads(whole1, ("w1_1", "w3_1", "w2_1"), H1, s_w1))

                @block.tensor
                def _(pe):
                    def tile(c, g, t):
                        k1 = c * TPC + t
                        tok = slice(t * P, (t + 1) * P)
                        stat = [v[:, g, tok] for v in (hs_high, hs_low)]
                        pe.wait_ge(hs_ready, c + 1)
                        for s, (_, wp) in enumerate(weights):
                            pe.wait_ge(sq_ready[s], k1 + 1)
                            for b in range(2):
                                mm = product(pe, bank(PR[s] + b), stat, [w[:, b * CH:(b + 1) * CH] for w in wp])
                            mm.then_inc(proj_ready[s], 1)
                        pe.wait_ge(hx_ready, k1 + 1)
                        pe.transpose(PS[:, HX * CH:HX * CH + P], hs[:, g, tok], ident[:]).then_inc(hx_psum, 1)
                        for s, (wd, _) in enumerate(weights):
                            pe.wait_ge(shifted[s], k1 + 1)
                            product(pe, bank(DD[s][t % 2]), stat, [w[:] for w in wd]).then_inc(dd_ready[s], 1)

                    pe.wait_ge(first_ready, 1)
                    with pe.Fori(0, NC, HS) as c:
                        for g in range(HS):
                            for t in range(TPC):
                                tile(c + g, g, t)

                @block.scalar
                def _(act):
                    for k in sq_ready:
                        act.sem_inc(k, 1)
                    act.sem_inc(hx_ready, 1)

                    def q_exponential(k1):
                        act.wait_ge(shifted[1], k1 + RD[1] + 1)
                        q = fq[:, ds(k1, 1), :].rearrange("p a f -> p (a f)")
                        act.activation(q, q, ACT.Exp)

                    def chunk(c, follows):
                        for t in range(TPC):
                            k1 = c * TPC + t
                            for s in range(2):
                                act.wait_ge(half_ready[s], k1 + 1)
                                act.wait_ge(proj_ready[s], k1 + 1)
                                act.activation(sq[:, s].rearrange("p h e -> p (h e)"), bank(PR[s], 2), ACT.Square,
                                               scale=DN * math.sqrt(0.5)).then_inc(sq_ready[s], 1)
                            act.wait_ge(hx_psum, k1 + 1)
                            act.activation(hx[:, ds(k1, 1), :].rearrange("p a d -> p (a d)"),
                                           PS[:, HX * CH:HX * CH + P], ACT.Copy).then_inc(hx_ready, 1)
                            if t > 0 or follows:
                                q_exponential(c * TPC + (t - 1))

                    chunk(0, False)
                    with act.Fori(1, NC) as c:
                        chunk(c, True)
                    q_exponential(NT - 1)

                @block.gpsimd
                def _(pool):
                    for k in half_ready:
                        pool.sem_inc(k, 1)
                    pool.sem_inc(hs_ready, 1)

                    def take(c, g, step):
                        one = ones[:, 0:1].broadcast_to([P, CH])
                        if step < 2:
                            pool.tensor_tensor((hs, hs_high)[step][:, g, :], h[:, ds(c * CH, CH)], one,
                                               ALU.mult).then_inc(hs_step, 1)
                        else:
                            pool.wait_ge(hs_step, 2 * c)
                            pool.tensor_tensor(hs_low[:, g, :], hs[:, g, :], hs_high[:, g, :].bitcast(F32),
                                               ALU.subtract).then_inc(hs_ready, 1)

                    def chunk(c, g, last):
                        for t in range(TPC):
                            k1 = c * TPC + t
                            for s in range(2):
                                pool.wait_ge(sq_ready[s], k1 + 2)
                                pool.wait_ge(dg_ready[s], k1 + 1)
                                pool.tensor_tensor(half[:, s], sq[:, s, :, 0:DH // 2], sq[:, s, :, DH // 2:DH],
                                                   ALU.add).then_inc(half_ready[s], 1)
                            if not last and t < 3:
                                take(c + 1, (g + 1) % HS, t)

                    with pool.Fori(0, NC - HS, HS) as c:
                        for g in range(HS):
                            chunk(c + g, g, False)
                    for g in range(HS):
                        chunk(NC - HS + g, g, g == HS - 1)

                @block.vector
                def _(dve):
                    for s in range(2):
                        dve.sem_inc(shifted[s], RD[s])
                        dve.sem_inc(dg_ready[s], 1)

                    def tile(k1, t):
                        dve.wait_ge(half_ready[0], k1 + 2)
                        dve.tensor_reduce(dg[:, 0, :], half[:, 0], axis=AX.X, op=ALU.add).then_inc(dg_ready[0], 1)
                        dve.wait_ge(dd_ready[0], k1 + 1)
                        dve.tensor_reduce(kmax[:, ds(k1, 1)], bank(DD[0][t % 2]), axis=AX.X, op=ALU.max)
                        dve.wait_ge(dg_ready[0], k1 + 2)
                        dve.tensor_tensor(fk[:, ds(k1, 1), :].rearrange("p a (h m) -> p (a h) m", m=M),
                                          heads(bank(DD[0][t % 2])), wide_m(dg[:, 0, :]),
                                          ALU.subtract).then_inc(shifted[0], 1)
                        dve.wait_ge(dd_ready[1], k1 + 1)
                        dve.tensor_reduce(mq[:, 0, :], heads(bank(DD[1][t % 2])), axis=AX.X, op=ALU.max).then_inc(q_max, 1)
                        dve.wait_ge(half_ready[1], k1 + 2)
                        dve.tensor_reduce(dg[:, 1, :], half[:, 1], axis=AX.X, op=ALU.add).then_inc(dg_ready[1], 1)
                        dve.wait_ge(dg_ready[1], k1 + 2)
                        dve.wait_ge(q_max, k1 + 1)
                        dve.tensor_tensor(mq[:, 1, :], mq[:, 0, :], dg[:, 1, :], ALU.add).then_inc(q_bias, 1)
                        dve.wait_ge(q_bias, k1 + 1)
                        dve.tensor_tensor(fq[:, ds(k1, 1), :].rearrange("p a (h m) -> p (a h) m", m=M),
                                          heads(bank(DD[1][t % 2])), wide_m(mq[:, 1, :]),
                                          ALU.subtract).then_inc(shifted[1], 1)

                    dve.tensor_copy(hs[:, 0, :], h[:, 0:CH]).then_inc(first_copied, 1)
                    dve.tensor_copy(hs_high[:, 0, :], h[:, 0:CH]).then_inc(first_copied, 1)
                    dve.wait_ge(first_copied, 2)
                    dve.tensor_tensor(hs_low[:, 0, :], hs[:, 0, :], hs_high[:, 0, :].bitcast(F32),
                                      ALU.subtract).then_inc(first_ready, 1)
                    with dve.Fori(0, NC) as c:
                        for t in range(TPC):
                            tile(c * TPC + t, t)

        def context():
            ctx = ExitStack()
            with ctx:
                km = sb("km", [P, 4], on=ctx)
                gt = sb("gt", [P, FE], on=ctx)
                kacc = sb("kacc", [P, 2, FE], on=ctx)
                kacc_zero = sem("kacc_zero")
                kacc_step = sem("kacc_step")
                odd_step = sem("odd_step")
                ks_psum = sem("ks_psum")
                ctxt = sb("ctxt", [P, NP, P], on=ctx)
                k_step = sem("k_step")
                km_t = sem("km_t")
                km_row = sem("km_row")
                km_b = sem("km_b")
                kneg = sem("kneg")
                k_exp = sem("k_exp")
                fk_ready = sem("fk_ready")
                gt_psum = sem("gt_psum")
                gt_ready = sem("gt_ready")
                ctx_psum = sem("ctx_psum")
                ctxt_ready = sem("ctxt_ready")
                ctxt_zero = sem("ctxt_zero")
                cwo_psum = sem("cwo_psum")
                block = ctx.enter_context(nc.Block())

                @block.gpsimd
                def _(pool):
                    pool.memset(ctxt[:], 0.0).then_inc(ctxt_zero, 1)
                    pool.memset(kacc[:], 0.0).then_inc(kacc_zero, 1)
                    pool.sem_inc(kacc_step, 1)
                    pool.wait_ge(kacc_zero, 1)
                    with pool.Fori(0, NT // 2) as t:
                        pool.wait_ge(kacc_step, t + 1)
                        pool.wait_ge(fk_ready, 2 * t + 1)
                        pool.tensor_tensor(kacc[:, 0, :], kacc[:, 0, :],
                                           fk[:, ds(2 * t, 1), :].rearrange("p a f -> p (a f)"),
                                           ALU.add).then_inc(kacc_step, 1)

                @block.vector
                def _(dve):
                    dve.tensor_reduce(km[:, 0:1], kmax[:], axis=AX.X, op=ALU.max).then_inc(k_step, 1)
                    dve.wait_ge(km_t, 1)
                    dve.tensor_reduce(km[0:1, 1:2], PS[0:1, 0:P], axis=AX.X, op=ALU.max).then_inc(km_row, 1)
                    dve.wait_ge(km_b, 1)
                    dve.tensor_scalar(km[:, 2:3], PS[:, CH:CH + 1], -1.0, None, ALU.mult).then_inc(kneg, 1)
                    dve.sem_inc(odd_step, 1)
                    dve.wait_ge(kacc_zero, 1)
                    with dve.Fori(0, NT // 2) as t:
                        for i in range(2):
                            dve.wait_ge(k_exp, 2 * t + (i + 1))
                            k, q = (v[:, ds(2 * t + i, 1), :].rearrange("p a f -> p (a f)") for v in (fk, fq))
                            dve.tensor_scalar(k, k, FEAT_EPS, RATIO, ALU.add, ALU.mult).then_inc(fk_ready, 1)
                            dve.tensor_scalar(q, q, FEAT_EPS, RATIO, ALU.add, ALU.mult)
                        dve.wait_ge(fk_ready, 2 * t + 2)
                        dve.wait_ge(odd_step, t + 1)
                        dve.tensor_tensor(kacc[:, 1, :], kacc[:, 1, :], k, ALU.add).then_inc(odd_step, 1)
                    dve.wait_ge(ctxt_zero, 1)
                    dve.wait_ge(ctx_psum, NP)
                    for p in range(NP):
                        for i in range(2):
                            o = (p % 2) * 2 * M + i * M
                            dve.tensor_copy(ctxt[i * DH:(i + 1) * DH, p, o:o + M],
                                            PS[i * DH:(i + 1) * DH,
                                               4 * CH + p * 2 * M + i * M:4 * CH + p * 2 * M + (i + 1) * M]
                                            ).then_inc(ctxt_ready, 1)

                @block.scalar
                def _(act):
                    act.wait_ge(kneg, 1)
                    with act.Fori(0, NT) as t:
                        k = fk[:, ds(t, 1), :].rearrange("p a f -> p (a f)")
                        act.activation(k, k, ACT.Exp, bias=km[:, 2:3]).then_inc(k_exp, 1)
                    act.wait_ge(gt_psum, 1)
                    act.activation(gt[:], bank(2), ACT.Copy).then_inc(gt_ready, 1)
                    act.wait_ge(ks_psum, 1)
                    act.activation(ksum[:], bank(3), ACT.Copy)
                    act.wait_ge(cwo_psum, 1)
                    act.activation(cwo[:].rearrange("p g d -> p (g d)"), bank(5), ACT.Copy)

                @block.tensor
                def _(pe):
                    pe.wait_ge(k_step, 1)
                    pe.transpose(PS[0:1, 0:P], km[:, 0:1], ident[:]).then_inc(km_t, 1)
                    pe.wait_ge(km_row, 1)
                    pe.matmul(PS[:, CH:CH + 1], ones[0:1, :], km[0:1, 1:2], start=True, stop=True).then_inc(km_b, 1)
                    for t in range(NT):
                        pe.wait_ge(fk_ready, t + 1)
                        mm = pe.matmul(bank(2), hx[:, t, :], fk[:, t, :], start=(t == 0), stop=(t == NT - 1))
                    mm.then_inc(gt_psum, 1)
                    pe.wait_ge(kacc_step, NT // 2 + 1)
                    pe.wait_ge(odd_step, NT // 2 + 1)
                    for i in range(2):
                        mm = pe.matmul(bank(3), ones[:], kacc[:, i, :], start=(i == 0), stop=(i == 1))
                    mm.then_inc(ks_psum, 1)
                    pe.wait_ge(gt_ready, 1)
                    for p in range(NP):
                        pe.matmul(PS[:, 4 * CH + p * 2 * M:4 * CH + (p + 1) * 2 * M], wv[:, p * P:(p + 1) * P],
                                  gt[:, p * 2 * M:(p + 1) * 2 * M], start=True, stop=True,
                                  skip_group_check=True).then_inc(ctx_psum, 1)
                    pe.wait_ge(ctxt_ready, 2 * NP)
                    for p in range(NP):
                        g = p // 2
                        mm = pe.matmul(PS[:, 5 * CH + g * P:5 * CH + (g + 1) * P], ctxt[:, p, :], wo[:, p, :],
                                       start=(p % 2 == 0), stop=(p % 2 == 1), skip_group_check=True)
                    mm.then_inc(cwo_psum, 1)

        def attend(cuts):
            ctx = ExitStack()
            with ctx:
                G = FE // P
                RG, RQ = 2, 4
                qk = sb("qk", [P, RG, FE], on=ctx)
                den = sb("den", [P, RQ, 2, NH], on=ctx)
                qs = sb("qs", [P, RQ, FE], on=ctx)
                qt = sb("qt", [P, G, T], on=ctx)
                ob = sb("ob1", [P, CH], on=ctx)
                qk_ready = sem("qk_ready")
                den_ready = sem("den_ready")
                den_inverse = sem("den_inverse")
                qs_ready = sem("qs_ready")
                qt_psum = sem("qt_psum")
                qt_ready = sem("qt_ready")
                o1_ready = sem("o1_ready")
                ob1_ready = sem("ob1_ready")
                x1_added = sem("x1_added")
                w1_high = sem("w1_high")
                block = ctx.enter_context(nc.Block())
                O_BANK = RQ
                assert G == TPC

                @block.gpsimd
                def _(pool):
                    pool.sem_inc(qk_ready, RG)
                    with pool.Fori(0, NC) as c:
                        for t in range(TPC):
                            q = fq[:, ds(c * TPC + t, 1), :].rearrange("p a f -> p (a f)")
                            pool.wait_ge(den_ready, c * TPC + (t + 1))
                            pool.tensor_tensor(qk[:, t % RG, :], q, ksum[:], ALU.mult).then_inc(qk_ready, 1)
                    cut_low(pool, cuts, w1_high)

                @block.vector
                def _(dve):
                    dve.sem_inc(den_ready, RG)
                    dve.sem_inc(qs_ready, RQ)
                    dve.sem_inc(x1_added, 1)

                    def add_x(c):
                        dve.wait_ge(ob1_ready, c + 2)
                        dve.tensor_tensor(x[:, ds(c * CH, CH)], x[:, ds(c * CH, CH)], ob[:],
                                          ALU.add).then_inc(x1_added, 1)

                    def total(c, t):
                        dve.wait_ge(qk_ready, c * TPC + (t + RG + 1))
                        dve.tensor_reduce(den[:, t % RQ, 0, :], heads(qk[:, t % RG, :]), axis=AX.X,
                                          op=ALU.add).then_inc(den_ready, 1)

                    def chunk(c, before):
                        total(c, 0)
                        for t in range(TPC):
                            k1 = c * TPC + t
                            dve.wait_ge(den_ready, c * TPC + (t + RG + 1))
                            dve.reciprocal(den[:, t % RQ, 1, :], den[:, t % RQ, 0, :]).then_inc(den_inverse, 1)
                            if t + 1 < TPC:
                                total(c, t + 1)
                            dve.wait_ge(den_inverse, c * TPC + (t + 1))
                            dve.wait_ge(qt_psum, c * TPC + (t + 1))
                            dve.tensor_tensor(heads(qs[:, t % RQ, :]),
                                              fq[:, ds(k1, 1), :].rearrange("p a (h m) -> p (a h) m", m=M),
                                              wide_m(den[:, t % RQ, 1, :]), ALU.mult).then_inc(qs_ready, 1)
                            if t == 2 and before > 1:
                                add_x(c - 2)

                    chunk(0, 0)
                    chunk(1, 1)
                    with dve.Fori(2, NC) as c:
                        chunk(c, 2)
                    add_x(NC - 2)
                    add_x(NC - 1)

                @block.tensor
                def _(pe):
                    pe.sem_inc(qt_psum, RQ)

                    def project(c, g):
                        if g == 0:
                            pe.wait_ge(qt_ready, c * TPC + (TPC + RQ))
                            pe.wait_ge(ob1_ready, c + 1)
                        mm = pe.matmul(bank(O_BANK), cwo[:, g, :], qt[:, g, ds(c * CH, CH)],
                                       start=(g == 0), stop=(g == G - 1))
                        if g == G - 1:
                            mm.then_inc(o1_ready, 1)

                    def chunk(c, before):
                        for t in range(TPC):
                            r = t % RQ
                            pe.wait_ge(qs_ready, c * TPC + (t + RQ + 1))
                            pe.wait_ge(qt_ready, c * TPC + (t + 1))
                            for g in range(G):
                                mm = pe.transpose(PS[:, r * CH + g * P:r * CH + (g + 1) * P],
                                                  qs[:, r, g * P:(g + 1) * P], ident[:])
                            mm.then_inc(qt_psum, 1)
                            if before > 0:
                                project(c - 1, t)

                    chunk(0, 0)
                    with pe.Fori(1, NC) as c:
                        chunk(c, 1)
                    for g in range(G):
                        project(NC - 1, g)

                @block.scalar
                def _(act):
                    act.sem_inc(qt_ready, RQ)
                    act.sem_inc(ob1_ready, 1)
                    cut_high(act, cuts, w1_high)

                    def out(c):
                        act.wait_ge(o1_ready, c + 1)
                        act.wait_ge(x1_added, c + 1)
                        act.activation(ob[:], bank(O_BANK), ACT.Identity, bias=ga_bo[:],
                                       scale=mod[:, 1, 2:3]).then_inc(ob1_ready, 1)

                    def chunk(c, before):
                        for t in range(TPC):
                            r = t % RQ
                            act.wait_ge(qt_psum, c * TPC + (t + RQ + 1))
                            act.activation(qt[:, :, ds(c * CH + t * P, P)],
                                           bank(r).rearrange("p (g t) -> p g t", g=G), ACT.Copy).then_inc(qt_ready, 1)
                            if t == TPC - 1 and before > 0:
                                out(c - 1)

                    chunk(0, 0)
                    with act.Fori(1, NC) as c:
                        chunk(c, 1)
                    out(NC - 1)

        features()
        context()
        fb.close()
        wb = ExitStack()
        high1 = expert_tensors("high1", H1, F32R, wb, side="right")
        low1 = expert_tensors("low1", H1, F32R, wb, side="right")
        cuts1 = expert_cuts(whole1, high1, low1, H1, s_w1)
        attend(cuts1[:8])
        tb.close()

        hp1 = sb("hp1", [P, 2, T], F32R)
        last_high = sem("last_high")
        layernorm("f1", 1, 3, 4, hp1, beside=dict(pe_end=lambda pe, h_ready: logits(pe, h_ready, 1),
                                                  dve_mid=lambda dve: copy_high(dve, cuts1[8:], last_high),
                                                  pool=lambda pool: cut_low(pool, cuts1[8:], last_high)))
        route("f1", 1, 1e-9, True, [])
        s_out = sem("s_out")
        experts("f1", H1, *[(high1[k], low1[k]) for k in range(3)], hp1, 5, 1, store=out)
        wb.close()
        rw.close()


def kernel(**inputs):
    import numpy as np
    import concourse.bacc as bacc
    from concourse.bass_utils import run_bass_kernel_spmd

    def lay(v):
        return np.ascontiguousarray(v)

    def cols(v, n):
        return lay(np.reshape(v, (n, P)).T)

    i = {k: np.asarray(v) for k, v in inputs.items()}
    arrays = {
        "x": lay(i["L0_attn_x"][0].T),
        "c": lay(np.concatenate([i["L0_c"], i["L1_c"]], axis=0).T),
        "wmod0": i["L0_wmod"], "wmod1": i["L1_wmod"],
        "w_in": i["L0_attn_W_in"], "b_in": cols(i["L0_attn_b_in"], 2 * HV),
        "conv_w": lay(i["L0_attn_conv_w"].reshape(HV, P, KW).transpose(1, 0, 2)),
        "conv_b": cols(i["L0_attn_conv_b"], HV),
        "w_x": lay(i["L0_attn_W_x"].reshape(HV, P, RK + 2 * NS).transpose(1, 0, 2)),
        "w_dt": i["L0_attn_W_dt"], "b_dt": cols(i["L0_attn_b_dt"], HV),
        "w_out": lay(i["L0_attn_W_out"].reshape(HV, P, P).transpose(1, 0, 2)),
        "b_out": cols(i["L0_attn_b_out"], 1),
        "a_log": lay(i["L0_attn_A_log"].reshape(HV, P, NS).transpose(1, 0, 2)),
        "wg": lay(np.stack([i["L0_ffn_Wg"].T, i["L1_ffn_router_w"].T], axis=1)),
        "router_b": i["L1_ffn_router_b"],
        "w1_0": lay(i["L0_ffn_W1"].transpose(2, 0, 1).reshape(P, NE * H0)),
        "w3_0": lay(i["L0_ffn_W3"].transpose(2, 0, 1).reshape(P, NE * H0)),
        "w2_0": lay(i["L0_ffn_W2"].transpose(0, 2, 1).reshape(NE * H0, P)),
        "wq": i["L1_attn_Wq"], "wk": i["L1_attn_Wk"], "wv": i["L1_attn_Wv"], "wo": i["L1_attn_Wo"],
        "wqt": lay(i["L1_attn_Wq"].T), "wkt": lay(i["L1_attn_Wk"].T),
        "bo": cols(i["L1_attn_bo"], 1), "pt": lay(i["L1_attn_P"].T),
        "w1_1": lay(i["L1_ffn_w_gate"].transpose(2, 0, 1).reshape(P, NE * H1)),
        "w3_1": lay(i["L1_ffn_w_up"].transpose(2, 0, 1).reshape(P, NE * H1)),
        "w2_1": lay(i["L1_ffn_w_down"].transpose(0, 2, 1).reshape(NE * H1, P)),
    }
    nc = bacc.Bacc("TRN2", target_bir_lowering=False, num_devices=1)
    arrays = {f"in_{k}": lay(v) for k, v in arrays.items()}
    aps = {k[3:]: nc.dram_tensor(k, v.shape, mybir.dt.from_np(v.dtype), kind="ExternalInput").ap()
           for k, v in arrays.items()}
    out = nc.dram_tensor("out", (P, T), F32, kind="ExternalOutput").ap()
    build(nc, aps, out)
    r = run_bass_kernel_spmd(nc, [arrays], core_ids=[0])
    return lay(r.results[0]["out"].T)[None]
```
